# Optimizing a Trainium2 kernel written in Bass

```python
import numpy as np
import jax
import jax.numpy as jnp

def _softmax(x, axis=-1):
    return jax.nn.softmax(x, axis=axis)

def _gelu(x):
    return jax.nn.gelu(x, approximate=True)

def _silu(x):
    return jax.nn.silu(x)

def _sigmoid(x):
    return jax.nn.sigmoid(x)

def _layernorm(x, axis=-1, eps=1e-05):
    m = jnp.mean(x, axis=axis, keepdims=True)
    v = jnp.var(x, axis=axis, keepdims=True)
    return (x - m) / jnp.sqrt(v + eps)

def _scatter_add(tgt, idx, src, axis=0):
    return tgt.at[idx].add(src)

def _segment_sum(src, seg, n):
    return jax.ops.segment_sum(src, seg, n)
kernel_name = 'mk_xattn_ffn_d2_seqx_r4_37b101'

def setup_inputs(seed: int=0):
    np.random.seed(seed)
    _w = jnp.asarray

    def _rec_inputs():
        import jax
        import jax.numpy as jnp
        _rk = jax.random.key(seed)
        x = 0.0001212 + 1 * jax.random.normal(jax.random.fold_in(_rk, 1), (8, 256, 1024), jnp.float32)
        _lenS = 256 - jax.random.randint(jax.random.fold_in(_rk, 7), (8,), 0, max(1, 256 // 4) + 1, jnp.int32)
        _lenS2 = 256 - jax.random.randint(jax.random.fold_in(_rk, 8), (8,), 0, max(1, 256 // 4) + 1, jnp.int32)
        _ctx_4096P = jax.random.normal(jax.random.fold_in(_rk, 11), (8, 16, 1024), jnp.float32)
        _ctx_4096c = jax.random.dirichlet(jax.random.fold_in(_rk, 511), 0.3 * jnp.ones((16,), jnp.float32), (8, 256))
        _ctx_4096t = jnp.einsum('bsk,bkd->bsd', _ctx_4096c, _ctx_4096P)
        _ctx_4096t = _ctx_4096t * jax.lax.rsqrt(jnp.mean(jnp.square(_ctx_4096t)) + 1e-12) * 0.953939
        ctx_4096 = -0.000125008 + 0.999885 * (_ctx_4096t + 0.3 * jax.random.normal(jax.random.fold_in(_rk, 611), (8, 256, 1024), jnp.float32))
        return (x, ctx_4096)
    x, ctx_4096 = _rec_inputs()

    def _L0_xattn_setup():
        import jax, jax.numpy as jnp
        import numpy as np
        N, C, S = (16, 128, 1024)
        rng = jax.random.key(seed)
        k1, k2, k3 = jax.random.split(rng, 3)
        return {'key': jax.random.normal(k1, (N, C, S), dtype=jnp.float32), 'value': jax.random.normal(k2, (N, C, S), dtype=jnp.float32), 'query': jax.random.normal(k3, (N, C, S), dtype=jnp.float32)}
    _L0_xattn_all = _L0_xattn_setup()
    _L0_xattn_in = {k: v for k, v in _L0_xattn_all.items() if k in ()}
    del _L0_xattn_all

    def _L0_ffn_setup():
        import jax, jax.numpy as jnp
        import numpy as np
        NF4 = jnp.array([-1.0, -0.6961928009986877, -0.5250730514526367, -0.39491748809814453, -0.28444138169288635, -0.18477343022823334, -0.09105003625154495, 0.0, 0.07958029955625534, 0.16093020141124725, 0.24611230194568634, 0.33791524171829224, 0.44070982933044434, 0.5626170039176941, 0.7229568362236023, 1.0], dtype=jnp.float32)
        BLOCK = 64

        def dequant_nf4(codes, scales):
            out_dim, in_dim = codes.shape
            vals = NF4[codes].reshape(out_dim, in_dim // BLOCK, BLOCK)
            return (vals * scales[:, :, None]).reshape(out_dim, in_dim)
        key = jax.random.key(seed)
        ks = jax.random.split(key, 7)
        H, I = (1024, 2752)
        B, S = (4, 512)
        return {'x': jax.random.normal(ks[0], (B, S, H), dtype=jnp.float32), 'gate_codes': jax.random.randint(ks[1], (I, H), 0, 16, dtype=jnp.int32), 'gate_scales': jax.random.uniform(ks[2], (I, H // BLOCK), dtype=jnp.float32) * 0.02, 'up_codes': jax.random.randint(ks[3], (I, H), 0, 16, dtype=jnp.int32), 'up_scales': jax.random.uniform(ks[4], (I, H // BLOCK), dtype=jnp.float32) * 0.02, 'down_codes': jax.random.randint(ks[5], (H, I), 0, 16, dtype=jnp.int32), 'down_scales': jax.random.uniform(ks[6], (H, I // BLOCK), dtype=jnp.float32) * 0.02}
    _L0_ffn_all = _L0_ffn_setup()
    _L0_ffn_in = {k: v for k, v in _L0_ffn_all.items() if k in ('gate_codes', 'gate_scales', 'up_codes', 'up_scales', 'down_codes', 'down_scales')}
    del _L0_ffn_all

    def _L1_xattn_setup():
        import jax, jax.numpy as jnp
        import numpy as np
        import math
        EPS = 1e-05
        LAMBDA = 0.6

        def _crucial_k(C):
            f = math.floor(LAMBDA * C)
            return f + f % 2

        def _conv1d(y, w):
            return jax.lax.conv_general_dilated(y, w, window_strides=(1,), padding=((3, 3),), dimension_numbers=('NCH', 'OIH', 'NCH'))

        def _norm_active(z, gamma, beta):
            mu = jnp.mean(z, axis=(0, 2), keepdims=True)
            var = jnp.mean((z - mu) ** 2, axis=(0, 2), keepdims=True)
            zn = (z - mu) * jax.lax.rsqrt(var + EPS)
            zn = zn * gamma.reshape(1, -1, 1) + beta.reshape(1, -1, 1)
            return jax.nn.sigmoid(jax.nn.relu(zn))
        key = jax.random.key(seed)
        k1, k2, k3 = jax.random.split(key, 3)
        B, C, L = (32, 64, 1024)
        x = jax.random.normal(k1, (B, C, L), dtype=jnp.float32)
        channel_map = jax.random.normal(k2, (B, C, L), dtype=jnp.float32)
        fan_in = 2 * 7
        bound = 1.0 / math.sqrt(fan_in)
        conv_w = jax.random.uniform(k3, (1, 2, 7), jnp.float32, -bound, bound)
        bn_gamma = jnp.ones((1,), jnp.float32)
        bn_beta = jnp.zeros((1,), jnp.float32)
        return {'x': x, 'channel_map': channel_map, 'conv_w': conv_w, 'bn_gamma': bn_gamma, 'bn_beta': bn_beta}
    _L1_xattn_all = _L1_xattn_setup()
    _L1_xattn_in = {k: v for k, v in _L1_xattn_all.items() if k in ('conv_w', 'bn_gamma', 'bn_beta')}
    del _L1_xattn_all

    def _L1_ffn_setup():
        import jax, jax.numpy as jnp
        import numpy as np
        FP8 = jnp.float8_e4m3fn

        def _quant_fp8(x, scale_inv):
            return (x * scale_inv).astype(FP8)
        key = jax.random.key(seed)
        k1, k2, k3 = jax.random.split(key, 3)
        B, S, IN, OUT = (4, 512, 1024, 1024)
        inp = jax.random.normal(k1, (B, S, IN), dtype=jnp.float32)
        weight = jax.random.normal(k2, (IN, OUT), dtype=jnp.float32) * 0.02
        bias = jax.random.normal(k3, (OUT,), dtype=jnp.float32)
        input_scale = jnp.ones((1,), dtype=jnp.float32)
        weight_scale = jnp.ones((1,), dtype=jnp.float32)
        return {'inp': inp, 'weight': weight, 'bias': bias, 'input_scale': input_scale, 'weight_scale': weight_scale}
    _L1_ffn_all = _L1_ffn_setup()
    _L1_ffn_in = {k: v for k, v in _L1_ffn_all.items() if k in ('weight', 'bias', 'input_scale', 'weight_scale')}
    del _L1_ffn_all
    return {'x': x, 'ctx_4096': ctx_4096, 'L0_ffn_gate_codes': _L0_ffn_in['gate_codes'], 'L0_ffn_gate_scales': _L0_ffn_in['gate_scales'], 'L0_ffn_up_codes': _L0_ffn_in['up_codes'], 'L0_ffn_up_scales': _L0_ffn_in['up_scales'], 'L0_ffn_down_codes': _L0_ffn_in['down_codes'], 'L0_ffn_down_scales': _L0_ffn_in['down_scales'], 'L1_xattn_conv_w': _L1_xattn_in['conv_w'], 'L1_xattn_bn_gamma': _L1_xattn_in['bn_gamma'], 'L1_xattn_bn_beta': _L1_xattn_in['bn_beta'], 'L1_ffn_weight': _L1_ffn_in['weight'], 'L1_ffn_bias': _L1_ffn_in['bias'], 'L1_ffn_input_scale': _L1_ffn_in['input_scale'], 'L1_ffn_weight_scale': _L1_ffn_in['weight_scale']}

def reference(x, ctx_4096, L0_ffn_gate_codes, L0_ffn_gate_scales, L0_ffn_up_codes, L0_ffn_up_scales, L0_ffn_down_codes, L0_ffn_down_scales, L1_xattn_conv_w, L1_xattn_bn_gamma, L1_xattn_bn_beta, L1_ffn_weight, L1_ffn_bias, L1_ffn_input_scale, L1_ffn_weight_scale):
    import jax
    import jax.numpy as jnp

    def _L0_xattn_ref(key, value, query):
        import jax, jax.numpy as jnp
        import numpy as np
        N, C, S = (16, 128, 1024)
        KC = key.shape[1]
        sim = jnp.einsum('ncs,nds->ncd', key, query) * KC ** (-0.5)
        sim = jax.nn.softmax(sim, axis=1)
        context = jnp.einsum('ncd,nds->ncs', sim, value)
        return context

    def _L0_ffn_ref(x, gate_codes, gate_scales, up_codes, up_scales, down_codes, down_scales):
        import jax, jax.numpy as jnp
        import numpy as np
        NF4 = jnp.array([-1.0, -0.6961928009986877, -0.5250730514526367, -0.39491748809814453, -0.28444138169288635, -0.18477343022823334, -0.09105003625154495, 0.0, 0.07958029955625534, 0.16093020141124725, 0.24611230194568634, 0.33791524171829224, 0.44070982933044434, 0.5626170039176941, 0.7229568362236023, 1.0], dtype=jnp.float32)
        BLOCK = 64

        def dequant_nf4(codes, scales):
            out_dim, in_dim = codes.shape
            vals = NF4[codes].reshape(out_dim, in_dim // BLOCK, BLOCK)
            return (vals * scales[:, :, None]).reshape(out_dim, in_dim)
        Wg = dequant_nf4(gate_codes, gate_scales)
        Wu = dequant_nf4(up_codes, up_scales)
        Wd = dequant_nf4(down_codes, down_scales)
        gate = jnp.einsum('bsh,ih->bsi', x, Wg)
        up = jnp.einsum('bsh,ih->bsi', x, Wu)
        inter = jax.nn.silu(gate) * up
        return jnp.einsum('bsi,hi->bsh', inter, Wd)

    def _L1_xattn_ref(x, channel_map, conv_w, bn_gamma, bn_beta):
        import jax, jax.numpy as jnp
        import numpy as np
        import math
        EPS = 1e-05
        LAMBDA = 0.6

        def _crucial_k(C):
            f = math.floor(LAMBDA * C)
            return f + f % 2

        def _conv1d(y, w):
            return jax.lax.conv_general_dilated(y, w, window_strides=(1,), padding=((3, 3),), dimension_numbers=('NCH', 'OIH', 'NCH'))

        def _norm_active(z, gamma, beta):
            mu = jnp.mean(z, axis=(0, 2), keepdims=True)
            var = jnp.mean((z - mu) ** 2, axis=(0, 2), keepdims=True)
            zn = (z - mu) * jax.lax.rsqrt(var + EPS)
            zn = zn * gamma.reshape(1, -1, 1) + beta.reshape(1, -1, 1)
            return jax.nn.sigmoid(jax.nn.relu(zn))
        B, C, L = x.shape
        k = _crucial_k(C)
        cm = jnp.moveaxis(channel_map, 1, 2)
        _, topk_idx = jax.lax.top_k(cm, k)
        b_idx = jnp.arange(B)[:, None, None]
        l_idx = jnp.arange(L)[None, :, None]
        mask = jnp.zeros((B, L, C), x.dtype).at[b_idx, l_idx, topk_idx].set(1.0)
        crucial_channels = jnp.moveaxis(mask, 2, 1)
        subcrucial_channels = 1.0 - crucial_channels
        crucial_features = crucial_channels * x
        subcrucial_features = subcrucial_channels * x
        c_max = jnp.max(crucial_features, axis=1, keepdims=True)
        c_avg = jnp.mean(crucial_features, axis=1, keepdims=True) * (C / k)
        s_max = jnp.max(subcrucial_features, axis=1, keepdims=True)
        s_avg = jnp.mean(subcrucial_features, axis=1, keepdims=True) * (C / (C - k))
        crucial_x = jnp.concatenate([c_max, c_avg], axis=1)
        subcrucial_x = jnp.concatenate([s_max, s_avg], axis=1)
        A_S1 = _norm_active(_conv1d(crucial_x, conv_w), bn_gamma, bn_beta)
        A_S2 = _norm_active(_conv1d(subcrucial_x, conv_w), bn_gamma, bn_beta)
        return crucial_features * A_S1 + subcrucial_features * A_S2

    def _L1_ffn_ref(inp, weight, bias, input_scale, weight_scale):
        import jax, jax.numpy as jnp
        import numpy as np
        FP8 = jnp.float8_e4m3fn

        def _quant_fp8(x, scale_inv):
            return (x * scale_inv).astype(FP8)
        in_features = weight.shape[0]
        lead = inp.shape[:-1]
        x = inp.reshape(-1, in_features)
        x_q = _quant_fp8(x, 1.0 / input_scale)
        w_q = _quant_fp8(weight, 1.0 / weight_scale)
        acc = jnp.einsum('ni,io->no', x_q.astype(jnp.float32), w_q.astype(jnp.float32))
        out = acc * (input_scale * weight_scale) + bias
        return out.reshape(*lead, out.shape[-1])
    x = x + _L0_xattn_ref(ctx_4096, ctx_4096, _layernorm(x, axis=-1))
    x = x + _L0_ffn_ref(_layernorm(x, axis=-1), L0_ffn_gate_codes, L0_ffn_gate_scales, L0_ffn_up_codes, L0_ffn_up_scales, L0_ffn_down_codes, L0_ffn_down_scales)
    x = x + _L1_xattn_ref(_layernorm(x, axis=-1), ctx_4096, L1_xattn_conv_w, L1_xattn_bn_gamma, L1_xattn_bn_beta)
    x = x + _L1_ffn_ref(_layernorm(x, axis=-1), L1_ffn_weight, L1_ffn_bias, L1_ffn_input_scale, L1_ffn_weight_scale)
    return x

_drawn_inputs = setup_inputs


def setup_inputs(seed=0):
    import zlib

    import numpy as np

    out = dict(_drawn_inputs(seed))
    spreads = {}
    factors = {'L0_ffn_gate_scales': 8.0, 'L0_ffn_up_scales': 8.0, 'L0_ffn_down_scales': 8.0}
    for name, (base, spread) in spreads.items():
        noise = np.random.default_rng([zlib.crc32(name.encode()), seed]).standard_normal(out[name].shape)
        drawn = base * np.exp(spread * noise) if base else spread * noise
        out[name] = jnp.asarray(drawn.astype(out[name].dtype))
    for name, factor in factors.items():
        out[name] = (out[name] * factor).astype(out[name].dtype)
    return out
```

```python
import math
from contextlib import ExitStack

import numpy as np

import concourse.bass as bass
import concourse.mybir as mybir

F32 = mybir.dt.float32
BF16 = mybir.dt.bfloat16
I32 = mybir.dt.int32
ALU = mybir.AluOpType
ACT = mybir.ActivationFunctionType
AX = mybir.AxisListType

P = 128
B, C, D = 8, 256, 1024
CT = C // P
NT = B * CT
KT = D // P
I = 2752
NB = -(-I // P)
LAST = I - (NB - 1) * P
SB = 64
HW = 512
EPS = 1e-5
TOPK = math.floor(0.6 * C) + math.floor(0.6 * C) % 2
REST = C - TOPK
ROUNDS = -(-REST // 8)
GONE = -3.0e38

LOW = [(-0.09372339397668839, 0.6533904075622559), (-0.11047609895467758, 0.7263457775115967),
       (-0.060643620789051056, 0.14096669852733612), (-0.2653747797012329, 0.132687509059906)]
HIGH = [(0.08134989440441132, -0.5712188482284546), (0.0918029323220253, -0.6719170212745667),
        (0.0301042553037405, -0.350259393453598), (0.15513597428798676, -2.1334710121154785)]


class Steps:

    def __init__(self, eng, sem, base=0):
        self.eng, self.sem, self.base, self.n = eng, sem, base, 0

    def done(self, ins):
        ins.then_inc(self.sem, 1)
        self.n += 1

    def wait(self, held=None):
        self.eng.wait_ge(self.sem, self.base + self.n)
        if held is not None:
            self.eng.sem_inc(held, 1)


def at(m, n):
    return isinstance(m, int) and m == n


def identity(nc, pool, made, sem, n):
    nc.gpsimd.memset(made, 0.0).then_inc(sem, 1)
    pool.wait_ge(sem, n + 1)
    nc.gpsimd.affine_select(out=made, in_=made, compare_op=ALU.not_equal, fill=1.0, base=0,
                            pattern=[[-1, P]], channel_multiplier=1).then_inc(sem, 1)


def attention(nc, x, ctx, ctx_t, X, xT, ident, identb):
    with ExitStack() as st:
        def sb(name, shape, dt=F32):
            return st.enter_context(nc.sbuf_tensor(name, shape, dt))

        def sem(name):
            return st.enter_context(nc.semaphore(name))

        cb = [sb(f"a_ctx{p}", [P, CT, D]) for p in range(2)]
        q = sb("a_q", [P, CT, D])
        xn = sb("a_xn", [P, CT, D])
        qT = sb("a_qT", [P, KT, C])
        kT = sb("a_kT", [P, KT, C])
        prob = sb("a_prob", [P, CT, C])
        stats = sb("a_stats", [P, 2, CT, 2, 6])
        mv = sb("a_mv", [P, 2, CT, 2])
        ve = sb("a_ve", [P, 2, CT])
        rstd = sb("a_rstd", [P, 2, CT])
        power = sb("a_power", [P, CT])
        low = sb("a_low", [P, CT])
        bias = sb("a_bias", [P, CT])
        total = sb("a_total", [P, CT])
        rtotal = sb("a_rtotal", [P, CT])
        turned = [st.enter_context(nc.psum_tensor(f"a_turn{i}", [P, HW], F32)) for i in range(4)]
        scores = st.enter_context(nc.psum_tensor("a_scores", [P, CT, C], F32))
        cont = [st.enter_context(nc.psum_tensor(f"a_cont{i}", [P, HW], F32)) for i in range(2)]

        const = sem("a_const")
        x_in = [sem(f"a_x_in{p}") for p in range(2)]
        c_in = [sem(f"a_c_in{p}") for p in range(2)]
        kt_out = sem("a_kt_out")
        var_q = sem("a_var_q")
        var_x = sem("a_var_x")
        rstd_q = sem("a_rstd_q")
        rstd_x = sem("a_rstd_x")
        q_made = sem("a_q_made")
        t1 = sem("a_t1")
        t2 = sem("a_t2")
        qt_made = sem("a_qt_made")
        kt_made = sem("a_kt_made")
        scored = sem("a_scored")
        bias_made = sem("a_bias_made")
        exped = sem("a_exped")
        prob_made = sem("a_prob_made")
        cont_made = sem("a_cont_made")
        added = sem("a_added")
        xn_made = sem("a_xn_made")
        hi_made = sem("a_hi_made")
        lo_made = sem("a_lo_made")
        step = sem("a_step")
        held = sem("a_held")
        block = st.enter_context(nc.Block())

        x_rows = x.rearrange("b (a p) d -> b p a d", p=P)
        c_rows = ctx.rearrange("b (a p) d -> b p a d", p=P)
        ctx_tiles = ctx_t.rearrange("b k p c -> b p k c")

        def bodies(eng, body):
            body(0, 0, True, False)
            with eng.Fori(0, B // 2 - 1) as i:
                body(2 * i + 1, 1, True, True)
                body(2 * i + 2, 0, True, True)
            body(B - 1, 1, True, True)
            body(B, 0, False, True)

        @block.sync
        def _(sp):
            def load_x(n, p):
                sp.dma_start(X[:, bass.ds(CT * n, CT), :], x_rows[bass.ds(n, 1)].rearrange("o p a d -> (o p) a d")).then_inc(x_in[p], 16)

            def load_c(n, p):
                sp.dma_start(cb[p][:], c_rows[bass.ds(n, 1)].rearrange("o p a d -> (o p) a d")).then_inc(c_in[p], 16)

            def body(m, p, first, second):
                if first:
                    sp.wait_ge(kt_made, 4 * m + 4)
                    sp.dma_start(ctx_tiles[bass.ds(m, 1)].rearrange("o p k c -> (o p) k c"), kT[:]).then_inc(kt_out, 16)
                if first and second and not at(m, B - 1):
                    sp.wait_ge(cont_made, 4 * m)
                    load_c(m + 1, 1 - p)

            load_x(0, 0)
            load_c(0, 0)
            load_x(1, 1)
            load_c(1, 1)
            with sp.Fori(0, B // 2 - 1) as i:
                for p in range(2):
                    sp.wait_ge(x_in[p], 16 * i + 16)
                    load_x(2 * i + p + 2, p)
            bodies(sp, body)
            sp.wait_ge(kt_out, 16 * B)

        @block.gpsimd
        def _(pool):
            nc.gpsimd.memset(power[:], -0.5).then_inc(const, 1)
            identity(nc, pool, ident[:], const, 1)
            pool.wait_ge(const, 3)
            nc.gpsimd.tensor_copy(identb[:], ident[:]).then_inc(const, 1)
            pool.wait_ge(const, 4)

            def root(made, var, n):
                pool.wait_ge(var, n + 1)
                k = 0 if var is var_q else 1
                nc.gpsimd.tensor_tensor(rstd[:, k, :], ve[:, k, :], power[:], ALU.pow).then_inc(made, 1)

            def body(m, p, first, second):
                if second:
                    root(rstd_x, var_x, m - 1)
                if first and not at(m, B - 1):
                    root(rstd_q, var_q, m + 1)

            root(rstd_q, var_q, 0)
            bodies(pool, body)

        @block.scalar
        def _(act):
            def body(m, p, first, second):
                if first:
                    for f in range(4):
                        act.wait_ge(t1, 8 * m + 5 + f)
                        if f == 0 and not at(m, 0):
                            act.wait_ge(kt_out, 16 * m)
                        nc.scalar.activation(kT[:, 2 * f:2 * f + 2, :], turned[f][:].rearrange("p (k c) -> p k c", k=2),
                                             ACT.Copy, scale=-1.0).then_inc(kt_made, 1)
                    act.wait_ge(bias_made, m + 1)
                    for h in range(CT):
                        nc.scalar.activation(prob[:, h, :], scores[:, h, :], ACT.Exp, bias=bias[:, h:h + 1],
                                             scale=-1.0 / math.sqrt(C), accum_out=total[:, h:h + 1]).then_inc(exped, 1)
                if second:
                    for f in range(4):
                        a, kk = f // 2, f % 2
                        act.wait_ge(t2, 4 * m + f + 1)
                        nc.scalar.activation(xT[0][:, 4 * kk:4 * kk + 4, bass.ds((m - 1) * C + a * P, P)],
                                             turned[f][:].rearrange("p (k t) -> p k t", k=4),
                                             ACT.Copy).then_inc(hi_made, 1)

            bodies(act, body)

        @block.tensor
        def _(pe):
            pe.wait_ge(const, 4)

            def body(m, p, first, second):
                zero = at(m, 0)
                if first:
                    for f in range(8):
                        src = q if f < 4 else cb[p]
                        if f == 0:
                            pe.wait_ge(q_made, m + 1)
                        if f == 4:
                            pe.wait_ge(c_in[p], 8 * (m - p) + 16)
                        if f < 4 and not zero:
                            pe.wait_ge(lo_made, 4 * (m - 1) + f + 1)
                        if f >= 4:
                            pe.wait_ge(qt_made, 4 * m + f - 3)
                        for j in range(4):
                            k, a = 2 * (f % 4) + j // 2, j % 2
                            ins = nc.tensor.transpose(turned[f % 4][:, j * P:(j + 1) * P],
                                                      src[:, a, k * P:(k + 1) * P], ident[:])
                        ins.then_inc(t1, 1)
                if second:
                    pe.wait_ge(prob_made, m)
                    for o in range(4):
                        a, h = o // 2, o % 2
                        pe.wait_ge(added, 4 * (m - 1) + o + 1)
                        for d in range(CT):
                            ins = nc.tensor.matmul(cont[o % 2][:], prob[:, d, a * P:(a + 1) * P],
                                                   cb[1 - p][:, d, h * HW:(h + 1) * HW], start=(d == 0), stop=(d == CT - 1))
                        ins.then_inc(cont_made, 1)
                if first:
                    pe.wait_ge(kt_made, 4 * m + 4)
                    pe.wait_ge(qt_made, 4 * m + 4)
                    if not zero:
                        pe.wait_ge(exped, 2 * m)
                    for h in range(CT):
                        for k in range(KT):
                            ins = nc.tensor.matmul(scores[:, h, :], qT[:, k, h * P:(h + 1) * P], kT[:, k, :],
                                                   start=(k == 0), stop=(k == KT - 1))
                    ins.then_inc(scored, 1)
                if second:
                    pe.wait_ge(xn_made, m)
                    for f in range(4):
                        a, kk = f // 2, f % 2
                        if first:
                            pe.wait_ge(kt_made, 4 * m + f + 1)
                        else:
                            pe.wait_ge(lo_made, 4 * (m - 1) + f + 1)
                        for j in range(4):
                            k = 4 * kk + j
                            ins = nc.tensor.transpose(turned[f][:, j * P:(j + 1) * P], xn[:, a, k * P:(k + 1) * P], ident[:])
                        ins.then_inc(t2, 1)

            bodies(pe, body)

        @block.vector
        def _(dve):
            def variances(n, k, var):
                for a in range(CT):
                    for h in range(2):
                        ins = nc.vector.bn_stats(stats[:, k, a, h, :], X[:, bass.ds(CT * n + a, 1), h * HW:(h + 1) * HW])
                steps.done(ins)
                steps.wait(held)
                for a in range(CT):
                    ins = nc.vector.bn_aggr(mv[:, k, a, :], stats[:, k, a, :, :])
                steps.done(ins)
                steps.wait()
                nc.vector.tensor_scalar(ve[:, k, :], mv[:, k, :, 1], EPS, None, ALU.add).then_inc(var, 1)

            def normed(dst, n, k, made):
                for a in range(CT):
                    ins = nc.vector.tensor_scalar(dst[:, a:a + 1, :], X[:, bass.ds(CT * n + a, 1), :], mv[:, k, a, 0:1],
                                                  rstd[:, k, a:a + 1], ALU.subtract, ALU.mult)
                ins.then_inc(made, 1)

            def body(m, p, first, second):
                nonlocal steps
                steps = Steps(dve, step, 2 if at(m, 0) else 6 * m - 2 if at(m, B) else 6 * m)
                more = first and not at(m, B - 1)
                if first:
                    for f in range(4):
                        dve.wait_ge(t1, 8 * m + f + 1)
                        nc.vector.tensor_copy(qT[:, 2 * f:2 * f + 2, :],
                                              turned[f][:].rearrange("p (k c) -> p k c", k=2)).then_inc(qt_made, 1)
                if more:
                    dve.wait_ge(x_in[1 - p], 8 * (m + p) + 16)
                    dve.sem_inc(held, 1)
                    variances(m + 1, 0, var_q)
                if second:
                    for o in range(4):
                        a, h = o // 2, o % 2
                        dve.wait_ge(cont_made, 4 * (m - 1) + o + 1)
                        piece = X[:, bass.ds(CT * (m - 1) + a, 1), h * HW:(h + 1) * HW]
                        nc.vector.tensor_tensor(piece, piece, cont[o % 2][:].unsqueeze(1), ALU.add).then_inc(added, 1)
                    dve.wait_ge(added, 4 * m + 2)
                    dve.sem_inc(held, 1)
                    variances(m - 1, 1, var_x)
                if more:
                    dve.wait_ge(rstd_q, m + 2)
                    normed(q, m + 1, 0, q_made)
                if second:
                    dve.wait_ge(rstd_x, m)
                    dve.wait_ge(t2, 4 * m)
                    normed(xn, m - 1, 1, xn_made)
                if first:
                    dve.wait_ge(scored, m + 1)
                    steps.done(nc.vector.tensor_reduce(low[:], scores[:], AX.X, ALU.min))
                    steps.wait()
                    nc.vector.tensor_scalar(bias[:], low[:], 1.0 / math.sqrt(C), None, ALU.mult).then_inc(bias_made, 1)
                    dve.wait_ge(exped, 2 * m + 2)
                    steps.done(nc.vector.reciprocal(rtotal[:], total[:]))
                    steps.wait()
                    for h in range(CT):
                        ins = nc.vector.tensor_scalar(prob[:, h, :], prob[:, h, :], rtotal[:, h:h + 1], None, ALU.mult)
                    ins.then_inc(prob_made, 1)
                if second:
                    for f in range(4):
                        a, kk = f // 2, f % 2
                        cols = bass.ds((m - 1) * C + a * P, P)
                        dve.wait_ge(hi_made, 4 * (m - 1) + f + 1)
                        nc.vector.tensor_tensor(xT[1][:, 4 * kk:4 * kk + 4, cols],
                                                turned[f][:].rearrange("p (k t) -> p k t", k=4),
                                                xT[0][:, 4 * kk:4 * kk + 4, cols], ALU.subtract).then_inc(lo_made, 1)

            steps = Steps(dve, step)
            dve.sem_inc(lo_made, 4)
            dve.sem_inc(added, 2)
            dve.sem_inc(t2, 4)
            dve.wait_ge(x_in[0], 16)
            variances(0, 0, var_q)
            dve.wait_ge(rstd_q, 1)
            normed(q, 0, 0, q_made)
            bodies(dve, body)


CHUNK = 2
CHUNKS = NB // CHUNK
UNITS = 6 * CHUNK
GROUPS = NT * P // HW
PASSES = ((0, 0), (0, 1), (1, 0))
TILES = B * KT
TILE_CHUNK = 6


def unit(c, j):
    if j >= UNITS:
        c, j = c + 1, j - UNITS
    if at(c, CHUNKS - 1) and j >= 8:
        return None
    which, n, buf = (j // 2, CHUNK * c + 1, 1) if j < 4 else (2, CHUNK * c + (j - 4) // 2, (j - 4) // 2) if j < 8 else \
        ((j - 8) // 2, CHUNK * c + 2, 0)
    return which, n, j % 2, LAST if at(n, NB - 1) else P, buf


def number(c, j):
    return 4 + UNITS * c + j


def gated_ffn(nc, codes_in, scales_in, ctx_t, mask_t, X, xT, identb):
    with ExitStack() as st:
        def sb(name, shape, dt=F32):
            return st.enter_context(nc.sbuf_tensor(name, shape, dt))

        def ps(name, shape, dt=F32):
            return st.enter_context(nc.psum_tensor(name, shape, dt))

        def sem(name):
            return st.enter_context(nc.semaphore(name))

        code = [sb(f"b_code{i}", [P, HW], BF16) for i in range(3)]
        low_line = [sb(f"b_low_line{i}", [P, HW]) for i in range(4)]
        high_line = [sb(f"b_high_line{i}", [P, HW]) for i in range(4)]
        weight = [sb(f"b_weight{i}", [P, HW]) for i in range(2)]
        parts = [sb(f"b_parts{i}", [P, 2, HW], BF16) for i in range(2)]
        gu_w = [sb(f"b_gate_up{i}", [P, 2, 2, KT, P], BF16) for i in range(2)]
        dn_w = [sb(f"b_down{i}", [P, 2, D], BF16) for i in range(2)]
        inner = [[sb(f"b_inner{b}_{n}", [P, NT * P], BF16) for n in ("high", "low")] for b in range(CHUNK)]
        act_in = [sb(f"b_gated{i}", [P, HW]) for i in range(2)]
        gu_scale = [sb(f"b_scale{i}", [P, NB, D // SB]) for i in range(2)]
        dn_scale = sb("b_scale2", [P, KT, I // SB])
        left = [sb(f"b_left{i}", [P, C]) for i in range(2)]
        best = sb("b_best", [P, 8])
        line_bias = sb("b_line_bias", [P, 2, len(LOW)])
        mask = [sb(f"b_mask{i}", [P, C], BF16) for i in range(2)]
        gate_ps = [ps(f"b_gate_ps{i}", [P, HW]) for i in range(2)]
        up_ps = [ps(f"b_up_ps{i}", [P, HW]) for i in range(2)]
        turn_ps = [ps(f"b_turn_ps{i}", [P, 2, HW], BF16) for i in range(2)]
        down_ps = [ps(f"b_down_ps{i}", [P, HW]) for i in range(2)] + [gate_ps[1], up_ps[1]]

        scale_in = sem("b_scale_in")
        bias_made = sem("b_bias_made")
        code_in = [sem(f"b_code_in{i}") for i in range(3)]
        lined = sem("b_lined")
        paired = sem("b_paired")
        joined = sem("b_joined")
        decoded = sem("b_decoded")
        scaled = sem("b_scaled")
        high_made = sem("b_high_made")
        low_made = sem("b_low_made")
        turned = sem("b_turned")
        placed = sem("b_placed")
        gu_made = sem("b_gu_made")
        silu_made = sem("b_silu_made")
        gated = sem("b_gated")
        inner_high = sem("b_inner_high")
        inner_low = sem("b_inner_low")
        down_made = sem("b_down_made")
        added = sem("b_added")
        left_in = [sem(f"b_left_in{i}") for i in range(2)]
        found = sem("b_found")
        held, pool_held, sp_held = (sem(f"b_held_{e}") for e in ("dve", "pool", "sp"))
        mask_made = sem("b_mask_made")
        mask_out = [sem(f"b_mask_out{i}") for i in range(2)]
        block = st.enter_context(nc.Block())

        def size(un):
            which, _, _, r, _ = un
            return (r, HW) if which < 2 else (P, HW * r // P)

        def chunks(eng, chunk):
            with eng.Fori(0, CHUNKS - 2) as c:
                chunk(c)
            chunk(CHUNKS - 2)
            chunk(CHUNKS - 1)

        WITH_GROUP = (((0,), (1,), (2,), (3,)), ((4, 5), (6,), (7, 8), (9,)))
        WITH_TILE = {4: 10, 10: 11}

        @block.sync
        def _(sp):
            for i in range(2):
                sp.sem_inc(mask_out[i], 16)
            tiles = ctx_t.rearrange("b k p c -> (b k) p c")

            def load(t, i):
                sp.dma_start(left[i][:], tiles[bass.ds(t, 1)].rearrange("o p c -> (o p) c")).then_inc(left_in[i], 16)

            for which in range(2):
                sp.dma_start(gu_scale[which][:, 0:NB - 1, :],
                             scales_in[which][0:(NB - 1) * P, :].rearrange("(n p) s -> p n s", p=P)).then_inc(scale_in, 16)
                sp.dma_start(gu_scale[which][0:LAST, NB - 1, :], scales_in[which][(NB - 1) * P:I, :]).then_inc(scale_in, 16)
            sp.dma_start(dn_scale[:], scales_in[2].rearrange("(t p) s -> p t s", p=P)).then_inc(scale_in, 16)
            load(0, 0)
            load(1, 1)

            def chunk(c):
                for k in range(TILE_CHUNK):
                    t = TILE_CHUNK * c + k
                    if isinstance(t, int) and t >= TILES:
                        return
                    sp.wait_ge(mask_made, t + 1)
                    sp.sem_inc(sp_held, 1)
                    if not (isinstance(t, int) and t + 2 >= TILES):
                        load(t + 2, k % 2)
                    sp.dma_start(mask_t[bass.ds(t, 1)].rearrange("o p c -> (o p) c"), mask[k % 2][:]).then_inc(mask_out[k % 2], 16)

            chunks(sp, chunk)
            for i in range(2):
                sp.wait_ge(mask_out[i], 16 * (TILES // 2 + 1))

        @block.gpsimd
        def _(pool):
            pool.sem_inc(low_made, 2)
            pool.sem_inc(inner_low, 2)

            def load(c, j):
                un = unit(c, j)
                if un is None:
                    return
                which, n, half, r, _ = un
                slot = (j + 1) % 3
                if which < 2:
                    src = codes_in[which][bass.ds(n * P, r), half * HW:(half + 1) * HW]
                    dst = code[slot][0:r, :]
                else:
                    src = codes_in[2][half * HW:(half + 1) * HW, bass.ds(n * P, r)].rearrange("(t p) i -> p t i", p=P)
                    dst = code[slot][:, 0:4 * r].rearrange("p (t i) -> p t i", t=4)
                pool.dma_start(dst, src).then_inc(code_in[slot], 16)

            def low(c, j):
                a, n = size(unit(c, j))
                u = number(c, j)
                pool.wait_ge(high_made, u + 1)
                nc.gpsimd.tensor_tensor(parts[j % 2][0:a, 1, 0:n], weight[j % 2][0:a, 0:n], parts[j % 2][0:a, 0, 0:n],
                                        ALU.subtract).then_inc(low_made, 1)

            def pairs(c, j):
                un = unit(c, j)
                if un is None:
                    return
                a, n = size(un)
                u = number(c, j)
                for i, side in enumerate((low_line, high_line)):
                    pool.wait_ge(lined, 4 * u + i + 1)
                    nc.gpsimd.tensor_tensor(side[2][0:a, 0:n], side[2][0:a, 0:n], side[3][0:a, 0:n], ALU.add).then_inc(paired, 1)
                pool.wait_ge(paired, 3 * u + 2)
                nc.gpsimd.tensor_tensor(high_line[2][0:a, 0:n], high_line[2][0:a, 0:n], low_line[2][0:a, 0:n],
                                        ALU.subtract).then_inc(paired, 1)
                if unit(c, j + 3) is not None:
                    pool.wait_ge(lined, 4 * u + 4)
                    pool.sem_inc(pool_held, 1)
                    load(c, j + 3)

            def step(c, j):
                pairs(c, j + 1)
                low(c, j)

            for j in range(8, 11):
                load(-1, j)
            pairs(-1, 8)
            for j in range(8, 12):
                step(-1, j)

            def chunk(c):
                for b in range(CHUNK):
                    r = LAST if at(CHUNK * c + b, NB - 1) else P
                    for tg in range(GROUPS):
                        for j in WITH_GROUP[b][tg]:
                            if unit(c, j) is not None:
                                step(c, j)
                        g = 2 * GROUPS * c + GROUPS * b + tg
                        cols = slice(tg * HW, (tg + 1) * HW)
                        pool.wait_ge(inner_high, g + 1)
                        nc.gpsimd.tensor_tensor(inner[b][1][0:r, cols], act_in[tg % 2][0:r, :], inner[b][0][0:r, cols],
                                                ALU.subtract).then_inc(inner_low, 1)
                for j in WITH_TILE.values():
                    if unit(c, j) is not None:
                        step(c, j)

            chunks(pool, chunk)

        @block.scalar
        def _(act):
            act.sem_inc(placed, 2)

            def lines(c, j):
                un = unit(c, j)
                if un is None:
                    return
                a, n = size(un)
                u = number(c, j)
                act.wait_ge(code_in[(j + 1) % 3], 16 * (4 * c + (j + 4) // 3 + 1))
                for side, first in ((0, 2), (1, 2), (0, 0), (1, 0)):
                    if first == 2 and not at(u, 0):
                        act.wait_ge((paired, decoded)[side], (3, 1)[side] * u)
                    for i in (first, first + 1):
                        ins = nc.scalar.activation((low_line, high_line)[side][i][0:a, 0:n], code[(j + 1) % 3][0:a, 0:n], ACT.Relu,
                                                   bias=line_bias[0:a, side, i:i + 1], scale=(LOW, HIGH)[side][i][0])
                    ins.then_inc(lined, 1)

            def high(c, j):
                a, n = size(unit(c, j))
                u = number(c, j)
                act.wait_ge(scaled, u + 1)
                act.wait_ge(turned, u + 1)
                nc.scalar.activation(parts[j % 2][0:a, 0, 0:n], weight[j % 2][0:a, 0:n], ACT.Copy).then_inc(high_made, 1)

            def place(c, j):
                which, n, half, r, buf = unit(c, j)
                u = number(c, j)
                act.wait_ge(turned, u + 3)
                if which < 2:
                    dst = gu_w[buf][:, which, :, 4 * half:4 * half + 4, 0:r]
                    src = turn_ps[j % 2][:, :, 0:4 * r].rearrange("p h (k i) -> p h k i", k=4)
                else:
                    dst = dn_w[buf][0:r, :, half * HW:(half + 1) * HW]
                    src = turn_ps[j % 2][0:r, :, :]
                nc.scalar.activation(dst, src, ACT.Copy).then_inc(placed, 1)

            def step(c, j):
                lines(c, j + 1)
                high(c, j)

            act.wait_ge(bias_made, 1)
            lines(-1, 8)
            for j in range(8, 12):
                step(-1, j)
                place(-1, j)

            def chunk(c):
                for b in range(CHUNK):
                    r = LAST if at(CHUNK * c + b, NB - 1) else P
                    for tg in range(GROUPS):
                        units = [j for j in WITH_GROUP[b][tg] if unit(c, j) is not None]
                        for j in units:
                            step(c, j)
                        g = 2 * GROUPS * c + GROUPS * b + tg
                        act.wait_ge(gu_made, g + 1)
                        act.wait_ge(inner_low, g + 1)
                        nc.scalar.activation(act_in[tg % 2][0:r, :], gate_ps[tg % 2][0:r, :], ACT.Silu).then_inc(silu_made, 1)
                        act.wait_ge(gated, g + 3)
                        nc.scalar.activation(inner[b][0][0:r, tg * HW:(tg + 1) * HW], act_in[tg % 2][0:r, :],
                                             ACT.Copy).then_inc(inner_high, 1)
                        for j in units:
                            place(c, j)
                for j in WITH_TILE.values():
                    if unit(c, j) is not None:
                        step(c, j)
                        place(c, j)

            chunks(act, chunk)

        @block.tensor
        def _(pe):
            pe.sem_inc(turned, 2)

            def turn(c, j):
                which, n, half, r, buf = unit(c, j)
                u = number(c, j)
                pe.wait_ge(low_made, u + 3)
                pe.wait_ge(placed, u + 1)
                for h in range(2):
                    for k in range(4):
                        if which < 2:
                            ins = nc.tensor.transpose(turn_ps[j % 2][:, h, k * r:(k + 1) * r],
                                                      parts[j % 2][0:r, h, k * P:(k + 1) * P], identb[0:r, 0:r])
                        else:
                            ins = nc.tensor.transpose(turn_ps[j % 2][0:r, h, k * P:(k + 1) * P],
                                                      parts[j % 2][:, h, k * r:(k + 1) * r], identb[:])
                ins.then_inc(turned, 1)

            for j in range(8, 12):
                turn(-1, j)

            def chunk(c):
                for b in range(CHUNK):
                    r = LAST if at(CHUNK * c + b, NB - 1) else P
                    pe.wait_ge(placed, (number(c, 0) if b == 0 else number(c, 4)) + 2)
                    for tg in range(GROUPS):
                        g = 2 * GROUPS * c + GROUPS * b + tg
                        pe.wait_ge(gated, g + 1)
                        if b == 0 and tg == 1:
                            pe.wait_ge(added, 2 * NT * c + 4)
                        for which in range(2):
                            out = (gate_ps, up_ps)[which][tg % 2][0:r, :]
                            for k in range(KT):
                                for n, (wp, xp) in enumerate(PASSES):
                                    ins = nc.tensor.matmul(out, gu_w[b][:, which, wp, k, 0:r], xT[xp][:, k, tg * HW:(tg + 1) * HW],
                                                           start=(k == 0 and n == 0), stop=(k == KT - 1 and n == 2))
                        ins.then_inc(gu_made, 1)
                        for j in WITH_GROUP[b][tg]:
                            if unit(c, j) is not None:
                                turn(c, j)
                pe.wait_ge(placed, number(c, 8) + 2)
                for t in range(NT):
                    if t % 4 == 0:
                        pe.wait_ge(inner_low, 2 * GROUPS * c + GROUPS + t // 4 + 3)
                    for h in range(2):
                        o = 2 * t + h
                        if o == 2:
                            pe.wait_ge(gated, 2 * GROUPS * (c + 1) + 2)
                        pe.wait_ge(added, 2 * NT * c + o + 1)
                        for b in range(CHUNK):
                            r = LAST if at(CHUNK * c + b, NB - 1) else P
                            for n, (wp, xp) in enumerate(PASSES):
                                ins = nc.tensor.matmul(down_ps[o % 4][:], inner[b][xp][0:r, t * P:(t + 1) * P],
                                                       dn_w[b][0:r, wp, h * HW:(h + 1) * HW],
                                                       start=(b == 0 and n == 0), stop=(b == CHUNK - 1 and n == 2))
                        ins.then_inc(down_made, 1)
                    if t in WITH_TILE and unit(c, WITH_TILE[t]) is not None:
                        turn(c, WITH_TILE[t])

            chunks(pe, chunk)

        @block.vector
        def _(dve):
            def join(c, j):
                which, n, half, r, _ = un = unit(c, j)
                a, m = size(un)
                u = number(c, j)
                lo, hi = ([x[0:a, 0:m] for x in side] for side in (low_line, high_line))
                w = weight[j % 2][0:a, 0:m]
                dve.wait_ge(lined, 4 * u + 3)
                dve.wait_ge(low_made, u + 1)
                nc.vector.tensor_tensor(w, lo[0], lo[1], ALU.max)
                dve.wait_ge(lined, 4 * u + 4)
                nc.vector.tensor_tensor(hi[0], hi[0], hi[1], ALU.max).then_inc(joined, 1)
                dve.wait_ge(joined, 2 * u + 1)
                nc.vector.tensor_tensor(w, hi[0], w, ALU.subtract).then_inc(joined, 1)
                dve.wait_ge(joined, 2 * u + 2)
                dve.wait_ge(paired, 3 * u + 3)
                nc.vector.tensor_tensor(w, w, hi[2], ALU.add).then_inc(decoded, 1)
                if which < 2:
                    scale = gu_scale[which][0:r, bass.ds(n, 1), 8 * half:8 * half + 8].rearrange("p o s -> p (o s)")
                    scale = scale.unsqueeze(2).to_broadcast([r, HW // SB, SB])
                    w = w.rearrange("p (s i) -> p s i", i=SB)
                else:
                    scale = dn_scale[:, 4 * half:4 * half + 4, bass.ds(n * (P // SB), r // SB)]
                    scale = scale.unsqueeze(3).to_broadcast([P, 4, r // SB, SB])
                    w = w.rearrange("p (t s i) -> p t s i", t=4, i=SB)
                dve.wait_ge(decoded, u + 1)
                nc.vector.tensor_tensor(w, w, scale, ALU.mult).then_inc(scaled, 1)

            steps = None

            def rounds(c, k, first, last):
                row = left[k % 2][:, ::-1]
                if first == 0:
                    dve.wait_ge(left_in[k % 2], 16 * (3 * c + k // 2 + 1))
                    dve.sem_inc(held, 1)
                for n in range(first, last):
                    if n:
                        steps.wait()
                    steps.done(nc.vector.max(best[:], row))
                    steps.wait()
                    if n == ROUNDS - 1 and REST % 8:
                        steps.done(nc.vector.memset(best[:, REST % 8:8], GONE))
                        steps.wait()
                    steps.done(nc.vector.match_replace(row, best[:], row, GONE))
                if last == ROUNDS:
                    steps.wait()
                    dve.wait_ge(mask_out[k % 2], 16 * (3 * c + k // 2 + 1))
                    nc.vector.tensor_scalar(mask[k % 2][:], left[k % 2][:], GONE, None, ALU.is_gt).then_inc(mask_made, 1)

            def tile_of(c, k):
                t = TILE_CHUNK * c + k
                return not (isinstance(t, int) and t >= TILES)

            dve.sem_inc(gated, 2)
            dve.sem_inc(added, 4)
            for side, table in enumerate((LOW, HIGH)):
                for i, (_, bias) in enumerate(table):
                    ins = nc.vector.memset(line_bias[:, side, i:i + 1], bias)
            ins.then_inc(bias_made, 1)
            dve.wait_ge(scale_in, 16 * 5)
            for j in range(8, 12):
                join(-1, j)

            def chunk(c):
                nonlocal steps
                steps = Steps(dve, found)
                half = ROUNDS // 2
                for b in range(CHUNK):
                    r = LAST if at(CHUNK * c + b, NB - 1) else P
                    for tg in range(GROUPS):
                        for j in WITH_GROUP[b][tg]:
                            if unit(c, j) is not None:
                                join(c, j)
                            if j < 8 and tile_of(c, j // 2):
                                rounds(c, j // 2, *((0, half) if j % 2 == 0 else (half, ROUNDS)))
                        g = 2 * GROUPS * c + GROUPS * b + tg
                        dve.wait_ge(silu_made, g + 1)
                        nc.vector.tensor_tensor(act_in[tg % 2][0:r, :], act_in[tg % 2][0:r, :], up_ps[tg % 2][0:r, :],
                                                ALU.mult).then_inc(gated, 1)
                for t in range(NT):
                    for h in range(2):
                        o = 2 * t + h
                        piece = X[:, t, h * HW:(h + 1) * HW]
                        dve.wait_ge(down_made, 2 * NT * c + o + 1)
                        nc.vector.tensor_tensor(piece, piece, down_ps[o % 4][:], ALU.add).then_inc(added, 1)
                        k = 4 + o // ROUNDS
                        if k < TILE_CHUNK and tile_of(c, k):
                            rounds(c, k, o % ROUNDS, o % ROUNDS + 1)
                    if t in WITH_TILE and unit(c, WITH_TILE[t]) is not None:
                        join(c, WITH_TILE[t])
                steps.wait()
                dve.sem_clear(found)

            chunks(dve, chunk)



def rows_variances(nc, dve, steps, held, X, n, stats, mv, ve, var):
    for a in range(CT):
        for h in range(2):
            ins = nc.vector.bn_stats(stats[:, a, h, :], X[:, bass.ds(CT * n + a, 1), h * HW:(h + 1) * HW])
    steps.done(ins)
    steps.wait(held)
    for a in range(CT):
        ins = nc.vector.bn_aggr(mv[:, a, :], stats[:, a, :, :])
    steps.done(ins)
    steps.wait()
    nc.vector.tensor_scalar(ve[:], mv[:, :, 1], EPS, None, ALU.add).then_inc(var, 1)


def pair_bodies(eng, body):
    with eng.Fori(0, B // 2 - 1) as i:
        body(2 * i, 0)
        body(2 * i + 1, 1)
    body(B - 2, 0)
    body(B - 1, 1)


EXPONENT = 0x7F800000
TO_GRID = 1.5 * 2.0 ** 20
FP8_LEAST = 2.0 ** -6
FP8_MOST = 448.0
OVERFLOW = 7.4e35


def pooled(nc, mask_t, conv, gamma, beta, weight, w_scale, X, xlT, gates, w8, ident):
    with ExitStack() as st:
        def sb(name, shape, dt=F32):
            return st.enter_context(nc.sbuf_tensor(name, shape, dt))

        def sem(name):
            return st.enter_context(nc.semaphore(name))

        mask = [sb(f"c_mask{p}", [P, KT, C], BF16) for p in range(2)]
        xn = [sb(f"c_xn{p}", [P, CT, D]) for p in range(2)]
        inside = sb("c_inside", [P, KT, C])
        outside = sb("c_outside", [P, KT, C])
        junk = sb("c_junk", [P, KT, C], BF16)
        stats = sb("c_stats", [P, CT, 2, 6])
        mv = sb("c_mv", [P, CT, 2])
        ve = sb("c_ve", [P, CT])
        rstd = sb("c_rstd", [P, CT])
        power = sb("c_power", [P, CT])
        feat = sb("c_feat", [P, 2, 2, TILES])
        sums = sb("c_sums", [P, 2, TILES])
        taps = sb("c_taps", [P, 2, 7])
        joint = sb("c_joint", [P, 3 * P + 6])
        band = sb("c_band", [P, 2, 3 * P])
        ones = sb("c_ones", [P, P])
        z = sb("c_z", [P, 2, TILES])
        zsq = sb("c_zsq", [P, 2, TILES])
        zsum = sb("c_zsum", [P, 2])
        mean = sb("c_mean", [P, 2])
        zvar = sb("c_zvar", [P, 2])
        zrstd = sb("c_zrstd", [P, 2])
        affine = sb("c_affine", [P, 2])
        gate = sb("c_gate", [P, 2, TILES])
        ws = sb("c_ws", [P, 2])
        wf = sb("c_wf", [P, D])
        wm = sb("c_wm", [P, D])
        turn_ps = [st.enter_context(nc.psum_tensor(f"c_turn{i}", [P, 2, C], F32)) for i in range(4)]
        z_ps = st.enter_context(nc.psum_tensor("c_z_ps", [P, 2, TILES], F32))
        sum_ps = st.enter_context(nc.psum_tensor("c_sum_ps", [P, 2, 2], F32))

        small_in = sem("c_small_in")
        mask_in = [sem(f"c_mask_in{p}") for p in range(2)]
        w_in = sem("c_w_in")
        const = sem("c_const")
        inverse = sem("c_inverse")
        var = sem("c_var")
        root = sem("c_root")
        normed = sem("c_normed")
        turned = sem("c_turned")
        placed = sem("c_placed")
        in_made = sem("c_in_made")
        out_made = sem("c_out_made")
        out_max = sem("c_out_max")
        in_sum = sem("c_in_sum")
        out_sum = sem("c_out_sum")
        w_scaled = sem("c_w_scaled")
        w_grid = sem("c_w_grid")
        w_added = sem("c_w_added")
        w_round = sem("c_w_round")
        w_done = sem("c_w_done")
        averaged = sem("c_averaged")
        convolved = sem("c_convolved")
        summed = sem("c_summed")
        totalled = sem("c_totalled")
        zvared = sem("c_zvared")
        zroot = sem("c_zroot")
        znormed = sem("c_znormed")
        gated = sem("c_gated")
        step = sem("c_step")
        held, act_held = (sem(f"c_held_{e}") for e in ("dve", "act"))
        block = st.enter_context(nc.Block())
        masks = mask_t.rearrange("(b k) p c -> b p k c", k=KT)
        w_rows = weight.rearrange("(k p) o -> k p o", p=P)

        @block.sync
        def _(sp):
            def load_mask(b, p):
                sp.dma_start(mask[p][:], masks[bass.ds(b, 1)].rearrange("o p k c -> (o p) k c")).then_inc(mask_in[p], 16)

            def load_w(k):
                sp.dma_start(wf[:], w_rows[bass.ds(k, 1)].rearrange("o p n -> (o p) n")).then_inc(w_in, 16)

            sp.dma_start(ws[:, 0:1], w_scale.partition_broadcast(P)).then_inc(small_in, 16)
            sp.dma_start(taps[:], conv.rearrange("o c t -> (o c) t").partition_broadcast(P)).then_inc(small_in, 16)
            sp.dma_start(affine[:, 0:1], gamma.partition_broadcast(P)).then_inc(small_in, 16)
            sp.dma_start(affine[:, 1:2], beta.partition_broadcast(P)).then_inc(small_in, 16)
            load_mask(0, 0)
            load_mask(1, 1)
            load_w(0)

            def body(b, p):
                sp.wait_ge(in_made, b)
                load_mask(b + 1, 1 - p)
                sp.wait_ge(w_done, b)
                load_w(b)

            with sp.Fori(0, B // 2 - 1) as i:
                body(2 * i + 1, 1)
                body(2 * i + 2, 0)
            sp.wait_ge(w_done, B - 1)
            load_w(B - 1)

        @block.gpsimd
        def _(pool):
            nc.gpsimd.memset(power[:], -0.5).then_inc(const, 1)
            nc.gpsimd.memset(ones[:], 1.0).then_inc(const, 1)

            def rstd_of(b):
                pool.wait_ge(var, b + 1)
                nc.gpsimd.tensor_tensor(rstd[:], ve[:], power[:], ALU.pow).then_inc(root, 1)

            pool.wait_ge(const, 2)
            rstd_of(0)
            nc.gpsimd.memset(joint[:], 0.0).then_inc(const, 1)
            pool.wait_ge(const, 3)
            nc.gpsimd.affine_select(out=joint[:], in_=joint[:], compare_op=ALU.not_equal, fill=1.0, base=P + 3,
                                    pattern=[[-1, 3 * P + 6]], channel_multiplier=1).then_inc(const, 1)

            def body(b, p):
                if not at(b, B - 1):
                    rstd_of(b + 1)
                pool.wait_ge(w_grid, b + 1)
                nc.gpsimd.tensor_tensor(wf[:], wf[:], wm[:], ALU.add).then_inc(w_added, 1)
                pool.wait_ge(w_added, b + 1)
                nc.gpsimd.tensor_tensor(wf[:], wf[:], wm[:], ALU.subtract).then_inc(w_round, 1)
                pool.wait_ge(in_made, b + 1)
                pool.wait_ge(out_max, b + 1)
                pool.wait_ge(out_sum, 8 * b + 8)
                nc.gpsimd.tensor_tensor(outside[:], xlT[:, bass.ds(KT * b, KT), :], inside[:], ALU.subtract).then_inc(out_made, 1)

            pair_bodies(pool, body)
            pool.wait_ge(zvared, 1)
            nc.gpsimd.tensor_tensor(zrstd[:], zvar[:], power[:], ALU.pow).then_inc(zroot, 1)

        @block.scalar
        def _(act):
            act.sem_inc(out_sum, KT)
            act.sem_inc(in_sum, KT)
            act.sem_inc(placed, 4)
            act.wait_ge(inverse, 1)

            def body(b, p):
                act.wait_ge(w_in, 16 * b + 16)
                nc.scalar.activation(wf[:], wf[:], ACT.Copy, scale=ws[:, 1:2]).then_inc(w_scaled, 1)
                for f in range(4):
                    act.wait_ge(turned, 4 * b + f + 9)
                    nc.scalar.activation(xlT[:, bass.ds(KT * b + 2 * f, 2), :], turn_ps[f][:], ACT.Copy).then_inc(placed, 1)
                for s in range(2):
                    act.wait_ge((in_made, out_made)[s], b + 1 + s)
                    act.wait_ge((out_sum, in_sum)[s], KT * (b + s) + KT)
                    act.sem_inc(act_held, 1)
                    for k in range(KT):
                        nc.scalar.activation(junk[:, k, :], (inside, outside)[s][:, k, :], ACT.Copy,
                                             accum_out=sums[:, s, bass.ds(KT * b + k, 1)]).then_inc((in_sum, out_sum)[s], 1)

            pair_bodies(act, body)
            act.wait_ge(znormed, 1)
            nc.scalar.activation(gate[:], z[:], ACT.Sigmoid).then_inc(gated, 1)

        @block.tensor
        def _(pe):
            pe.sem_inc(turned, 8)

            def body(b, p):
                pe.wait_ge(normed, b + 1)
                for f in range(4):
                    pe.wait_ge(placed, 4 * b + f + 1)
                    for j in range(4):
                        k, a = 2 * f + j // 2, j % 2
                        ins = nc.tensor.transpose(turn_ps[f][:, j // 2, a * P:(a + 1) * P], xn[p][:, a, k * P:(k + 1) * P], ident[:])
                    ins.then_inc(turned, 1)

            pair_bodies(pe, body)
            pe.wait_ge(averaged, 1)
            n = 0
            for c in range(2):
                f3 = feat[:, c, :, :].rearrange("p s (b k) -> p (s b) k", k=KT)
                z3 = z_ps[:].rearrange("p s (b k) -> p (s b) k", k=KT)
                for lo, dst, src in ((P, slice(0, KT), slice(0, KT)), (2 * P, slice(1, KT), slice(0, KT - 1)),
                                     (0, slice(0, KT - 1), slice(1, KT))):
                    ins = nc.tensor.matmul(z3[:, :, dst], band[:, c, lo:lo + P], f3[:, :, src], start=(n == 0), stop=(n == 5),
                                           skip_group_check=True)
                    n += 1
            ins.then_inc(convolved, 1)
            for i in range(2):
                pe.wait_ge(summed, i + 1)
                nc.tensor.matmul(sum_ps[:, i, :], ones[:], zsum[:], start=True, stop=True).then_inc(totalled, 1)

        @block.vector
        def _(dve):
            dve.sem_inc(out_made, 1)
            dve.sem_inc(out_max, 1)
            dve.wait_ge(small_in, 64)
            nc.vector.reciprocal(ws[:, 1:2], ws[:, 0:1]).then_inc(inverse, 1)
            steps = Steps(dve, step)
            rows_variances(nc, dve, steps, held, X, 0, stats, mv, ve, var)

            def norm(b, p):
                dve.wait_ge(root, b + 1)
                dve.wait_ge(turned, 4 * b + 4)
                for a in range(CT):
                    ins = nc.vector.tensor_scalar(xn[p][:, a:a + 1, :], X[:, bass.ds(CT * b + a, 1), :], mv[:, a, 0:1],
                                                  rstd[:, a:a + 1], ALU.subtract, ALU.mult)
                ins.then_inc(normed, 1)

            norm(0, 0)
            dve.wait_ge(const, 4)
            for c in range(2):
                for t in range(7):
                    if t == 0:
                        steps.done(nc.vector.tensor_scalar(band[:, c, :], joint[:, t:t + 3 * P], taps[:, c, t:t + 1], None, ALU.mult))
                    else:
                        steps.wait()
                        steps.done(nc.vector.scalar_tensor_tensor(band[:, c, :], joint[:, t:t + 3 * P], taps[:, c, t:t + 1], band[:, c, :],
                                                                  ALU.mult, ALU.add))
            before = steps.n

            def body(b, p):
                nonlocal steps
                steps = Steps(dve, step, before + 4 * b)
                if not at(b, B - 1):
                    rows_variances(nc, dve, steps, held, X, b + 1, stats, mv, ve, var)
                dve.wait_ge(w_scaled, b + 1)
                steps.done(nc.vector.tensor_scalar(wm[:].bitcast(I32), wf[:].bitcast(I32), EXPONENT, None, ALU.bitwise_and))
                steps.wait()
                nc.vector.tensor_scalar(wm[:], wm[:], FP8_LEAST, TO_GRID, ALU.max, ALU.mult).then_inc(w_grid, 1)
                dve.wait_ge(placed, 4 * b + 8)
                dve.wait_ge(mask_in[p], 8 * (b - p) + 16)
                dve.wait_ge(in_sum, KT * b + KT)
                dve.wait_ge(out_made, b + 1)
                nc.vector.tensor_tensor(inside[:], xlT[:, bass.ds(KT * b, KT), :], mask[p][:], ALU.mult).then_inc(in_made, 1)
                if not at(b, B - 1):
                    norm(b + 1, 1 - p)
                dve.wait_ge(in_made, b + 1)
                nc.vector.tensor_reduce(feat[:, 0, 0, bass.ds(KT * b, KT)], inside[:], AX.X, ALU.max)
                dve.wait_ge(w_round, b + 1)
                steps.done(nc.vector.tensor_scalar(wm[:], wf[:], OVERFLOW, 0.0, ALU.mult, ALU.mult))
                steps.wait()
                nc.vector.tensor_tensor(w8[:, bass.ds(b, 1), :], wm[:].unsqueeze(1), wf[:].unsqueeze(1), ALU.add).then_inc(w_done, 1)
                dve.wait_ge(out_made, b + 2)
                nc.vector.tensor_reduce(feat[:, 0, 1, bass.ds(KT * b, KT)], outside[:], AX.X, ALU.max).then_inc(out_max, 1)

            pair_bodies(dve, body)
            steps = Steps(dve, step, before + 4 * B - 2)
            dve.wait_ge(in_sum, KT * (B + 1))
            dve.wait_ge(out_sum, KT * (B + 1))
            for s, n in enumerate((TOPK, REST)):
                ins = nc.vector.tensor_scalar(feat[:, 1, s, :], sums[:, s, :], 1.0 / C, C / n, ALU.mult, ALU.mult)
            ins.then_inc(averaged, 1)
            dve.wait_ge(convolved, 1)
            steps.done(nc.vector.tensor_copy(z[:], z_ps[:]))
            steps.wait()
            nc.vector.tensor_reduce(zsum[:], z[:], AX.X, ALU.add).then_inc(summed, 1)
            dve.wait_ge(totalled, 1)
            steps.done(nc.vector.tensor_scalar(mean[:], sum_ps[:, 0, :], 1.0 / (B * D), None, ALU.mult))
            steps.wait()
            for s in range(2):
                ins = nc.vector.tensor_scalar(z[:, s, :], z[:, s, :], mean[:, s:s + 1], None, ALU.subtract)
            steps.done(ins)
            steps.wait()
            steps.done(nc.vector.tensor_tensor(zsq[:], z[:], z[:], ALU.mult))
            steps.wait()
            nc.vector.tensor_reduce(zsum[:], zsq[:], AX.X, ALU.add).then_inc(summed, 1)
            dve.wait_ge(totalled, 2)
            nc.vector.tensor_scalar(zvar[:], sum_ps[:, 1, :], 1.0 / (B * D), EPS, ALU.mult, ALU.add).then_inc(zvared, 1)
            dve.wait_ge(zroot, 1)
            for s in range(2):
                ins = nc.vector.tensor_scalar(z[:, s, :], z[:, s, :], zrstd[:, s:s + 1], affine[:, 0:1], ALU.mult, ALU.mult)
            steps.done(ins)
            steps.wait()
            nc.vector.tensor_scalar(z[:], z[:], affine[:, 1:2], 0.0, ALU.add, ALU.max).then_inc(znormed, 1)
            dve.wait_ge(gated, 1)
            nc.vector.tensor_tensor(gates[:, 0, :], gate[:, 0, :], gate[:, 1, :], ALU.subtract)
            nc.vector.tensor_copy(gates[:, 1, :], gate[:, 1, :])


def apply_gates(nc, mask_t, X, xlT, gates, ident):
    with ExitStack() as st:
        def sb(name, shape, dt=F32):
            return st.enter_context(nc.sbuf_tensor(name, shape, dt))

        def sem(name):
            return st.enter_context(nc.semaphore(name))

        mask = [sb(f"e_mask{p}", [P, KT, C], BF16) for p in range(2)]
        own = [sb(f"e_own{p}", [P, 2, KT]) for p in range(2)]
        part = [sb(f"e_part{p}", [P, KT, C]) for p in range(2)]
        turn_ps = [st.enter_context(nc.psum_tensor(f"e_turn{i}", [P, HW], F32)) for i in range(4)]
        mask_in = [sem(f"e_mask_in{p}") for p in range(2)]
        owned = sem("e_owned")
        chosen = sem("e_chosen")
        multiplied = sem("e_multiplied")
        turned = sem("e_turned")
        added = sem("e_added")
        act_held = sem("e_held_act")
        block = st.enter_context(nc.Block())
        masks = mask_t.rearrange("(b k) p c -> b p k c", k=KT)

        @block.sync
        def _(sp):
            def load_mask(b, p):
                sp.dma_start(mask[p][:], masks[bass.ds(b, 1)].rearrange("o p k c -> (o p) k c")).then_inc(mask_in[p], 16)

            load_mask(0, 0)
            load_mask(1, 1)
            with sp.Fori(0, B // 2 - 1) as i:
                for p in range(2):
                    sp.wait_ge(chosen, KT * (2 * i + p) + KT + 16)
                    load_mask(2 * i + p + 2, p)

        @block.scalar
        def _(act):
            act.sem_inc(chosen, 2 * KT)

            def body(b, p):
                act.wait_ge(mask_in[p], 8 * (b - p) + 16)
                act.wait_ge(owned, b + 1)
                act.wait_ge(turned, 4 * b + 4)
                act.sem_inc(act_held, 1)
                for k in range(KT):
                    nc.scalar.activation(part[p][:, k, :], mask[p][:, k, :], ACT.Identity, scale=own[p][:, 0, k:k + 1],
                                         bias=own[p][:, 1, k:k + 1]).then_inc(chosen, 1)

            pair_bodies(act, body)

        @block.tensor
        def _(pe):
            pe.sem_inc(turned, 8)

            def body(b, p):
                pe.wait_ge(multiplied, b + 1)
                for f in range(4):
                    a, h = f // 2, f % 2
                    pe.wait_ge(added, 4 * b + f + 1)
                    for j in range(4):
                        ins = nc.tensor.transpose(turn_ps[f][:, j * P:(j + 1) * P], part[p][:, 4 * h + j, a * P:(a + 1) * P], ident[:])
                    ins.then_inc(turned, 1)

            pair_bodies(pe, body)

        @block.vector
        def _(dve):
            dve.sem_inc(added, 4)

            def take(b, p):
                dve.wait_ge(chosen, KT * b + KT)
                nc.vector.tensor_copy(own[p][:], gates[:, :, bass.ds(KT * b, KT)]).then_inc(owned, 1)

            take(0, 0)
            take(1, 1)

            def body(b, p):
                dve.wait_ge(chosen, KT * b + KT + 16)
                nc.vector.tensor_tensor(part[p][:], part[p][:], xlT[:, bass.ds(KT * b, KT), :], ALU.mult).then_inc(multiplied, 1)
                if not (isinstance(b, int) and b >= B - 2):
                    take(b + 2, p)
                for f in range(4):
                    a, h = f // 2, f % 2
                    piece = X[:, bass.ds(CT * b + a, 1), h * HW:(h + 1) * HW]
                    dve.wait_ge(turned, 4 * b + f + 9)
                    nc.vector.tensor_tensor(piece, piece, turn_ps[f][:].unsqueeze(1), ALU.add).then_inc(added, 1)

            pair_bodies(dve, body)


def fp8_ffn(nc, bias, in_scale, w_scale, out, X, w8, identb):
    with ExitStack() as st:
        def sb(name, shape, dt=F32):
            return st.enter_context(nc.sbuf_tensor(name, shape, dt))

        def ps(name, shape, dt=F32):
            return st.enter_context(nc.psum_tensor(name, shape, dt))

        def sem(name):
            return st.enter_context(nc.semaphore(name))

        stats = sb("d_stats", [P, CT, 2, 6])
        mv = sb("d_mv", [P, CT, 2])
        ve = sb("d_ve", [P, CT])
        rstd = sb("d_rstd", [P, CT])
        power = sb("d_power", [P, CT])
        rate = [sb(f"d_rate{p}", [P, CT]) for p in range(2)]
        offset = [sb(f"d_offset{p}", [P, CT]) for p in range(2)]
        y = [sb(f"d_y{p}", [P, CT, D]) for p in range(2)]
        grid = [sb(f"d_grid{p}", [P, CT, D]) for p in range(2)]
        x8 = [sb(f"d_x8_{p}", [P, CT, D], BF16) for p in range(2)]
        x8T = [sb(f"d_x8T{p}", [P, CT, KT, P], BF16) for p in range(2)]
        most = sb("d_most", [P, CT])
        flag = sb("d_flag", [P, CT])
        back = [sb(f"d_back{p}", [P, CT]) for p in range(2)]
        scales = sb("d_scales", [P, 4])
        bias_row = sb("d_bias", [P, 1, D])
        made = [sb(f"d_out{p}", [P, CT, D]) for p in range(2)]
        turn_ps = [ps(f"d_turn{i}", [P, KT, P], BF16) for i in range(2)]
        out_ps = [ps(f"d_out_ps{i}", [P, HW]) for i in range(4)]

        small_in = sem("d_small_in")
        const = sem("d_const")
        inverse = sem("d_inverse")
        var = sem("d_var")
        root = sem("d_root")
        rated = sem("d_rated")
        scaled = sem("d_scaled")
        gridded = sem("d_gridded")
        lifted = sem("d_lifted")
        biased = sem("d_biased")
        rounded = sem("d_rounded")
        backed = sem("d_backed")
        turned = sem("d_turned")
        placed = sem("d_placed")
        multiplied = sem("d_multiplied")
        finished = sem("d_finished")
        stored = [sem(f"d_stored{p}") for p in range(2)]
        step = sem("d_step")
        held, pool_held = (sem(f"d_held_{e}") for e in ("dve", "pool"))
        block = st.enter_context(nc.Block())
        out_rows = out.rearrange("b (a p) d -> b p a d", p=P)

        @block.sync
        def _(sp):
            sp.dma_start(scales[:, 0:1], in_scale.partition_broadcast(P)).then_inc(small_in, 16)
            sp.dma_start(scales[:, 1:2], w_scale.partition_broadcast(P)).then_inc(small_in, 16)
            sp.dma_start(bias_row[:, 0, :], bias.partition_broadcast(P)).then_inc(small_in, 16)
            for p in range(2):
                sp.sem_inc(stored[p], 16)

            def body(b, p):
                sp.wait_ge(finished, 4 * b + 8)
                sp.dma_start(out_rows[bass.ds(b, 1)].rearrange("o p a d -> (o p) a d"), made[p][:]).then_inc(stored[p], 16)

            pair_bodies(sp, body)
            for p in range(2):
                sp.wait_ge(stored[p], 8 * B + 16)

        @block.gpsimd
        def _(pool):
            nc.gpsimd.memset(power[:], -0.5).then_inc(const, 1)
            pool.wait_ge(const, 1)

            def rstd_of(b):
                pool.wait_ge(var, b + 1)
                nc.gpsimd.tensor_tensor(rstd[:], ve[:], power[:], ALU.pow).then_inc(root, 1)

            rstd_of(0)
            pool.wait_ge(small_in, 48)

            def body(b, p):
                if not at(b, B - 1):
                    rstd_of(b + 1)
                pool.wait_ge(gridded, b + 1)
                nc.gpsimd.tensor_tensor(y[p][:], y[p][:], grid[p][:], ALU.add).then_inc(lifted, 1)
                rows = X[:, bass.ds(CT * b, CT), :]
                nc.gpsimd.tensor_tensor(rows, rows, bias_row[:].to_broadcast([P, CT, D]), ALU.add).then_inc(biased, 1)

            pair_bodies(pool, body)

        @block.scalar
        def _(act):
            act.sem_inc(placed, 2)

            def scale_rows(b, p):
                act.wait_ge(rated, b + 1)
                act.wait_ge(rounded, b + 1)
                for a in range(CT):
                    nc.scalar.activation(y[p][:, a:a + 1, :], X[:, bass.ds(CT * b + a, 1), :], ACT.Identity,
                                         scale=rate[p][:, a:a + 1], bias=offset[p][:, a:a + 1]).then_inc(scaled, 1)

            scale_rows(0, 0)

            def body(b, p):
                if not at(b, B - 1):
                    scale_rows(b + 1, 1 - p)
                for a in range(CT):
                    act.wait_ge(turned, 2 * b + a + 5)
                    if a == 0:
                        act.wait_ge(multiplied, 4 * b + 4)
                    nc.scalar.activation(x8T[p][:, a, :, :], turn_ps[a][:], ACT.Copy).then_inc(placed, 1)

            pair_bodies(act, body)

        @block.tensor
        def _(pe):
            pe.sem_inc(turned, 4)
            pe.sem_inc(multiplied, 8)

            def turn(b, p):
                pe.wait_ge(rounded, b + 3)
                for a in range(CT):
                    pe.wait_ge(placed, 2 * b + a + 1)
                    for k in range(KT):
                        ins = nc.tensor.transpose(turn_ps[a][:, k, :], x8[p][:, a, k * P:(k + 1) * P], identb[:])
                    ins.then_inc(turned, 1)

            def multiply(b, p):
                for a in range(CT):
                    pe.wait_ge(placed, 2 * b + a + 3)
                    for h in range(2):
                        o = 2 * a + h
                        pe.wait_ge(finished, 4 * b + o + 1)
                        for k in range(KT):
                            ins = nc.tensor.matmul(out_ps[o][:], x8T[p][:, a, k, :], w8[:, k, h * HW:(h + 1) * HW],
                                                   start=(k == 0), stop=(k == KT - 1))
                        ins.then_inc(multiplied, 1)

            turn(0, 0)

            def body(b, p):
                if not at(b, B - 1):
                    turn(b + 1, 1 - p)
                multiply(b, p)

            pair_bodies(pe, body)

        @block.vector
        def _(dve):
            dve.sem_inc(rounded, 2)
            dve.sem_inc(finished, 4)
            steps = Steps(dve, step)
            rows_variances(nc, dve, steps, held, X, 0, stats, mv, ve, var)
            dve.wait_ge(small_in, 48)
            nc.vector.tensor_tensor(scales[:, 3:4], scales[:, 0:1], scales[:, 1:2], ALU.mult)
            steps.done(nc.vector.reciprocal(scales[:, 2:3], scales[:, 0:1]))
            steps.wait()

            def rates(b, p):
                dve.wait_ge(root, b + 1)
                if not at(b, 0):
                    dve.wait_ge(scaled, 2 * b)
                steps.done(nc.vector.tensor_scalar(rate[p][:], rstd[:], scales[:, 2:3], None, ALU.mult))
                steps.wait()
                nc.vector.scalar_tensor_tensor(offset[p][:], mv[:, :, 0], -1.0, rate[p][:], ALU.mult, ALU.mult).then_inc(rated, 1)

            rates(0, 0)
            before = steps.n

            def finish(b, p):
                dve.wait_ge(backed, b + 1)
                dve.wait_ge(biased, b + 1)
                dve.wait_ge(stored[p], 8 * (b - p) + 16)
                for a in range(CT):
                    for h in range(2):
                        o = 2 * a + h
                        cols = slice(h * HW, (h + 1) * HW)
                        dve.wait_ge(multiplied, 4 * b + o + 9)
                        nc.vector.scalar_tensor_tensor(made[p][:, a:a + 1, cols], out_ps[o][:].unsqueeze(1), back[p][:, a:a + 1],
                                                       X[:, bass.ds(CT * b + a, 1), cols], ALU.mult, ALU.add).then_inc(finished, 1)

            def body(b, p):
                nonlocal steps
                steps = Steps(dve, step, before + 6 * b)
                dve.wait_ge(scaled, 2 * b + 2)
                steps.done(nc.vector.tensor_scalar(grid[p][:].bitcast(I32), y[p][:].bitcast(I32), EXPONENT, None, ALU.bitwise_and))
                steps.wait()
                nc.vector.tensor_scalar(grid[p][:], grid[p][:], FP8_LEAST, TO_GRID, ALU.max, ALU.mult).then_inc(gridded, 1)
                if not at(b, B - 1):
                    rows_variances(nc, dve, steps, held, X, b + 1, stats, mv, ve, var)
                dve.wait_ge(lifted, b + 1)
                dve.wait_ge(turned, 2 * b + 2)
                nc.vector.tensor_tensor(x8[p][:], y[p][:], grid[p][:], ALU.subtract).then_inc(rounded, 1)
                if not at(b, B - 1):
                    rates(b + 1, 1 - p)
                dve.wait_ge(rounded, b + 3)
                steps.done(nc.vector.tensor_reduce(most[:], x8[p][:], AX.X, ALU.max, apply_absolute_value=True))
                steps.wait()
                steps.done(nc.vector.tensor_scalar(flag[:], most[:], OVERFLOW, 0.0, ALU.mult, ALU.mult))
                steps.wait()
                nc.vector.tensor_scalar(back[p][:], flag[:], scales[:, 3:4], None, ALU.add).then_inc(backed, 1)
                if not at(b, 0):
                    finish(b - 1, 1 - p)

            body(0, 0)
            with dve.Fori(0, B // 2 - 1) as i:
                body(2 * i + 1, 1)
                body(2 * i + 2, 0)
            body(B - 1, 1)
            finish(B - 1, 1)


def program(nc, x, ctx, gate_codes, gate_scales, up_codes, up_scales, down_codes, down_scales, conv_w, gamma, beta,
            weight, bias, in_scale, w_scale, out):
    ctx_t = nc.dram_tensor("ctx_t", [B, KT, P, C], F32, kind="Internal").ap()
    mask_t = nc.dram_tensor("mask_t", [TILES, P, C], BF16, kind="Internal").ap()
    with ExitStack() as st:
        X = st.enter_context(nc.sbuf_tensor("x_rows", [P, NT, D], F32))
        ident = st.enter_context(nc.sbuf_tensor("ident", [P, P], F32))
        identb = st.enter_context(nc.sbuf_tensor("identb", [P, P], BF16))
        with ExitStack() as ffn:
            xT = [ffn.enter_context(nc.sbuf_tensor(f"xT_{n}", [P, KT, NT * P], BF16)) for n in ("high", "low")]
            attention(nc, x, ctx, ctx_t, X, xT, ident, identb)
            gated_ffn(nc, (gate_codes, up_codes, down_codes), (gate_scales, up_scales, down_scales), ctx_t, mask_t, X, xT, identb)
        w8 = st.enter_context(nc.sbuf_tensor("w8", [P, KT, D], BF16))
        with ExitStack() as channels:
            xlT = channels.enter_context(nc.sbuf_tensor("xlT", [P, TILES, C], F32))
            gates = channels.enter_context(nc.sbuf_tensor("gates", [P, 2, TILES], F32))
            pooled(nc, mask_t, conv_w, gamma, beta, weight, w_scale, X, xlT, gates, w8, ident)
            apply_gates(nc, mask_t, X, xlT, gates, ident)
        fp8_ffn(nc, bias, in_scale, w_scale, out, X, w8, identb)


_INS = ["x", "ctx_4096", "L0_ffn_gate_codes", "L0_ffn_gate_scales", "L0_ffn_up_codes", "L0_ffn_up_scales",
        "L0_ffn_down_codes", "L0_ffn_down_scales", "L1_xattn_conv_w", "L1_xattn_bn_gamma", "L1_xattn_bn_beta",
        "L1_ffn_weight", "L1_ffn_bias", "L1_ffn_input_scale", "L1_ffn_weight_scale"]
_OUTS = [((B, C, D), "float32")]


def kernel(**inputs):
    import numpy as _np
    import concourse.bacc as _bacc
    from concourse import mybir as _mybir
    from concourse.bass_utils import run_bass_kernel_spmd as _run

    nc = _bacc.Bacc("TRN2", target_bir_lowering=False, num_devices=1)
    arrays, args = {}, []
    for name in _INS:
        a = _np.ascontiguousarray(inputs[name])
        arrays[f"in_{name}_dram"] = a
        args.append(nc.dram_tensor(f"in_{name}_dram", a.shape, _mybir.dt.from_np(a.dtype), kind="ExternalInput").ap())
    for i, (shape, dtype) in enumerate(_OUTS):
        dt = _mybir.dt.from_np(_np.dtype(dtype))
        args.append(nc.dram_tensor(f"out_{i}_dram", shape, dt, kind="ExternalOutput").ap())
    program(nc, *args)
    r = _run(nc, [arrays], core_ids=[0])
    got = tuple(r.results[0][f"out_{i}_dram"] for i in range(len(_OUTS)))
    return got[0]
```

```python
import math
from contextlib import ExitStack

import numpy as np

import concourse.bass as bass
import concourse.mybir as mybir

F32 = mybir.dt.float32
BF16 = mybir.dt.bfloat16
I32 = mybir.dt.int32
ALU = mybir.AluOpType
ACT = mybir.ActivationFunctionType
AX = mybir.AxisListType

P = 128
B, C, D = 8, 256, 1024
CT = C // P
NT = B * CT
KT = D // P
I = 2752
NB = -(-I // P)
LAST = I - (NB - 1) * P
SB = 64
HW = 512
EPS = 1e-5
TOPK = math.floor(0.6 * C) + math.floor(0.6 * C) % 2
REST = C - TOPK
ROUNDS = -(-REST // 8)
GONE = -3.0e38

LOW = [(-0.09372339397668839, 0.6533904075622559), (-0.11047609895467758, 0.7263457775115967),
       (-0.060643620789051056, 0.14096669852733612), (-0.2653747797012329, 0.132687509059906)]
HIGH = [(0.08134989440441132, -0.5712188482284546), (0.0918029323220253, -0.6719170212745667),
        (0.0301042553037405, -0.350259393453598), (0.15513597428798676, -2.1334710121154785)]


class Steps:

    def __init__(self, eng, sem, base=0):
        self.eng, self.sem, self.base, self.n = eng, sem, base, 0

    def done(self, ins):
        ins.then_inc(self.sem, 1)
        self.n += 1

    def wait(self, held=None):
        self.eng.wait_ge(self.sem, self.base + self.n)
        if held is not None:
            self.eng.sem_inc(held, 1)


def at(m, n):
    return isinstance(m, int) and m == n


def identity(nc, pool, made, sem, n):
    nc.gpsimd.memset(made, 0.0).then_inc(sem, 1)
    pool.wait_ge(sem, n + 1)
    nc.gpsimd.affine_select(out=made, in_=made, compare_op=ALU.not_equal, fill=1.0, base=0,
                            pattern=[[-1, P]], channel_multiplier=1).then_inc(sem, 1)


def attention(nc, x, ctx, ctx_t, X, xT, ident, identb):
    with ExitStack() as st:
        def sb(name, shape, dt=F32):
            return st.enter_context(nc.sbuf_tensor(name, shape, dt))

        def sem(name):
            return st.enter_context(nc.semaphore(name))

        cb = [sb(f"a_ctx{p}", [P, CT, D]) for p in range(2)]
        q = sb("a_q", [P, CT, D])
        xn = sb("a_xn", [P, CT, D])
        qT = sb("a_qT", [P, KT, C])
        kT = sb("a_kT", [P, KT, C])
        prob = sb("a_prob", [P, CT, C])
        stats = sb("a_stats", [P, 2, CT, 2, 6])
        mv = sb("a_mv", [P, 2, CT, 2])
        ve = sb("a_ve", [P, 2, CT])
        rstd = sb("a_rstd", [P, 2, CT])
        power = sb("a_power", [P, CT])
        low = sb("a_low", [P, CT])
        bias = sb("a_bias", [P, CT])
        total = sb("a_total", [P, CT])
        rtotal = sb("a_rtotal", [P, CT])
        turned = [st.enter_context(nc.psum_tensor(f"a_turn{i}", [P, HW], F32)) for i in range(4)]
        scores = st.enter_context(nc.psum_tensor("a_scores", [P, CT, C], F32))
        cont = [st.enter_context(nc.psum_tensor(f"a_cont{i}", [P, HW], F32)) for i in range(2)]

        const = sem("a_const")
        x_in = [sem(f"a_x_in{p}") for p in range(2)]
        c_in = [sem(f"a_c_in{p}") for p in range(2)]
        kt_out = sem("a_kt_out")
        var_q = sem("a_var_q")
        var_x = sem("a_var_x")
        rstd_q = sem("a_rstd_q")
        rstd_x = sem("a_rstd_x")
        q_made = sem("a_q_made")
        t1 = sem("a_t1")
        t2 = sem("a_t2")
        qt_made = sem("a_qt_made")
        kt_made = sem("a_kt_made")
        scored = sem("a_scored")
        bias_made = sem("a_bias_made")
        exped = sem("a_exped")
        prob_made = sem("a_prob_made")
        cont_made = sem("a_cont_made")
        added = sem("a_added")
        xn_made = sem("a_xn_made")
        hi_made = sem("a_hi_made")
        lo_made = sem("a_lo_made")
        step = sem("a_step")
        held = sem("a_held")
        block = st.enter_context(nc.Block())

        x_rows = x.rearrange("b (a p) d -> b p a d", p=P)
        c_rows = ctx.rearrange("b (a p) d -> b p a d", p=P)
        ctx_tiles = ctx_t.rearrange("b k p c -> b p k c")

        def bodies(eng, body):
            body(0, 0, True, False)
            with eng.Fori(0, B // 2 - 1) as i:
                body(2 * i + 1, 1, True, True)
                body(2 * i + 2, 0, True, True)
            body(B - 1, 1, True, True)
            body(B, 0, False, True)

        @block.sync
        def _(sp):
            def load_x(n, p):
                sp.dma_start(X[:, bass.ds(CT * n, CT), :], x_rows[bass.ds(n, 1)].rearrange("o p a d -> (o p) a d")).then_inc(x_in[p], 16)

            def load_c(n, p):
                sp.dma_start(cb[p][:], c_rows[bass.ds(n, 1)].rearrange("o p a d -> (o p) a d")).then_inc(c_in[p], 16)

            def body(m, p, first, second):
                if first:
                    sp.wait_ge(kt_made, 4 * m + 4)
                    sp.dma_start(ctx_tiles[bass.ds(m, 1)].rearrange("o p k c -> (o p) k c"), kT[:]).then_inc(kt_out, 16)
                if first and second and not at(m, B - 1):
                    sp.wait_ge(cont_made, 4 * m)
                    load_c(m + 1, 1 - p)

            load_x(0, 0)
            load_c(0, 0)
            load_x(1, 1)
            load_c(1, 1)
            with sp.Fori(0, B // 2 - 1) as i:
                for p in range(2):
                    sp.wait_ge(x_in[p], 16 * i + 16)
                    load_x(2 * i + p + 2, p)
            bodies(sp, body)
            sp.wait_ge(kt_out, 16 * B)

        @block.gpsimd
        def _(pool):
            nc.gpsimd.memset(power[:], -0.5).then_inc(const, 1)
            identity(nc, pool, ident[:], const, 1)
            pool.wait_ge(const, 3)
            nc.gpsimd.tensor_copy(identb[:], ident[:]).then_inc(const, 1)
            pool.wait_ge(const, 4)

            def root(made, var, n):
                pool.wait_ge(var, n + 1)
                k = 0 if var is var_q else 1
                nc.gpsimd.tensor_tensor(rstd[:, k, :], ve[:, k, :], power[:], ALU.pow).then_inc(made, 1)

            def body(m, p, first, second):
                if second:
                    root(rstd_x, var_x, m - 1)
                if first and not at(m, B - 1):
                    root(rstd_q, var_q, m + 1)

            root(rstd_q, var_q, 0)
            bodies(pool, body)

        @block.scalar
        def _(act):
            def body(m, p, first, second):
                if first:
                    for f in range(4):
                        act.wait_ge(t1, 8 * m + 5 + f)
                        if f == 0 and not at(m, 0):
                            act.wait_ge(kt_out, 16 * m)
                        nc.scalar.activation(kT[:, 2 * f:2 * f + 2, :], turned[f][:].rearrange("p (k c) -> p k c", k=2),
                                             ACT.Copy, scale=-1.0).then_inc(kt_made, 1)
                    act.wait_ge(bias_made, m + 1)
                    for h in range(CT):
                        nc.scalar.activation(prob[:, h, :], scores[:, h, :], ACT.Exp, bias=bias[:, h:h + 1],
                                             scale=-1.0 / math.sqrt(C), accum_out=total[:, h:h + 1]).then_inc(exped, 1)
                if second:
                    for f in range(4):
                        a, kk = f // 2, f % 2
                        act.wait_ge(t2, 4 * m + f + 1)
                        nc.scalar.activation(xT[0][:, 4 * kk:4 * kk + 4, bass.ds((m - 1) * C + a * P, P)],
                                             turned[f][:].rearrange("p (k t) -> p k t", k=4),
                                             ACT.Copy).then_inc(hi_made, 1)

            bodies(act, body)

        @block.tensor
        def _(pe):
            pe.wait_ge(const, 4)

            def body(m, p, first, second):
                zero = at(m, 0)
                if first:
                    for f in range(8):
                        src = q if f < 4 else cb[p]
                        if f == 0:
                            pe.wait_ge(q_made, m + 1)
                        if f == 4:
                            pe.wait_ge(c_in[p], 8 * (m - p) + 16)
                        if f < 4 and not zero:
                            pe.wait_ge(lo_made, 4 * (m - 1) + f + 1)
                        if f >= 4:
                            pe.wait_ge(qt_made, 4 * m + f - 3)
                        for j in range(4):
                            k, a = 2 * (f % 4) + j // 2, j % 2
                            ins = nc.tensor.transpose(turned[f % 4][:, j * P:(j + 1) * P],
                                                      src[:, a, k * P:(k + 1) * P], ident[:])
                        ins.then_inc(t1, 1)
                if second:
                    pe.wait_ge(prob_made, m)
                    for o in range(4):
                        a, h = o // 2, o % 2
                        pe.wait_ge(added, 4 * (m - 1) + o + 1)
                        for d in range(CT):
                            ins = nc.tensor.matmul(cont[o % 2][:], prob[:, d, a * P:(a + 1) * P],
                                                   cb[1 - p][:, d, h * HW:(h + 1) * HW], start=(d == 0), stop=(d == CT - 1))
                        ins.then_inc(cont_made, 1)
                if first:
                    pe.wait_ge(kt_made, 4 * m + 4)
                    pe.wait_ge(qt_made, 4 * m + 4)
                    if not zero:
                        pe.wait_ge(exped, 2 * m)
                    for h in range(CT):
                        for k in range(KT):
                            ins = nc.tensor.matmul(scores[:, h, :], qT[:, k, h * P:(h + 1) * P], kT[:, k, :],
                                                   start=(k == 0), stop=(k == KT - 1))
                    ins.then_inc(scored, 1)
                if second:
                    pe.wait_ge(xn_made, m)
                    for f in range(4):
                        a, kk = f // 2, f % 2
                        if first:
                            pe.wait_ge(kt_made, 4 * m + f + 1)
                        else:
                            pe.wait_ge(lo_made, 4 * (m - 1) + f + 1)
                        for j in range(4):
                            k = 4 * kk + j
                            ins = nc.tensor.transpose(turned[f][:, j * P:(j + 1) * P], xn[:, a, k * P:(k + 1) * P], ident[:])
                        ins.then_inc(t2, 1)

            bodies(pe, body)

        @block.vector
        def _(dve):
            def variances(n, k, var):
                for a in range(CT):
                    for h in range(2):
                        ins = nc.vector.bn_stats(stats[:, k, a, h, :], X[:, bass.ds(CT * n + a, 1), h * HW:(h + 1) * HW])
                steps.done(ins)
                steps.wait(held)
                for a in range(CT):
                    ins = nc.vector.bn_aggr(mv[:, k, a, :], stats[:, k, a, :, :])
                steps.done(ins)
                steps.wait()
                nc.vector.tensor_scalar(ve[:, k, :], mv[:, k, :, 1], EPS, None, ALU.add).then_inc(var, 1)

            def normed(dst, n, k, made):
                for a in range(CT):
                    ins = nc.vector.tensor_scalar(dst[:, a:a + 1, :], X[:, bass.ds(CT * n + a, 1), :], mv[:, k, a, 0:1],
                                                  rstd[:, k, a:a + 1], ALU.subtract, ALU.mult)
                ins.then_inc(made, 1)

            def body(m, p, first, second):
                nonlocal steps
                steps = Steps(dve, step, 2 if at(m, 0) else 6 * m - 2 if at(m, B) else 6 * m)
                more = first and not at(m, B - 1)
                if first:
                    for f in range(4):
                        dve.wait_ge(t1, 8 * m + f + 1)
                        nc.vector.tensor_copy(qT[:, 2 * f:2 * f + 2, :],
                                              turned[f][:].rearrange("p (k c) -> p k c", k=2)).then_inc(qt_made, 1)
                if more:
                    dve.wait_ge(x_in[1 - p], 8 * (m + p) + 16)
                    dve.sem_inc(held, 1)
                    variances(m + 1, 0, var_q)
                if second:
                    for o in range(4):
                        a, h = o // 2, o % 2
                        dve.wait_ge(cont_made, 4 * (m - 1) + o + 1)
                        piece = X[:, bass.ds(CT * (m - 1) + a, 1), h * HW:(h + 1) * HW]
                        nc.vector.tensor_tensor(piece, piece, cont[o % 2][:].unsqueeze(1), ALU.add).then_inc(added, 1)
                    dve.wait_ge(added, 4 * m + 2)
                    dve.sem_inc(held, 1)
                    variances(m - 1, 1, var_x)
                if more:
                    dve.wait_ge(rstd_q, m + 2)
                    normed(q, m + 1, 0, q_made)
                if second:
                    dve.wait_ge(rstd_x, m)
                    dve.wait_ge(t2, 4 * m)
                    normed(xn, m - 1, 1, xn_made)
                if first:
                    dve.wait_ge(scored, m + 1)
                    steps.done(nc.vector.tensor_reduce(low[:], scores[:], AX.X, ALU.min))
                    steps.wait()
                    nc.vector.tensor_scalar(bias[:], low[:], 1.0 / math.sqrt(C), None, ALU.mult).then_inc(bias_made, 1)
                    dve.wait_ge(exped, 2 * m + 2)
                    steps.done(nc.vector.reciprocal(rtotal[:], total[:]))
                    steps.wait()
                    for h in range(CT):
                        ins = nc.vector.tensor_scalar(prob[:, h, :], prob[:, h, :], rtotal[:, h:h + 1], None, ALU.mult)
                    ins.then_inc(prob_made, 1)
                if second:
                    for f in range(4):
                        a, kk = f // 2, f % 2
                        cols = bass.ds((m - 1) * C + a * P, P)
                        dve.wait_ge(hi_made, 4 * (m - 1) + f + 1)
                        nc.vector.tensor_tensor(xT[1][:, 4 * kk:4 * kk + 4, cols],
                                                turned[f][:].rearrange("p (k t) -> p k t", k=4),
                                                xT[0][:, 4 * kk:4 * kk + 4, cols], ALU.subtract).then_inc(lo_made, 1)

            steps = Steps(dve, step)
            dve.sem_inc(lo_made, 4)
            dve.sem_inc(added, 2)
            dve.sem_inc(t2, 4)
            dve.wait_ge(x_in[0], 16)
            variances(0, 0, var_q)
            dve.wait_ge(rstd_q, 1)
            normed(q, 0, 0, q_made)
            bodies(dve, body)


CHUNK = 2
CHUNKS = NB // CHUNK
UNITS = 6 * CHUNK
EARLY = 5
GROUPS = NT * P // HW
PASSES = ((0, 0), (0, 1), (1, 0))
TILES = B * KT
TILE_CHUNK = 6
LANE_ROUNDS = TILE_CHUNK // 2 * ROUNDS
AHEAD = ROUNDS // 2
GROUP_ROUNDS = 4


def unit(c, j):
    if j >= UNITS:
        c, j = c + 1, j - UNITS
    if isinstance(c, int) and UNITS * c + j >= UNITS * CHUNKS - EARLY:
        return None
    if j < 3:
        which, half, n, buf = (j + 1) // 2, (j + 1) % 2, CHUNK * c + 1, 1
    elif j < 7:
        which, half, n, buf = 2, (j - 3) % 2, CHUNK * c + (j - 3) // 2, (j - 3) // 2
    elif j < 11:
        which, half, n, buf = (j - 7) // 2, (j - 7) % 2, CHUNK * c + 2, 0
    else:
        which, half, n, buf = 0, 0, CHUNK * c + 3, 1
    return which, n, half, LAST if at(n, NB - 1) else P, buf


def number(c, j):
    return EARLY + UNITS * c + j


def code_slot(j):
    return (j + EARLY) % 3


def gated_ffn(nc, codes_in, scales_in, ctx_t, mask_t, X, xT, identb):
    with ExitStack() as st:
        def sb(name, shape, dt=F32):
            return st.enter_context(nc.sbuf_tensor(name, shape, dt))

        def ps(name, shape, dt=F32):
            return st.enter_context(nc.psum_tensor(name, shape, dt))

        def sem(name):
            return st.enter_context(nc.semaphore(name))

        code = [sb(f"b_code{i}", [P, HW], BF16) for i in range(3)]
        low_line = [sb(f"b_low_line{i}", [P, HW]) for i in range(4)]
        high_line = [sb(f"b_high_line{i}", [P, HW]) for i in range(4)]
        weight = [sb(f"b_weight{i}", [P, HW]) for i in range(2)]
        parts = [sb(f"b_parts{i}", [P, 2, HW], BF16) for i in range(2)]
        gu_w = [sb(f"b_gate_up{i}", [P, 2, 2, KT, P], BF16) for i in range(2)]
        dn_w = [sb(f"b_down{i}", [P, 2, D], BF16) for i in range(2)]
        inner = [[sb(f"b_inner{b}_{n}", [P, NT * P], BF16) for n in ("high", "low")] for b in range(CHUNK)]
        act_in = [sb(f"b_gated{i}", [P, HW]) for i in range(2)]
        gu_scale = [sb(f"b_scale{i}", [P, NB, D // SB]) for i in range(2)]
        dn_scale = sb("b_scale2", [P, KT, I // SB])
        left = [sb(f"b_left{i}", [P, C]) for i in range(3)]
        best = [sb(f"b_best{i}", [P, 8]) for i in range(2)]
        line_bias = sb("b_line_bias", [P, 2, len(LOW)])
        mask = sb("b_mask", [P, C], BF16)
        gate_ps = [ps(f"b_gate_ps{i}", [P, HW]) for i in range(2)]
        up_ps = [ps(f"b_up_ps{i}", [P, HW]) for i in range(2)]
        turn_ps = [ps(f"b_turn_ps{i}", [P, 2, HW], BF16) for i in range(2)]
        down_ps = [ps(f"b_down_ps{i}", [P, HW]) for i in range(2)] + [gate_ps[1], up_ps[1]]

        scale_in = sem("b_scale_in")
        bias_made = sem("b_bias_made")
        code_in = [sem(f"b_code_in{i}") for i in range(3)]
        lined = sem("b_lined")
        paired = sem("b_paired")
        joined = sem("b_joined")
        decoded = sem("b_decoded")
        scaled = sem("b_scaled")
        high_made = sem("b_high_made")
        low_made = sem("b_low_made")
        turned = sem("b_turned")
        placed = sem("b_placed")
        gu_made = sem("b_gu_made")
        silu_made = sem("b_silu_made")
        gated = sem("b_gated")
        inner_high = sem("b_inner_high")
        inner_low = sem("b_inner_low")
        down_made = sem("b_down_made")
        added = sem("b_added")
        left_in = [sem(f"b_left_in{i}") for i in range(3)]
        found = sem("b_found")
        held, pool_held, sp_held = (sem(f"b_held_{e}") for e in ("dve", "pool", "sp"))
        mask_made = sem("b_mask_made")
        mask_out = sem("b_mask_out")
        block = st.enter_context(nc.Block())

        def size(un):
            which, _, _, r, _ = un
            return (r, HW) if which < 2 else (P, HW * r // P)

        def chunks(eng, chunk):
            with eng.Fori(0, CHUNKS - 2) as c:
                chunk(c)
            chunk(CHUNKS - 2)
            chunk(CHUNKS - 1)

        @block.sync
        def _(sp):
            sp.sem_inc(mask_out, 16)
            tiles = ctx_t.rearrange("b k p c -> (b k) p c")

            def load(t, i):
                sp.dma_start(left[i][:], tiles[bass.ds(t, 1)].rearrange("o p c -> (o p) c")).then_inc(left_in[i], 16)

            for which in range(2):
                sp.dma_start(gu_scale[which][:, 0:NB - 1, :],
                             scales_in[which][0:(NB - 1) * P, :].rearrange("(n p) s -> p n s", p=P)).then_inc(scale_in, 16)
                sp.dma_start(gu_scale[which][0:LAST, NB - 1, :], scales_in[which][(NB - 1) * P:I, :]).then_inc(scale_in, 16)
            sp.dma_start(dn_scale[:], scales_in[2].rearrange("(t p) s -> p t s", p=P)).then_inc(scale_in, 16)
            for t in range(3):
                load(t, t)

            def chunk(c):
                for k in range(TILE_CHUNK):
                    t = TILE_CHUNK * c + k
                    if isinstance(t, int) and t >= TILES:
                        return
                    sp.wait_ge(mask_made, t + 1)
                    sp.sem_inc(sp_held, 1)
                    sp.dma_start(mask_t[bass.ds(t, 1)].rearrange("o p c -> (o p) c"), mask[:]).then_inc(mask_out, 16)
                    if not (isinstance(t, int) and t + 3 >= TILES):
                        load(t + 3, k % 3)

            chunks(sp, chunk)
            sp.wait_ge(mask_out, 16 * (TILES + 1))

        @block.gpsimd
        def _(pool):
            pool.sem_inc(low_made, 2)
            pool.sem_inc(inner_low, 2)

            def load(c, j):
                un = unit(c, j)
                if un is None:
                    return
                which, n, half, r, _ = un
                slot = code_slot(j)
                if which < 2:
                    src = codes_in[which][bass.ds(n * P, r), half * HW:(half + 1) * HW]
                    dst = code[slot][0:r, :]
                else:
                    src = codes_in[2][half * HW:(half + 1) * HW, bass.ds(n * P, r)].rearrange("(t p) i -> p t i", p=P)
                    dst = code[slot][:, 0:4 * r].rearrange("p (t i) -> p t i", t=4)
                pool.dma_start(dst, src).then_inc(code_in[slot], 16)

            def low(c, j):
                a, n = size(unit(c, j))
                u = number(c, j)
                pool.wait_ge(high_made, u + 1)
                nc.gpsimd.tensor_tensor(parts[j % 2][0:a, 1, 0:n], weight[j % 2][0:a, 0:n], parts[j % 2][0:a, 0, 0:n],
                                        ALU.subtract).then_inc(low_made, 1)

            def pair(c, j, i):
                a, n = size(unit(c, j))
                side = (low_line, high_line)[i]
                pool.wait_ge(lined, 4 * number(c, j) + i + 1)
                nc.gpsimd.tensor_tensor(side[2][0:a, 0:n], side[2][0:a, 0:n], side[3][0:a, 0:n], ALU.add).then_inc(paired, 1)

            def difference(c, j):
                a, n = size(unit(c, j))
                u = number(c, j)
                pool.wait_ge(paired, 3 * u + 2)
                nc.gpsimd.tensor_tensor(high_line[2][0:a, 0:n], high_line[2][0:a, 0:n], low_line[2][0:a, 0:n],
                                        ALU.subtract).then_inc(paired, 1)
                if unit(c, j + 3) is not None:
                    pool.wait_ge(lined, 4 * u + 4)
                    pool.sem_inc(pool_held, 1)
                    load(c, j + 3)

            def step(c, j):
                more = unit(c, j + 1) is not None
                if more:
                    pair(c, j + 1, 0)
                if unit(c, j) is not None:
                    low(c, j)
                if more:
                    pair(c, j + 1, 1)
                    difference(c, j + 1)

            for j in range(UNITS - EARLY, UNITS - EARLY + 3):
                load(-1, j)
            for i in range(2):
                pair(-1, UNITS - EARLY, i)
            difference(-1, UNITS - EARLY)
            for j in range(UNITS - EARLY, UNITS):
                step(-1, j)

            def chunk(c):
                for s in range(UNITS):
                    step(c, s)
                    if s < CHUNK * GROUPS:
                        b, tg = s // GROUPS, s % GROUPS
                        r = LAST if at(CHUNK * c + b, NB - 1) else P
                        cols = slice(tg * HW, (tg + 1) * HW)
                        pool.wait_ge(inner_high, CHUNK * GROUPS * c + s + 1)
                        nc.gpsimd.tensor_tensor(inner[b][1][0:r, cols], act_in[tg % 2][0:r, :], inner[b][0][0:r, cols],
                                                ALU.subtract).then_inc(inner_low, 1)

            chunks(pool, chunk)

        @block.scalar
        def _(act):
            act.sem_inc(placed, 2)

            def lines(c, j, first):
                un = unit(c, j)
                if un is None:
                    return
                a, n = size(un)
                u = number(c, j)
                slot = code_slot(j)
                if first == 2:
                    act.wait_ge(code_in[slot], 16 * (4 * c + (j + EARLY) // 3 + 1))
                for side in range(2):
                    if first == 2 and not at(u, 0):
                        act.wait_ge((paired, decoded)[side], (3, 1)[side] * u)
                    for i in (first, first + 1):
                        ins = nc.scalar.activation((low_line, high_line)[side][i][0:a, 0:n], code[slot][0:a, 0:n], ACT.Relu,
                                                   bias=line_bias[0:a, side, i:i + 1], scale=(LOW, HIGH)[side][i][0])
                    ins.then_inc(lined, 1)

            def high(c, j):
                a, n = size(unit(c, j))
                u = number(c, j)
                act.wait_ge(scaled, u + 1)
                act.wait_ge(turned, u + 1)
                nc.scalar.activation(parts[j % 2][0:a, 0, 0:n], weight[j % 2][0:a, 0:n], ACT.Copy).then_inc(high_made, 1)

            def place(c, j):
                which, n, half, r, buf = unit(c, j)
                u = number(c, j)
                act.wait_ge(turned, u + 3)
                if which < 2:
                    dst = gu_w[buf][:, which, :, 4 * half:4 * half + 4, 0:r]
                    src = turn_ps[j % 2][:, :, 0:4 * r].rearrange("p h (k i) -> p h k i", k=4)
                else:
                    dst = dn_w[buf][0:r, :, half * HW:(half + 1) * HW]
                    src = turn_ps[j % 2][0:r, :, :]
                nc.scalar.activation(dst, src, ACT.Copy).then_inc(placed, 1)

            def step(c, j):
                lines(c, j + 1, 2)
                if unit(c, j) is not None:
                    high(c, j)
                lines(c, j + 1, 0)

            act.wait_ge(bias_made, 1)
            for first in (2, 0):
                lines(-1, UNITS - EARLY, first)
            for j in range(UNITS - EARLY, UNITS):
                step(-1, j)
                place(-1, j)

            def chunk(c):
                for s in range(UNITS):
                    step(c, s)
                    if s < CHUNK * GROUPS:
                        b, tg = s // GROUPS, s % GROUPS
                        r = LAST if at(CHUNK * c + b, NB - 1) else P
                        g = CHUNK * GROUPS * c + s
                        act.wait_ge(gu_made, g + 1)
                        act.wait_ge(inner_low, g + 1)
                        nc.scalar.activation(act_in[tg % 2][0:r, :], gate_ps[tg % 2][0:r, :], ACT.Silu).then_inc(silu_made, 1)
                        act.wait_ge(gated, g + 3)
                        nc.scalar.activation(inner[b][0][0:r, tg * HW:(tg + 1) * HW], act_in[tg % 2][0:r, :],
                                             ACT.Copy).then_inc(inner_high, 1)
                    if unit(c, s) is not None:
                        place(c, s)

            chunks(act, chunk)

        @block.tensor
        def _(pe):
            pe.sem_inc(turned, 2)

            def turn(c, j):
                which, n, half, r, buf = unit(c, j)
                u = number(c, j)
                pe.wait_ge(low_made, u + 3)
                pe.wait_ge(placed, u + 1)
                for h in range(2):
                    for k in range(4):
                        if which < 2:
                            ins = nc.tensor.transpose(turn_ps[j % 2][:, h, k * r:(k + 1) * r],
                                                      parts[j % 2][0:r, h, k * P:(k + 1) * P], identb[0:r, 0:r])
                        else:
                            ins = nc.tensor.transpose(turn_ps[j % 2][0:r, h, k * P:(k + 1) * P],
                                                      parts[j % 2][:, h, k * r:(k + 1) * r], identb[:])
                ins.then_inc(turned, 1)

            for j in range(UNITS - EARLY, UNITS):
                turn(-1, j)

            def chunk(c):
                for b in range(CHUNK):
                    r = LAST if at(CHUNK * c + b, NB - 1) else P
                    pe.wait_ge(placed, number(c, b * GROUPS - 1) + 2)
                    for tg in range(GROUPS):
                        g = 2 * GROUPS * c + GROUPS * b + tg
                        pe.wait_ge(gated, g + 1)
                        if b == 0 and tg == 1:
                            pe.wait_ge(added, 2 * NT * c + 4)
                        for which in range(2):
                            out = (gate_ps, up_ps)[which][tg % 2][0:r, :]
                            for k in range(KT):
                                for n, (wp, xp) in enumerate(PASSES):
                                    ins = nc.tensor.matmul(out, gu_w[b][:, which, wp, k, 0:r], xT[xp][:, k, tg * HW:(tg + 1) * HW],
                                                           start=(k == 0 and n == 0), stop=(k == KT - 1 and n == 2))
                        ins.then_inc(gu_made, 1)
                        if unit(c, GROUPS * b + tg) is not None:
                            turn(c, GROUPS * b + tg)
                pe.wait_ge(placed, number(c, 7) + 2)
                for t in range(NT):
                    if t % 4 == 0:
                        pe.wait_ge(inner_low, 2 * GROUPS * c + GROUPS + t // 4 + 3)
                    for h in range(2):
                        o = 2 * t + h
                        if o == 2:
                            pe.wait_ge(gated, 2 * GROUPS * (c + 1) + 2)
                        pe.wait_ge(added, 2 * NT * c + o + 1)
                        for b in range(CHUNK):
                            r = LAST if at(CHUNK * c + b, NB - 1) else P
                            for n, (wp, xp) in enumerate(PASSES):
                                ins = nc.tensor.matmul(down_ps[o % 4][:], inner[b][xp][0:r, t * P:(t + 1) * P],
                                                       dn_w[b][0:r, wp, h * HW:(h + 1) * HW],
                                                       start=(b == 0 and n == 0), stop=(b == CHUNK - 1 and n == 2))
                        ins.then_inc(down_made, 1)
                    s = CHUNK * GROUPS + t // 4
                    if t % 4 == 3 and unit(c, s) is not None:
                        turn(c, s)

            chunks(pe, chunk)

        @block.vector
        def _(dve):
            def join(c, j, part):
                un = unit(c, j)
                if un is None:
                    return
                which, n, half, r, _ = un
                a, m = size(un)
                u = number(c, j)
                lo, hi = ([x[0:a, 0:m] for x in side] for side in (low_line, high_line))
                w = weight[j % 2][0:a, 0:m]
                if part == 0:
                    dve.wait_ge(lined, 4 * u + 3)
                    dve.wait_ge(low_made, u + 1)
                    nc.vector.tensor_tensor(w, lo[0], lo[1], ALU.max)
                    dve.wait_ge(lined, 4 * u + 4)
                    nc.vector.tensor_tensor(hi[0], hi[0], hi[1], ALU.max).then_inc(joined, 1)
                elif part == 1:
                    dve.wait_ge(joined, 2 * u + 1)
                    nc.vector.tensor_tensor(w, hi[0], w, ALU.subtract).then_inc(joined, 1)
                elif part == 2:
                    dve.wait_ge(joined, 2 * u + 2)
                    dve.wait_ge(paired, 3 * u + 3)
                    nc.vector.tensor_tensor(w, w, hi[2], ALU.add).then_inc(decoded, 1)
                else:
                    if which < 2:
                        scale = gu_scale[which][0:r, bass.ds(n, 1), 8 * half:8 * half + 8].rearrange("p o s -> p (o s)")
                        scale = scale.unsqueeze(2).to_broadcast([r, HW // SB, SB])
                        w = w.rearrange("p (s i) -> p s i", i=SB)
                    else:
                        scale = dn_scale[:, 4 * half:4 * half + 4, bass.ds(n * (P // SB), r // SB)]
                        scale = scale.unsqueeze(3).to_broadcast([P, 4, r // SB, SB])
                        w = w.rearrange("p (t s i) -> p t s i", t=4, i=SB)
                    dve.wait_ge(decoded, u + 1)
                    nc.vector.tensor_tensor(w, w, scale, ALU.mult).then_inc(scaled, 1)

            steps, last = None, [0, 0]

            def turn_of(c, lane, n):
                if lane == 0:
                    k, n = 2 * (n // ROUNDS) + 1, n % ROUNDS
                else:
                    n += AHEAD
                    k, n = 2 * (n // ROUNDS), n % ROUNDS
                t = TILE_CHUNK * c + k
                return None if isinstance(t, int) and t >= TILES else (k, n)

            def find(c, n, lanes=(0, 1)):
                for lane in lanes:
                    turn = turn_of(c, lane, n)
                    if turn is None:
                        continue
                    k, m = turn
                    if m == 0:
                        dve.wait_ge(left_in[k % 3], 16 * (2 * c + k // 3 + 1))
                        dve.sem_inc(held, 1)
                    elif last[lane]:
                        dve.wait_ge(found, last[lane])
                    steps.done(nc.vector.max(best[lane][:], left[k % 3][:, ::-1]))
                    last[lane] = steps.n

            def mark(c, n, lanes=(0, 1)):
                for lane in lanes:
                    turn = turn_of(c, lane, n)
                    if turn is None:
                        continue
                    k, m = turn
                    dve.wait_ge(found, last[lane])
                    if m == ROUNDS - 1 and REST % 8:
                        steps.done(nc.vector.memset(best[lane][:, REST % 8:8], GONE))
                        steps.wait()
                    row = left[k % 3][:, ::-1]
                    steps.done(nc.vector.match_replace(row, best[lane][:], row, GONE))
                    last[lane] = steps.n
                    if m == ROUNDS - 1:
                        steps.wait()
                        dve.wait_ge(mask_out, 16 * (TILE_CHUNK * c + k + 1))
                        nc.vector.tensor_scalar(mask[:], left[k % 3][:], GONE, None, ALU.is_gt).then_inc(mask_made, 1)

            def clear():
                steps.wait()
                dve.sem_clear(found)
                last[:] = 0, 0

            dve.sem_inc(gated, 2)
            dve.sem_inc(added, 4)
            for side, table in enumerate((LOW, HIGH)):
                for i, (_, bias) in enumerate(table):
                    ins = nc.vector.memset(line_bias[:, side, i:i + 1], bias)
            ins.then_inc(bias_made, 1)
            dve.wait_ge(scale_in, 16 * 5)
            steps = Steps(dve, found)
            for j in range(UNITS - EARLY, UNITS):
                for part in range(4):
                    join(-1, j, part)
            for n in range(-AHEAD, 0):
                find(0, n, (1,))
                mark(0, n, (1,))
            clear()

            def chunk(c):
                nonlocal steps
                steps = Steps(dve, found)
                n = 0
                for s in range(CHUNK * GROUPS):
                    join(c, s, 0)
                    find(c, n)
                    join(c, s, 1)
                    mark(c, n)
                    join(c, s, 2)
                    find(c, n + 1)
                    join(c, s, 3)
                    mark(c, n + 1)
                    for m in range(n + 2, n + GROUP_ROUNDS):
                        find(c, m)
                        mark(c, m)
                    n += GROUP_ROUNDS
                    b, tg = s // GROUPS, s % GROUPS
                    r = LAST if at(CHUNK * c + b, NB - 1) else P
                    g = CHUNK * GROUPS * c + s
                    dve.wait_ge(silu_made, g + 1)
                    nc.vector.tensor_tensor(act_in[tg % 2][0:r, :], act_in[tg % 2][0:r, :], up_ps[tg % 2][0:r, :],
                                            ALU.mult).then_inc(gated, 1)
                for o in range(2 * NT):
                    s, m = CHUNK * GROUPS + o // 8, o % 8
                    t, h = o // 2, o % 2
                    piece = X[:, t, h * HW:(h + 1) * HW]
                    dve.wait_ge(down_made, 2 * NT * c + o + 1)
                    nc.vector.tensor_tensor(piece, piece, down_ps[o % 4][:], ALU.add).then_inc(added, 1)
                    if m < 4:
                        join(c, s, m)
                    elif n < LANE_ROUNDS:
                        if m % 2 == 0:
                            find(c, n)
                        else:
                            mark(c, n)
                            n += 1
                clear()

            chunks(dve, chunk)


def rows_variances(nc, dve, steps, held, X, n, stats, mv, ve, var):
    for a in range(CT):
        for h in range(2):
            ins = nc.vector.bn_stats(stats[:, a, h, :], X[:, bass.ds(CT * n + a, 1), h * HW:(h + 1) * HW])
    steps.done(ins)
    steps.wait(held)
    for a in range(CT):
        ins = nc.vector.bn_aggr(mv[:, a, :], stats[:, a, :, :])
    steps.done(ins)
    steps.wait()
    nc.vector.tensor_scalar(ve[:], mv[:, :, 1], EPS, None, ALU.add).then_inc(var, 1)


def pair_bodies(eng, body):
    with eng.Fori(0, B // 2 - 1) as i:
        body(2 * i, 0)
        body(2 * i + 1, 1)
    body(B - 2, 0)
    body(B - 1, 1)


EXPONENT = 0x7F800000
TO_GRID = 1.5 * 2.0 ** 20
FP8_LEAST = 2.0 ** -6
FP8_MOST = 448.0
OVERFLOW = 7.4e35


def pooled(nc, mask_t, conv, gamma, beta, weight, w_scale, X, xlT, gates, w8, ident):
    with ExitStack() as st:
        def sb(name, shape, dt=F32):
            return st.enter_context(nc.sbuf_tensor(name, shape, dt))

        def sem(name):
            return st.enter_context(nc.semaphore(name))

        mask = [sb(f"c_mask{p}", [P, KT, C], BF16) for p in range(2)]
        xn = [sb(f"c_xn{p}", [P, CT, D]) for p in range(2)]
        inside = sb("c_inside", [P, KT, C])
        outside = sb("c_outside", [P, KT, C])
        junk = sb("c_junk", [P, KT, C], BF16)
        stats = sb("c_stats", [P, CT, 2, 6])
        mv = sb("c_mv", [P, CT, 2])
        ve = sb("c_ve", [P, CT])
        rstd = sb("c_rstd", [P, CT])
        power = sb("c_power", [P, CT])
        feat = sb("c_feat", [P, 2, 2, TILES])
        sums = sb("c_sums", [P, 2, TILES])
        taps = sb("c_taps", [P, 2, 7])
        joint = sb("c_joint", [P, 3 * P + 6])
        band = sb("c_band", [P, 2, 3 * P])
        ones = sb("c_ones", [P, P])
        z = sb("c_z", [P, 2, TILES])
        zsq = sb("c_zsq", [P, 2, TILES])
        zsum = sb("c_zsum", [P, 2])
        mean = sb("c_mean", [P, 2])
        zvar = sb("c_zvar", [P, 2])
        zrstd = sb("c_zrstd", [P, 2])
        affine = sb("c_affine", [P, 2])
        gate = sb("c_gate", [P, 2, TILES])
        ws = sb("c_ws", [P, 2])
        wf = sb("c_wf", [P, D])
        wm = sb("c_wm", [P, D])
        turn_ps = [st.enter_context(nc.psum_tensor(f"c_turn{i}", [P, 2, C], F32)) for i in range(4)]
        z_ps = st.enter_context(nc.psum_tensor("c_z_ps", [P, 2, TILES], F32))
        sum_ps = st.enter_context(nc.psum_tensor("c_sum_ps", [P, 2, 2], F32))

        small_in = sem("c_small_in")
        mask_in = [sem(f"c_mask_in{p}") for p in range(2)]
        w_in = sem("c_w_in")
        const = sem("c_const")
        inverse = sem("c_inverse")
        var = sem("c_var")
        root = sem("c_root")
        normed = sem("c_normed")
        turned = sem("c_turned")
        placed = sem("c_placed")
        in_made = sem("c_in_made")
        out_made = sem("c_out_made")
        out_max = sem("c_out_max")
        in_sum = sem("c_in_sum")
        out_sum = sem("c_out_sum")
        w_scaled = sem("c_w_scaled")
        w_grid = sem("c_w_grid")
        w_added = sem("c_w_added")
        w_round = sem("c_w_round")
        w_done = sem("c_w_done")
        averaged = sem("c_averaged")
        convolved = sem("c_convolved")
        summed = sem("c_summed")
        totalled = sem("c_totalled")
        zvared = sem("c_zvared")
        zroot = sem("c_zroot")
        znormed = sem("c_znormed")
        gated = sem("c_gated")
        step = sem("c_step")
        held, act_held = (sem(f"c_held_{e}") for e in ("dve", "act"))
        block = st.enter_context(nc.Block())
        masks = mask_t.rearrange("(b k) p c -> b p k c", k=KT)
        w_rows = weight.rearrange("(k p) o -> k p o", p=P)

        @block.sync
        def _(sp):
            def load_mask(b, p):
                sp.dma_start(mask[p][:], masks[bass.ds(b, 1)].rearrange("o p k c -> (o p) k c")).then_inc(mask_in[p], 16)

            def load_w(k):
                sp.dma_start(wf[:], w_rows[bass.ds(k, 1)].rearrange("o p n -> (o p) n")).then_inc(w_in, 16)

            sp.dma_start(ws[:, 0:1], w_scale.partition_broadcast(P)).then_inc(small_in, 16)
            sp.dma_start(taps[:], conv.rearrange("o c t -> (o c) t").partition_broadcast(P)).then_inc(small_in, 16)
            sp.dma_start(affine[:, 0:1], gamma.partition_broadcast(P)).then_inc(small_in, 16)
            sp.dma_start(affine[:, 1:2], beta.partition_broadcast(P)).then_inc(small_in, 16)
            load_mask(0, 0)
            load_mask(1, 1)
            load_w(0)

            def body(b, p):
                sp.wait_ge(in_made, b)
                load_mask(b + 1, 1 - p)
                sp.wait_ge(w_done, b)
                load_w(b)

            with sp.Fori(0, B // 2 - 1) as i:
                body(2 * i + 1, 1)
                body(2 * i + 2, 0)
            sp.wait_ge(w_done, B - 1)
            load_w(B - 1)

        @block.gpsimd
        def _(pool):
            nc.gpsimd.memset(power[:], -0.5).then_inc(const, 1)
            nc.gpsimd.memset(ones[:], 1.0).then_inc(const, 1)

            def rstd_of(b):
                pool.wait_ge(var, b + 1)
                nc.gpsimd.tensor_tensor(rstd[:], ve[:], power[:], ALU.pow).then_inc(root, 1)

            pool.wait_ge(const, 2)
            rstd_of(0)
            nc.gpsimd.memset(joint[:], 0.0).then_inc(const, 1)
            pool.wait_ge(const, 3)
            nc.gpsimd.affine_select(out=joint[:], in_=joint[:], compare_op=ALU.not_equal, fill=1.0, base=P + 3,
                                    pattern=[[-1, 3 * P + 6]], channel_multiplier=1).then_inc(const, 1)

            def body(b, p):
                if not at(b, B - 1):
                    rstd_of(b + 1)
                pool.wait_ge(w_grid, b + 1)
                nc.gpsimd.tensor_tensor(wf[:], wf[:], wm[:], ALU.add).then_inc(w_added, 1)
                pool.wait_ge(w_added, b + 1)
                nc.gpsimd.tensor_tensor(wf[:], wf[:], wm[:], ALU.subtract).then_inc(w_round, 1)
                pool.wait_ge(in_made, b + 1)
                pool.wait_ge(out_max, b + 1)
                pool.wait_ge(out_sum, 8 * b + 8)
                nc.gpsimd.tensor_tensor(outside[:], xlT[:, bass.ds(KT * b, KT), :], inside[:], ALU.subtract).then_inc(out_made, 1)

            pair_bodies(pool, body)
            pool.wait_ge(zvared, 1)
            nc.gpsimd.tensor_tensor(zrstd[:], zvar[:], power[:], ALU.pow).then_inc(zroot, 1)

        @block.scalar
        def _(act):
            act.sem_inc(out_sum, KT)
            act.sem_inc(in_sum, KT)
            act.sem_inc(placed, 4)
            act.wait_ge(inverse, 1)

            def body(b, p):
                act.wait_ge(w_in, 16 * b + 16)
                nc.scalar.activation(wf[:], wf[:], ACT.Copy, scale=ws[:, 1:2]).then_inc(w_scaled, 1)
                for f in range(4):
                    act.wait_ge(turned, 4 * b + f + 9)
                    nc.scalar.activation(xlT[:, bass.ds(KT * b + 2 * f, 2), :], turn_ps[f][:], ACT.Copy).then_inc(placed, 1)
                for s in range(2):
                    act.wait_ge((in_made, out_made)[s], b + 1 + s)
                    act.wait_ge((out_sum, in_sum)[s], KT * (b + s) + KT)
                    act.sem_inc(act_held, 1)
                    for k in range(KT):
                        nc.scalar.activation(junk[:, k, :], (inside, outside)[s][:, k, :], ACT.Copy,
                                             accum_out=sums[:, s, bass.ds(KT * b + k, 1)]).then_inc((in_sum, out_sum)[s], 1)

            pair_bodies(act, body)
            act.wait_ge(znormed, 1)
            nc.scalar.activation(gate[:], z[:], ACT.Sigmoid).then_inc(gated, 1)

        @block.tensor
        def _(pe):
            pe.sem_inc(turned, 8)

            def body(b, p):
                pe.wait_ge(normed, b + 1)
                for f in range(4):
                    pe.wait_ge(placed, 4 * b + f + 1)
                    for j in range(4):
                        k, a = 2 * f + j // 2, j % 2
                        ins = nc.tensor.transpose(turn_ps[f][:, j // 2, a * P:(a + 1) * P], xn[p][:, a, k * P:(k + 1) * P], ident[:])
                    ins.then_inc(turned, 1)

            pair_bodies(pe, body)
            pe.wait_ge(averaged, 1)
            n = 0
            for c in range(2):
                f3 = feat[:, c, :, :].rearrange("p s (b k) -> p (s b) k", k=KT)
                z3 = z_ps[:].rearrange("p s (b k) -> p (s b) k", k=KT)
                for lo, dst, src in ((P, slice(0, KT), slice(0, KT)), (2 * P, slice(1, KT), slice(0, KT - 1)),
                                     (0, slice(0, KT - 1), slice(1, KT))):
                    ins = nc.tensor.matmul(z3[:, :, dst], band[:, c, lo:lo + P], f3[:, :, src], start=(n == 0), stop=(n == 5),
                                           skip_group_check=True)
                    n += 1
            ins.then_inc(convolved, 1)
            for i in range(2):
                pe.wait_ge(summed, i + 1)
                nc.tensor.matmul(sum_ps[:, i, :], ones[:], zsum[:], start=True, stop=True).then_inc(totalled, 1)

        @block.vector
        def _(dve):
            dve.sem_inc(out_made, 1)
            dve.sem_inc(out_max, 1)
            dve.wait_ge(small_in, 64)
            nc.vector.reciprocal(ws[:, 1:2], ws[:, 0:1]).then_inc(inverse, 1)
            steps = Steps(dve, step)
            rows_variances(nc, dve, steps, held, X, 0, stats, mv, ve, var)

            def norm(b, p):
                dve.wait_ge(root, b + 1)
                dve.wait_ge(turned, 4 * b + 4)
                for a in range(CT):
                    ins = nc.vector.tensor_scalar(xn[p][:, a:a + 1, :], X[:, bass.ds(CT * b + a, 1), :], mv[:, a, 0:1],
                                                  rstd[:, a:a + 1], ALU.subtract, ALU.mult)
                ins.then_inc(normed, 1)

            norm(0, 0)
            dve.wait_ge(const, 4)
            for c in range(2):
                for t in range(7):
                    if t == 0:
                        steps.done(nc.vector.tensor_scalar(band[:, c, :], joint[:, t:t + 3 * P], taps[:, c, t:t + 1], None, ALU.mult))
                    else:
                        steps.wait()
                        steps.done(nc.vector.scalar_tensor_tensor(band[:, c, :], joint[:, t:t + 3 * P], taps[:, c, t:t + 1], band[:, c, :],
                                                                  ALU.mult, ALU.add))
            before = steps.n

            def body(b, p):
                nonlocal steps
                steps = Steps(dve, step, before + 4 * b)
                if not at(b, B - 1):
                    rows_variances(nc, dve, steps, held, X, b + 1, stats, mv, ve, var)
                dve.wait_ge(w_scaled, b + 1)
                steps.done(nc.vector.tensor_scalar(wm[:].bitcast(I32), wf[:].bitcast(I32), EXPONENT, None, ALU.bitwise_and))
                steps.wait()
                nc.vector.tensor_scalar(wm[:], wm[:], FP8_LEAST, TO_GRID, ALU.max, ALU.mult).then_inc(w_grid, 1)
                dve.wait_ge(placed, 4 * b + 8)
                dve.wait_ge(mask_in[p], 8 * (b - p) + 16)
                dve.wait_ge(in_sum, KT * b + KT)
                dve.wait_ge(out_made, b + 1)
                nc.vector.tensor_tensor(inside[:], xlT[:, bass.ds(KT * b, KT), :], mask[p][:], ALU.mult).then_inc(in_made, 1)
                if not at(b, B - 1):
                    norm(b + 1, 1 - p)
                dve.wait_ge(in_made, b + 1)
                nc.vector.tensor_reduce(feat[:, 0, 0, bass.ds(KT * b, KT)], inside[:], AX.X, ALU.max)
                dve.wait_ge(w_round, b + 1)
                steps.done(nc.vector.tensor_scalar(wm[:], wf[:], OVERFLOW, 0.0, ALU.mult, ALU.mult))
                steps.wait()
                nc.vector.tensor_tensor(w8[:, bass.ds(b, 1), :], wm[:].unsqueeze(1), wf[:].unsqueeze(1), ALU.add).then_inc(w_done, 1)
                dve.wait_ge(out_made, b + 2)
                nc.vector.tensor_reduce(feat[:, 0, 1, bass.ds(KT * b, KT)], outside[:], AX.X, ALU.max).then_inc(out_max, 1)

            pair_bodies(dve, body)
            steps = Steps(dve, step, before + 4 * B - 2)
            dve.wait_ge(in_sum, KT * (B + 1))
            dve.wait_ge(out_sum, KT * (B + 1))
            for s, n in enumerate((TOPK, REST)):
                ins = nc.vector.tensor_scalar(feat[:, 1, s, :], sums[:, s, :], 1.0 / C, C / n, ALU.mult, ALU.mult)
            ins.then_inc(averaged, 1)
            dve.wait_ge(convolved, 1)
            steps.done(nc.vector.tensor_copy(z[:], z_ps[:]))
            steps.wait()
            nc.vector.tensor_reduce(zsum[:], z[:], AX.X, ALU.add).then_inc(summed, 1)
            dve.wait_ge(totalled, 1)
            steps.done(nc.vector.tensor_scalar(mean[:], sum_ps[:, 0, :], 1.0 / (B * D), None, ALU.mult))
            steps.wait()
            for s in range(2):
                ins = nc.vector.tensor_scalar(z[:, s, :], z[:, s, :], mean[:, s:s + 1], None, ALU.subtract)
            steps.done(ins)
            steps.wait()
            steps.done(nc.vector.tensor_tensor(zsq[:], z[:], z[:], ALU.mult))
            steps.wait()
            nc.vector.tensor_reduce(zsum[:], zsq[:], AX.X, ALU.add).then_inc(summed, 1)
            dve.wait_ge(totalled, 2)
            nc.vector.tensor_scalar(zvar[:], sum_ps[:, 1, :], 1.0 / (B * D), EPS, ALU.mult, ALU.add).then_inc(zvared, 1)
            dve.wait_ge(zroot, 1)
            for s in range(2):
                ins = nc.vector.tensor_scalar(z[:, s, :], z[:, s, :], zrstd[:, s:s + 1], affine[:, 0:1], ALU.mult, ALU.mult)
            steps.done(ins)
            steps.wait()
            nc.vector.tensor_scalar(z[:], z[:], affine[:, 1:2], 0.0, ALU.add, ALU.max).then_inc(znormed, 1)
            dve.wait_ge(gated, 1)
            nc.vector.tensor_tensor(gates[:, 0, :], gate[:, 0, :], gate[:, 1, :], ALU.subtract)
            nc.vector.tensor_copy(gates[:, 1, :], gate[:, 1, :])


def apply_gates(nc, mask_t, X, xlT, gates, ident):
    with ExitStack() as st:
        def sb(name, shape, dt=F32):
            return st.enter_context(nc.sbuf_tensor(name, shape, dt))

        def sem(name):
            return st.enter_context(nc.semaphore(name))

        mask = [sb(f"e_mask{p}", [P, KT, C], BF16) for p in range(2)]
        own = [sb(f"e_own{p}", [P, 2, KT]) for p in range(2)]
        part = [sb(f"e_part{p}", [P, KT, C]) for p in range(2)]
        turn_ps = [st.enter_context(nc.psum_tensor(f"e_turn{i}", [P, HW], F32)) for i in range(4)]
        mask_in = [sem(f"e_mask_in{p}") for p in range(2)]
        owned = sem("e_owned")
        chosen = sem("e_chosen")
        multiplied = sem("e_multiplied")
        turned = sem("e_turned")
        added = sem("e_added")
        act_held = sem("e_held_act")
        block = st.enter_context(nc.Block())
        masks = mask_t.rearrange("(b k) p c -> b p k c", k=KT)

        @block.sync
        def _(sp):
            def load_mask(b, p):
                sp.dma_start(mask[p][:], masks[bass.ds(b, 1)].rearrange("o p k c -> (o p) k c")).then_inc(mask_in[p], 16)

            load_mask(0, 0)
            load_mask(1, 1)
            with sp.Fori(0, B // 2 - 1) as i:
                for p in range(2):
                    sp.wait_ge(chosen, KT * (2 * i + p) + KT + 16)
                    load_mask(2 * i + p + 2, p)

        @block.scalar
        def _(act):
            act.sem_inc(chosen, 2 * KT)

            def body(b, p):
                act.wait_ge(mask_in[p], 8 * (b - p) + 16)
                act.wait_ge(owned, b + 1)
                act.wait_ge(turned, 4 * b + 4)
                act.sem_inc(act_held, 1)
                for k in range(KT):
                    nc.scalar.activation(part[p][:, k, :], mask[p][:, k, :], ACT.Identity, scale=own[p][:, 0, k:k + 1],
                                         bias=own[p][:, 1, k:k + 1]).then_inc(chosen, 1)

            pair_bodies(act, body)

        @block.tensor
        def _(pe):
            pe.sem_inc(turned, 8)

            def body(b, p):
                pe.wait_ge(multiplied, b + 1)
                for f in range(4):
                    a, h = f // 2, f % 2
                    pe.wait_ge(added, 4 * b + f + 1)
                    for j in range(4):
                        ins = nc.tensor.transpose(turn_ps[f][:, j * P:(j + 1) * P], part[p][:, 4 * h + j, a * P:(a + 1) * P], ident[:])
                    ins.then_inc(turned, 1)

            pair_bodies(pe, body)

        @block.vector
        def _(dve):
            dve.sem_inc(added, 4)

            def take(b, p):
                dve.wait_ge(chosen, KT * b + KT)
                nc.vector.tensor_copy(own[p][:], gates[:, :, bass.ds(KT * b, KT)]).then_inc(owned, 1)

            take(0, 0)
            take(1, 1)

            def body(b, p):
                dve.wait_ge(chosen, KT * b + KT + 16)
                nc.vector.tensor_tensor(part[p][:], part[p][:], xlT[:, bass.ds(KT * b, KT), :], ALU.mult).then_inc(multiplied, 1)
                if not (isinstance(b, int) and b >= B - 2):
                    take(b + 2, p)
                for f in range(4):
                    a, h = f // 2, f % 2
                    piece = X[:, bass.ds(CT * b + a, 1), h * HW:(h + 1) * HW]
                    dve.wait_ge(turned, 4 * b + f + 9)
                    nc.vector.tensor_tensor(piece, piece, turn_ps[f][:].unsqueeze(1), ALU.add).then_inc(added, 1)

            pair_bodies(dve, body)


def fp8_ffn(nc, bias, in_scale, w_scale, out, X, w8, identb):
    with ExitStack() as st:
        def sb(name, shape, dt=F32):
            return st.enter_context(nc.sbuf_tensor(name, shape, dt))

        def ps(name, shape, dt=F32):
            return st.enter_context(nc.psum_tensor(name, shape, dt))

        def sem(name):
            return st.enter_context(nc.semaphore(name))

        stats = sb("d_stats", [P, CT, 2, 6])
        mv = sb("d_mv", [P, CT, 2])
        ve = sb("d_ve", [P, CT])
        rstd = sb("d_rstd", [P, CT])
        power = sb("d_power", [P, CT])
        rate = [sb(f"d_rate{p}", [P, CT]) for p in range(2)]
        offset = [sb(f"d_offset{p}", [P, CT]) for p in range(2)]
        y = [sb(f"d_y{p}", [P, CT, D]) for p in range(2)]
        grid = [sb(f"d_grid{p}", [P, CT, D]) for p in range(2)]
        x8 = [sb(f"d_x8_{p}", [P, CT, D], BF16) for p in range(2)]
        x8T = [sb(f"d_x8T{p}", [P, CT, KT, P], BF16) for p in range(2)]
        most = sb("d_most", [P, CT])
        flag = sb("d_flag", [P, CT])
        back = [sb(f"d_back{p}", [P, CT]) for p in range(2)]
        scales = sb("d_scales", [P, 4])
        bias_row = sb("d_bias", [P, 1, D])
        made = [sb(f"d_out{p}", [P, CT, D]) for p in range(2)]
        turn_ps = [ps(f"d_turn{i}", [P, KT, P], BF16) for i in range(2)]
        out_ps = [ps(f"d_out_ps{i}", [P, HW]) for i in range(4)]

        small_in = sem("d_small_in")
        const = sem("d_const")
        inverse = sem("d_inverse")
        var = sem("d_var")
        root = sem("d_root")
        rated = sem("d_rated")
        scaled = sem("d_scaled")
        gridded = sem("d_gridded")
        lifted = sem("d_lifted")
        biased = sem("d_biased")
        rounded = sem("d_rounded")
        backed = sem("d_backed")
        turned = sem("d_turned")
        placed = sem("d_placed")
        multiplied = sem("d_multiplied")
        finished = sem("d_finished")
        stored = [sem(f"d_stored{p}") for p in range(2)]
        step = sem("d_step")
        held, pool_held = (sem(f"d_held_{e}") for e in ("dve", "pool"))
        block = st.enter_context(nc.Block())
        out_rows = out.rearrange("b (a p) d -> b p a d", p=P)

        @block.sync
        def _(sp):
            sp.dma_start(scales[:, 0:1], in_scale.partition_broadcast(P)).then_inc(small_in, 16)
            sp.dma_start(scales[:, 1:2], w_scale.partition_broadcast(P)).then_inc(small_in, 16)
            sp.dma_start(bias_row[:, 0, :], bias.partition_broadcast(P)).then_inc(small_in, 16)
            for p in range(2):
                sp.sem_inc(stored[p], 16)

            def body(b, p):
                sp.wait_ge(finished, 4 * b + 8)
                sp.dma_start(out_rows[bass.ds(b, 1)].rearrange("o p a d -> (o p) a d"), made[p][:]).then_inc(stored[p], 16)

            pair_bodies(sp, body)
            for p in range(2):
                sp.wait_ge(stored[p], 8 * B + 16)

        @block.gpsimd
        def _(pool):
            nc.gpsimd.memset(power[:], -0.5).then_inc(const, 1)
            pool.wait_ge(const, 1)

            def rstd_of(b):
                pool.wait_ge(var, b + 1)
                nc.gpsimd.tensor_tensor(rstd[:], ve[:], power[:], ALU.pow).then_inc(root, 1)

            rstd_of(0)
            pool.wait_ge(small_in, 48)

            def body(b, p):
                if not at(b, B - 1):
                    rstd_of(b + 1)
                pool.wait_ge(gridded, b + 1)
                nc.gpsimd.tensor_tensor(y[p][:], y[p][:], grid[p][:], ALU.add).then_inc(lifted, 1)
                rows = X[:, bass.ds(CT * b, CT), :]
                nc.gpsimd.tensor_tensor(rows, rows, bias_row[:].to_broadcast([P, CT, D]), ALU.add).then_inc(biased, 1)

            pair_bodies(pool, body)

        @block.scalar
        def _(act):
            act.sem_inc(placed, 2)

            def scale_rows(b, p):
                act.wait_ge(rated, b + 1)
                act.wait_ge(rounded, b + 1)
                for a in range(CT):
                    nc.scalar.activation(y[p][:, a:a + 1, :], X[:, bass.ds(CT * b + a, 1), :], ACT.Identity,
                                         scale=rate[p][:, a:a + 1], bias=offset[p][:, a:a + 1]).then_inc(scaled, 1)

            scale_rows(0, 0)

            def body(b, p):
                if not at(b, B - 1):
                    scale_rows(b + 1, 1 - p)
                for a in range(CT):
                    act.wait_ge(turned, 2 * b + a + 5)
                    if a == 0:
                        act.wait_ge(multiplied, 4 * b + 4)
                    nc.scalar.activation(x8T[p][:, a, :, :], turn_ps[a][:], ACT.Copy).then_inc(placed, 1)

            pair_bodies(act, body)

        @block.tensor
        def _(pe):
            pe.sem_inc(turned, 4)
            pe.sem_inc(multiplied, 8)

            def turn(b, p):
                pe.wait_ge(rounded, b + 3)
                for a in range(CT):
                    pe.wait_ge(placed, 2 * b + a + 1)
                    for k in range(KT):
                        ins = nc.tensor.transpose(turn_ps[a][:, k, :], x8[p][:, a, k * P:(k + 1) * P], identb[:])
                    ins.then_inc(turned, 1)

            def multiply(b, p):
                for a in range(CT):
                    pe.wait_ge(placed, 2 * b + a + 3)
                    for h in range(2):
                        o = 2 * a + h
                        pe.wait_ge(finished, 4 * b + o + 1)
                        for k in range(KT):
                            ins = nc.tensor.matmul(out_ps[o][:], x8T[p][:, a, k, :], w8[:, k, h * HW:(h + 1) * HW],
                                                   start=(k == 0), stop=(k == KT - 1))
                        ins.then_inc(multiplied, 1)

            turn(0, 0)

            def body(b, p):
                if not at(b, B - 1):
                    turn(b + 1, 1 - p)
                multiply(b, p)

            pair_bodies(pe, body)

        @block.vector
        def _(dve):
            dve.sem_inc(rounded, 2)
            dve.sem_inc(finished, 4)
            steps = Steps(dve, step)
            rows_variances(nc, dve, steps, held, X, 0, stats, mv, ve, var)
            dve.wait_ge(small_in, 48)
            nc.vector.tensor_tensor(scales[:, 3:4], scales[:, 0:1], scales[:, 1:2], ALU.mult)
            steps.done(nc.vector.reciprocal(scales[:, 2:3], scales[:, 0:1]))
            steps.wait()

            def rates(b, p):
                dve.wait_ge(root, b + 1)
                if not at(b, 0):
                    dve.wait_ge(scaled, 2 * b)
                steps.done(nc.vector.tensor_scalar(rate[p][:], rstd[:], scales[:, 2:3], None, ALU.mult))
                steps.wait()
                nc.vector.scalar_tensor_tensor(offset[p][:], mv[:, :, 0], -1.0, rate[p][:], ALU.mult, ALU.mult).then_inc(rated, 1)

            rates(0, 0)
            before = steps.n

            def finish(b, p):
                dve.wait_ge(backed, b + 1)
                dve.wait_ge(biased, b + 1)
                dve.wait_ge(stored[p], 8 * (b - p) + 16)
                for a in range(CT):
                    for h in range(2):
                        o = 2 * a + h
                        cols = slice(h * HW, (h + 1) * HW)
                        dve.wait_ge(multiplied, 4 * b + o + 9)
                        nc.vector.scalar_tensor_tensor(made[p][:, a:a + 1, cols], out_ps[o][:].unsqueeze(1), back[p][:, a:a + 1],
                                                       X[:, bass.ds(CT * b + a, 1), cols], ALU.mult, ALU.add).then_inc(finished, 1)

            def body(b, p):
                nonlocal steps
                steps = Steps(dve, step, before + 6 * b)
                dve.wait_ge(scaled, 2 * b + 2)
                steps.done(nc.vector.tensor_scalar(grid[p][:].bitcast(I32), y[p][:].bitcast(I32), EXPONENT, None, ALU.bitwise_and))
                steps.wait()
                nc.vector.tensor_scalar(grid[p][:], grid[p][:], FP8_LEAST, TO_GRID, ALU.max, ALU.mult).then_inc(gridded, 1)
                if not at(b, B - 1):
                    rows_variances(nc, dve, steps, held, X, b + 1, stats, mv, ve, var)
                dve.wait_ge(lifted, b + 1)
                dve.wait_ge(turned, 2 * b + 2)
                nc.vector.tensor_tensor(x8[p][:], y[p][:], grid[p][:], ALU.subtract).then_inc(rounded, 1)
                if not at(b, B - 1):
                    rates(b + 1, 1 - p)
                dve.wait_ge(rounded, b + 3)
                steps.done(nc.vector.tensor_reduce(most[:], x8[p][:], AX.X, ALU.max, apply_absolute_value=True))
                steps.wait()
                steps.done(nc.vector.tensor_scalar(flag[:], most[:], OVERFLOW, 0.0, ALU.mult, ALU.mult))
                steps.wait()
                nc.vector.tensor_scalar(back[p][:], flag[:], scales[:, 3:4], None, ALU.add).then_inc(backed, 1)
                if not at(b, 0):
                    finish(b - 1, 1 - p)

            body(0, 0)
            with dve.Fori(0, B // 2 - 1) as i:
                body(2 * i + 1, 1)
                body(2 * i + 2, 0)
            body(B - 1, 1)
            finish(B - 1, 1)


def program(nc, x, ctx, gate_codes, gate_scales, up_codes, up_scales, down_codes, down_scales, conv_w, gamma, beta,
            weight, bias, in_scale, w_scale, out):
    ctx_t = nc.dram_tensor("ctx_t", [B, KT, P, C], F32, kind="Internal").ap()
    mask_t = nc.dram_tensor("mask_t", [TILES, P, C], BF16, kind="Internal").ap()
    with ExitStack() as st:
        X = st.enter_context(nc.sbuf_tensor("x_rows", [P, NT, D], F32))
        ident = st.enter_context(nc.sbuf_tensor("ident", [P, P], F32))
        identb = st.enter_context(nc.sbuf_tensor("identb", [P, P], BF16))
        with ExitStack() as ffn:
            xT = [ffn.enter_context(nc.sbuf_tensor(f"xT_{n}", [P, KT, NT * P], BF16)) for n in ("high", "low")]
            attention(nc, x, ctx, ctx_t, X, xT, ident, identb)
            gated_ffn(nc, (gate_codes, up_codes, down_codes), (gate_scales, up_scales, down_scales), ctx_t, mask_t, X, xT, identb)
        w8 = st.enter_context(nc.sbuf_tensor("w8", [P, KT, D], BF16))
        with ExitStack() as channels:
            xlT = channels.enter_context(nc.sbuf_tensor("xlT", [P, TILES, C], F32))
            gates = channels.enter_context(nc.sbuf_tensor("gates", [P, 2, TILES], F32))
            pooled(nc, mask_t, conv_w, gamma, beta, weight, w_scale, X, xlT, gates, w8, ident)
            apply_gates(nc, mask_t, X, xlT, gates, ident)
        fp8_ffn(nc, bias, in_scale, w_scale, out, X, w8, identb)


_INS = ["x", "ctx_4096", "L0_ffn_gate_codes", "L0_ffn_gate_scales", "L0_ffn_up_codes", "L0_ffn_up_scales",
        "L0_ffn_down_codes", "L0_ffn_down_scales", "L1_xattn_conv_w", "L1_xattn_bn_gamma", "L1_xattn_bn_beta",
        "L1_ffn_weight", "L1_ffn_bias", "L1_ffn_input_scale", "L1_ffn_weight_scale"]
_OUTS = [((B, C, D), "float32")]


def kernel(**inputs):
    import numpy as _np
    import concourse.bacc as _bacc
    from concourse import mybir as _mybir
    from concourse.bass_utils import run_bass_kernel_spmd as _run

    nc = _bacc.Bacc("TRN2", target_bir_lowering=False, num_devices=1)
    arrays, args = {}, []
    for name in _INS:
        a = _np.ascontiguousarray(inputs[name])
        arrays[f"in_{name}_dram"] = a
        args.append(nc.dram_tensor(f"in_{name}_dram", a.shape, _mybir.dt.from_np(a.dtype), kind="ExternalInput").ap())
    for i, (shape, dtype) in enumerate(_OUTS):
        dt = _mybir.dt.from_np(_np.dtype(dtype))
        args.append(nc.dram_tensor(f"out_{i}_dram", shape, dt, kind="ExternalOutput").ap())
    program(nc, *args)
    r = _run(nc, [arrays], core_ids=[0])
    got = tuple(r.results[0][f"out_{i}_dram"] for i in range(len(_OUTS)))
    return got[0]
```

```python
import math
from contextlib import ExitStack

import numpy as np

import concourse.bass as bass
import concourse.mybir as mybir

F32 = mybir.dt.float32
BF16 = mybir.dt.bfloat16
I32 = mybir.dt.int32
ALU = mybir.AluOpType
ACT = mybir.ActivationFunctionType
AX = mybir.AxisListType

P = 128
B, C, D = 8, 256, 1024
CT = C // P
NT = B * CT
KT = D // P
I = 2752
NB = -(-I // P)
LAST = I - (NB - 1) * P
SB = 64
HW = 512
EPS = 1e-5
TOPK = math.floor(0.6 * C) + math.floor(0.6 * C) % 2
REST = C - TOPK
ROUNDS = -(-REST // 8)
GONE = -3.0e38

EXPONENT = 0x7F800000
TO_GRID = 1.5 * 2.0 ** 20
FP8_LEAST = 2.0 ** -6
OVERFLOW = 7.4e35

LOW = [(-0.09372339397668839, 0.6533904075622559), (-0.11047609895467758, 0.7263457775115967),
       (-0.060643620789051056, 0.14096669852733612), (-0.2653747797012329, 0.132687509059906)]
HIGH = [(0.08134989440441132, -0.5712188482284546), (0.0918029323220253, -0.6719170212745667),
        (0.0301042553037405, -0.350259393453598), (0.15513597428798676, -2.1334710121154785)]


class Steps:

    def __init__(self, eng, sem, base=0):
        self.eng, self.sem, self.base, self.n = eng, sem, base, 0

    def done(self, ins):
        ins.then_inc(self.sem, 1)
        self.n += 1

    def wait(self, held=None):
        self.eng.wait_ge(self.sem, self.base + self.n)
        if held is not None:
            self.eng.sem_inc(held, 1)


def at(m, n):
    return isinstance(m, int) and m == n


def identity(nc, pool, made, sem, n):
    nc.gpsimd.memset(made, 0.0).then_inc(sem, 1)
    pool.wait_ge(sem, n + 1)
    nc.gpsimd.affine_select(out=made, in_=made, compare_op=ALU.not_equal, fill=1.0, base=0,
                            pattern=[[-1, P]], channel_multiplier=1).then_inc(sem, 1)


CHUNK = 2
CHUNKS = NB // CHUNK
UNITS = 6 * CHUNK
PACKED = 2 * LAST <= P
EARLY = 5
GROUPS = NT * P // HW
PASSES = ((0, 0), (0, 1), (1, 0))
TILES = B * KT
TILE_CHUNK = 6
LANE_ROUNDS = TILE_CHUNK // 2 * ROUNDS
AHEAD = ROUNDS // 2
GROUP_ROUNDS = 4


def unit(c, j):
    if j >= UNITS:
        c, j = c + 1, j - UNITS
    if isinstance(c, int) and UNITS * c + j >= UNITS * CHUNKS - EARLY:
        return None
    if j < 3:
        which, half, n, buf = (j + 1) // 2, (j + 1) % 2, CHUNK * c + 1, 1
    elif j < 7:
        which, half, n, buf = 2, (j - 3) % 2, CHUNK * c + (j - 3) // 2, (j - 3) // 2
    elif j < 11:
        which, half, n, buf = (j - 7) // 2, (j - 7) % 2, CHUNK * c + 2, 0
    else:
        which, half, n, buf = 0, 0, CHUNK * c + 3, 1
    return which, n, half, LAST if at(n, NB - 1) else P, buf


def number(c, j):
    return EARLY + UNITS * c + j


def code_slot(j):
    return (j + EARLY) % 3


def load_codes(pool, codes_in, code, code_in, c, j):
    un = unit(c, j)
    if un is None:
        return
    which, n, half, r, _ = un
    slot = code_slot(j)
    if which < 2:
        src = codes_in[which][bass.ds(n * P, r), half * HW:(half + 1) * HW]
        dst = code[slot][0:r, :]
    else:
        src = codes_in[2][half * HW:(half + 1) * HW, bass.ds(n * P, r)].rearrange("(t p) i -> p t i", p=P)
        dst = code[slot][:, 0:4 * r].rearrange("p (t i) -> p t i", t=4)
    pool.dma_start(dst, src).then_inc(code_in[slot], 16)


def attention(nc, x, ctx, weight, w_scale, codes_in, scales_in, ctx_t, w8_t, X, xT, codes, ident, identb):
    with ExitStack() as st:
        def sb(name, shape, dt=F32):
            return st.enter_context(nc.sbuf_tensor(name, shape, dt))

        def sem(name):
            return st.enter_context(nc.semaphore(name))

        cb = [sb(f"a_ctx{p}", [P, CT, D]) for p in range(2)]
        q = sb("a_q", [P, CT, D])
        xn = sb("a_xn", [P, CT, D])
        qT = sb("a_qT", [P, KT, C])
        kT = sb("a_kT", [P, KT, C])
        prob = sb("a_prob", [P, CT, C])
        stats = sb("a_stats", [P, 2, CT, 2, 6])
        mv = sb("a_mv", [P, 2, CT, 2])
        ve = sb("a_ve", [P, 2, CT])
        rstd = sb("a_rstd", [P, 2, CT])
        power = sb("a_power", [P, CT])
        low = sb("a_low", [P, CT])
        bias = sb("a_bias", [P, CT])
        total = sb("a_total", [P, CT])
        rtotal = sb("a_rtotal", [P, CT])
        ws = sb("a_ws", [P, 2])
        wf = [sb(f"a_wf{p}", [P, D]) for p in range(2)]
        wm = sb("a_wm", [P, D])
        w8 = sb("a_w8", [P, D], BF16)
        turned = [st.enter_context(nc.psum_tensor(f"a_turn{i}", [P, HW], F32)) for i in range(4)]
        scores = st.enter_context(nc.psum_tensor("a_scores", [P, CT, C], F32))
        cont = [st.enter_context(nc.psum_tensor(f"a_cont{i}", [P, HW], F32)) for i in range(2)]

        code, code_in, gu_scale, dn_scale, scale_in = codes
        const = sem("a_const")
        x_in = [sem(f"a_x_in{p}") for p in range(2)]
        c_in = [sem(f"a_c_in{p}") for p in range(2)]
        kt_out = sem("a_kt_out")
        var_q = sem("a_var_q")
        var_x = sem("a_var_x")
        rstd_q = sem("a_rstd_q")
        rstd_x = sem("a_rstd_x")
        q_made = sem("a_q_made")
        t1 = sem("a_t1")
        t2 = sem("a_t2")
        qt_made = sem("a_qt_made")
        kt_made = sem("a_kt_made")
        scored = sem("a_scored")
        bias_made = sem("a_bias_made")
        exped = sem("a_exped")
        prob_made = sem("a_prob_made")
        cont_made = sem("a_cont_made")
        added = sem("a_added")
        xn_made = sem("a_xn_made")
        hi_made = sem("a_hi_made")
        lo_made = sem("a_lo_made")
        ws_in = sem("a_ws_in")
        inverse = sem("a_inverse")
        w_in = [sem(f"a_w_in{p}") for p in range(2)]
        w_scaled = sem("a_w_scaled")
        w_grid = sem("a_w_grid")
        w_added = sem("a_w_added")
        w_round = sem("a_w_round")
        w_beyond = sem("a_w_beyond")
        w_done = sem("a_w_done")
        w_out = sem("a_w_out")
        step = sem("a_step")
        held, sp_held = (sem(f"a_held_{e}") for e in ("dve", "sp"))
        block = st.enter_context(nc.Block())

        x_rows = x.rearrange("b (a p) d -> b p a d", p=P)
        c_rows = ctx.rearrange("b (a p) d -> b p a d", p=P)
        ctx_tiles = ctx_t.rearrange("b k p c -> b p k c")
        w_rows = weight.rearrange("(k p) o -> k p o", p=P)

        def bodies(eng, body):
            body(0, 0, True, False)
            with eng.Fori(0, B // 2 - 1) as i:
                body(2 * i + 1, 1, True, True)
                body(2 * i + 2, 0, True, True)
            body(B - 1, 1, True, True)
            body(B, 0, False, True)

        @block.sync
        def _(sp):
            def load_x(n, p):
                sp.dma_start(X[:, bass.ds(CT * n, CT), :], x_rows[bass.ds(n, 1)].rearrange("o p a d -> (o p) a d")).then_inc(x_in[p], 16)

            def load_c(n, p):
                sp.dma_start(cb[p][:], c_rows[bass.ds(n, 1)].rearrange("o p a d -> (o p) a d")).then_inc(c_in[p], 16)

            def load_w(k, p):
                sp.dma_start(wf[p][:], w_rows[bass.ds(k, 1)].rearrange("o p n -> (o p) n")).then_inc(w_in[p], 16)

            def body(m, p, first, second):
                if second:
                    sp.wait_ge(w_done, m)
                    sp.sem_inc(sp_held, 1)
                    sp.dma_start(w8_t[bass.ds(m - 1, 1)].rearrange("o p n -> (o p) n"), w8[:]).then_inc(w_out, 16)
                    if first and not at(m, B - 1):
                        load_w(m + 1, 1 - p)
                if first:
                    sp.wait_ge(kt_made, 4 * m + 4)
                    sp.dma_start(ctx_tiles[bass.ds(m, 1)].rearrange("o p k c -> (o p) k c"), kT[:]).then_inc(kt_out, 16)
                if first and second and not at(m, B - 1):
                    sp.wait_ge(cont_made, 4 * m)
                    load_c(m + 1, 1 - p)

            load_x(0, 0)
            sp.dma_start(ws[:, 0:1], w_scale.partition_broadcast(P)).then_inc(ws_in, 16)
            load_c(0, 0)
            load_x(1, 1)
            load_c(1, 1)
            for k in range(2):
                load_w(k, k)
            sp.sem_inc(w_out, 16)
            with sp.Fori(0, B // 2 - 1) as i:
                for p in range(2):
                    sp.wait_ge(x_in[p], 16 * i + 16)
                    load_x(2 * i + p + 2, p)
            bodies(sp, body)
            for which in range(2):
                sp.dma_start(gu_scale[which][:, 0:NB - 1, :],
                             scales_in[which][0:(NB - 1) * P, :].rearrange("(n p) s -> p n s", p=P)).then_inc(scale_in, 16)
                sp.dma_start(gu_scale[which][0:LAST, NB - 1, :], scales_in[which][(NB - 1) * P:I, :]).then_inc(scale_in, 16)
            sp.dma_start(dn_scale[:], scales_in[2].rearrange("(t p) s -> p t s", p=P)).then_inc(scale_in, 16)
            sp.wait_ge(kt_out, 16 * B)
            sp.wait_ge(w_out, 16 * B + 16)

        @block.gpsimd
        def _(pool):
            nc.gpsimd.memset(power[:], -0.5).then_inc(const, 1)
            identity(nc, pool, ident[:], const, 1)
            pool.wait_ge(const, 3)
            nc.gpsimd.tensor_copy(identb[:], ident[:]).then_inc(const, 1)
            pool.wait_ge(const, 4)

            def root(made, var, n):
                pool.wait_ge(var, n + 1)
                k = 0 if var is var_q else 1
                nc.gpsimd.tensor_tensor(rstd[:, k, :], ve[:, k, :], power[:], ALU.pow).then_inc(made, 1)

            def body(m, p, first, second):
                if first:
                    pool.wait_ge(w_grid, m + 1)
                    nc.gpsimd.tensor_tensor(wf[p][:], wf[p][:], wm[:], ALU.add).then_inc(w_added, 1)
                    pool.wait_ge(w_added, m + 1)
                    nc.gpsimd.tensor_tensor(wf[p][:], wf[p][:], wm[:], ALU.subtract).then_inc(w_round, 1)
                if second:
                    root(rstd_x, var_x, m - 1)
                if first and not at(m, B - 1):
                    root(rstd_q, var_q, m + 1)

            root(rstd_q, var_q, 0)
            bodies(pool, body)
            for j in range(UNITS - EARLY, UNITS - EARLY + 3):
                load_codes(pool, codes_in, code, code_in, -1, j)

        @block.scalar
        def _(act):
            act.wait_ge(inverse, 1)

            def body(m, p, first, second):
                if first:
                    for f in range(4):
                        act.wait_ge(t1, 8 * m + f + 1)
                        nc.scalar.activation(qT[:, 2 * f:2 * f + 2, :], turned[f][:].rearrange("p (k c) -> p k c", k=2),
                                             ACT.Copy).then_inc(qt_made, 1)
                    for f in range(4):
                        act.wait_ge(t1, 8 * m + 5 + f)
                        if f == 0 and not at(m, 0):
                            act.wait_ge(kt_out, 16 * m)
                        nc.scalar.activation(kT[:, 2 * f:2 * f + 2, :], turned[f][:].rearrange("p (k c) -> p k c", k=2),
                                             ACT.Copy, scale=-1.0).then_inc(kt_made, 1)
                    act.wait_ge(w_in[p], 8 * (m - p) + 16)
                    nc.scalar.activation(wf[p][:], wf[p][:], ACT.Copy, scale=ws[:, 1:2]).then_inc(w_scaled, 1)
                if second:
                    for f in range(4):
                        a, kk = f // 2, f % 2
                        act.wait_ge(t2, 4 * m + f + 1)
                        nc.scalar.activation(xT[0][:, 4 * kk:4 * kk + 4, bass.ds((m - 1) * C + a * P, P)],
                                             turned[f][:].rearrange("p (k t) -> p k t", k=4),
                                             ACT.Copy).then_inc(hi_made, 1)
                if first:
                    act.wait_ge(bias_made, m + 1)
                    for h in range(CT):
                        nc.scalar.activation(prob[:, h, :], scores[:, h, :], ACT.Exp, bias=bias[:, h:h + 1],
                                             scale=-1.0 / math.sqrt(C), accum_out=total[:, h:h + 1]).then_inc(exped, 1)
                    act.wait_ge(w_round, m + 1)
                    nc.scalar.activation(wm[:], wf[p][:], ACT.Copy, scale=OVERFLOW).then_inc(w_beyond, 1)

            bodies(act, body)

        @block.tensor
        def _(pe):
            pe.wait_ge(const, 4)

            def body(m, p, first, second):
                zero = at(m, 0)
                if first:
                    for f in range(8):
                        src = q if f < 4 else cb[p]
                        if f == 0:
                            pe.wait_ge(q_made, m + 1)
                        if f == 4:
                            pe.wait_ge(c_in[p], 8 * (m - p) + 16)
                        if f < 4 and not zero:
                            pe.wait_ge(lo_made, 4 * (m - 1) + f + 1)
                        if f >= 4:
                            pe.wait_ge(qt_made, 4 * m + f - 3)
                        for j in range(4):
                            k, a = 2 * (f % 4) + j // 2, j % 2
                            ins = nc.tensor.transpose(turned[f % 4][:, j * P:(j + 1) * P],
                                                      src[:, a, k * P:(k + 1) * P], ident[:])
                        ins.then_inc(t1, 1)
                if second:
                    pe.wait_ge(prob_made, m)
                    for o in range(4):
                        a, h = o // 2, o % 2
                        pe.wait_ge(added, 4 * (m - 1) + o + 1)
                        for d in range(CT):
                            ins = nc.tensor.matmul(cont[o % 2][:], prob[:, d, a * P:(a + 1) * P],
                                                   cb[1 - p][:, d, h * HW:(h + 1) * HW], start=(d == 0), stop=(d == CT - 1))
                        ins.then_inc(cont_made, 1)
                if first:
                    pe.wait_ge(kt_made, 4 * m + 4)
                    pe.wait_ge(qt_made, 4 * m + 4)
                    if not zero:
                        pe.wait_ge(exped, 2 * m)
                    for h in range(CT):
                        for k in range(KT):
                            ins = nc.tensor.matmul(scores[:, h, :], qT[:, k, h * P:(h + 1) * P], kT[:, k, :],
                                                   start=(k == 0), stop=(k == KT - 1))
                    ins.then_inc(scored, 1)
                if second:
                    pe.wait_ge(xn_made, m)
                    for f in range(4):
                        a, kk = f // 2, f % 2
                        if first:
                            pe.wait_ge(kt_made, 4 * m + f + 1)
                        else:
                            pe.wait_ge(lo_made, 4 * (m - 1) + f + 1)
                        for j in range(4):
                            k = 4 * kk + j
                            ins = nc.tensor.transpose(turned[f][:, j * P:(j + 1) * P], xn[:, a, k * P:(k + 1) * P], ident[:])
                        ins.then_inc(t2, 1)

            bodies(pe, body)

        @block.vector
        def _(dve):
            def variances(n, k, var):
                for a in range(CT):
                    for h in range(2):
                        ins = nc.vector.bn_stats(stats[:, k, a, h, :], X[:, bass.ds(CT * n + a, 1), h * HW:(h + 1) * HW])
                steps.done(ins)
                steps.wait(held)
                for a in range(CT):
                    ins = nc.vector.bn_aggr(mv[:, k, a, :], stats[:, k, a, :, :])
                steps.done(ins)
                steps.wait()
                nc.vector.tensor_scalar(ve[:, k, :], mv[:, k, :, 1], EPS, None, ALU.add).then_inc(var, 1)

            def normed(dst, n, k, made):
                for a in range(CT):
                    ins = nc.vector.tensor_scalar(dst[:, a:a + 1, :], X[:, bass.ds(CT * n + a, 1), :], mv[:, k, a, 0:1],
                                                  rstd[:, k, a:a + 1], ALU.subtract, ALU.mult)
                ins.then_inc(made, 1)

            def add(m, o):
                a, h = o // 2, o % 2
                piece = X[:, bass.ds(CT * (m - 1) + a, 1), h * HW:(h + 1) * HW]
                dve.wait_ge(cont_made, 4 * (m - 1) + o + 1)
                nc.vector.tensor_tensor(piece, piece, cont[o % 2][:].unsqueeze(1), ALU.add).then_inc(added, 1)

            def body(m, p, first, second):
                nonlocal steps
                steps = Steps(dve, step, 2 if at(m, 0) else 7 * m - 2 if at(m, B) else 7 * m)
                more = first and not at(m, B - 1)
                if more:
                    dve.wait_ge(x_in[1 - p], 8 * (m + p) + 16)
                    dve.sem_inc(held, 1)
                    variances(m + 1, 0, var_q)
                if second:
                    dve.wait_ge(w_beyond, m)
                    dve.wait_ge(w_out, 16 * m)
                    nc.vector.scalar_tensor_tensor(w8[:], wm[:], 0.0, wf[1 - p][:], ALU.mult, ALU.add).then_inc(w_done, 1)
                if second:
                    add(m, 0)
                    add(m, 1)
                if first:
                    dve.wait_ge(w_scaled, m + 1)
                    if second:
                        dve.wait_ge(w_done, m)
                    steps.done(nc.vector.tensor_scalar(wm[:].bitcast(I32), wf[p][:].bitcast(I32), EXPONENT, None, ALU.bitwise_and))
                    steps.wait()
                    nc.vector.tensor_scalar(wm[:], wm[:], FP8_LEAST, TO_GRID, ALU.max, ALU.mult).then_inc(w_grid, 1)
                if second:
                    add(m, 2)
                    add(m, 3)
                    dve.wait_ge(added, 4 * m + 2)
                    dve.sem_inc(held, 1)
                    variances(m - 1, 1, var_x)
                if second:
                    dve.wait_ge(rstd_x, m)
                    dve.wait_ge(t2, 4 * m)
                    normed(xn, m - 1, 1, xn_made)
                if more:
                    dve.wait_ge(rstd_q, m + 2)
                    dve.wait_ge(t1, 8 * m + 4)
                    normed(q, m + 1, 0, q_made)
                if first:
                    dve.wait_ge(scored, m + 1)
                    steps.done(nc.vector.tensor_reduce(low[:], scores[:], AX.X, ALU.min))
                    steps.wait()
                    nc.vector.tensor_scalar(bias[:], low[:], 1.0 / math.sqrt(C), None, ALU.mult).then_inc(bias_made, 1)
                if second:
                    for f in range(4):
                        a, kk = f // 2, f % 2
                        cols = bass.ds((m - 1) * C + a * P, P)
                        dve.wait_ge(hi_made, 4 * (m - 1) + f + 1)
                        nc.vector.tensor_tensor(xT[1][:, 4 * kk:4 * kk + 4, cols],
                                                turned[f][:].rearrange("p (k t) -> p k t", k=4),
                                                xT[0][:, 4 * kk:4 * kk + 4, cols], ALU.subtract).then_inc(lo_made, 1)
                if first:
                    dve.wait_ge(exped, 2 * m + 2)
                    steps.done(nc.vector.reciprocal(rtotal[:], total[:]))
                    steps.wait()
                    for h in range(CT):
                        ins = nc.vector.tensor_scalar(prob[:, h, :], prob[:, h, :], rtotal[:, h:h + 1], None, ALU.mult)
                    ins.then_inc(prob_made, 1)

            steps = Steps(dve, step)
            dve.sem_inc(lo_made, 4)
            dve.sem_inc(added, 2)
            dve.sem_inc(t2, 4)
            dve.wait_ge(x_in[0], 16)
            variances(0, 0, var_q)
            dve.wait_ge(rstd_q, 1)
            normed(q, 0, 0, q_made)
            dve.wait_ge(ws_in, 16)
            nc.vector.reciprocal(ws[:, 1:2], ws[:, 0:1]).then_inc(inverse, 1)
            bodies(dve, body)


def gated_ffn(nc, codes_in, ctx_t, mask_t, X, xT, codes, x2_mv, identb):
    with ExitStack() as st:
        def sb(name, shape, dt=F32):
            return st.enter_context(nc.sbuf_tensor(name, shape, dt))

        def ps(name, shape, dt=F32):
            return st.enter_context(nc.psum_tensor(name, shape, dt))

        def sem(name):
            return st.enter_context(nc.semaphore(name))

        code, code_in, gu_scale, dn_scale, scale_in = codes
        low_line = [sb(f"b_low_line{i}", [P, HW]) for i in range(4)]
        high_line = [sb(f"b_high_line{i}", [P, HW]) for i in range(4)]
        weight = [sb(f"b_weight{i}", [P, HW]) for i in range(2)]
        parts = [sb(f"b_parts{i}", [P, 2, HW], BF16) for i in range(2)]
        gu_w = [sb(f"b_gate_up{i}", [P, 2, 2, KT, P], BF16) for i in range(2)]
        dn_w = [sb(f"b_down{i}", [P, 2, D], BF16) for i in range(2)]
        inner = [[sb(f"b_inner{b}_{n}", [P, NT * P], BF16) for n in ("high", "low")] for b in range(CHUNK)]
        act_in = [sb(f"b_gated{i}", [P, HW]) for i in range(2)]
        left = [sb(f"b_left{i}", [P, C]) for i in range(3)]
        best = [sb(f"b_best{i}", [P, 8]) for i in range(2)]
        line_bias = sb("b_line_bias", [P, 2, len(LOW)])
        stats = sb("b_stats", [P, 2, 2, 6])
        mask = sb("b_mask", [P, C], BF16)
        gate_ps = [ps(f"b_gate_ps{i}", [P, HW]) for i in range(2)]
        up_ps = [ps(f"b_up_ps{i}", [P, HW]) for i in range(2)]
        turn_ps = [ps(f"b_turn_ps{i}", [P, 2, HW], BF16) for i in range(2)]
        down_ps = [ps(f"b_down_ps{i}", [P, HW]) for i in range(2)] + [gate_ps[1], up_ps[1]]

        bias_made = sem("b_bias_made")
        lined = sem("b_lined")
        paired = sem("b_paired")
        joined = sem("b_joined")
        decoded = sem("b_decoded")
        scaled = sem("b_scaled")
        high_made = sem("b_high_made")
        low_made = sem("b_low_made")
        turned = sem("b_turned")
        placed = sem("b_placed")
        gu_made = sem("b_gu_made")
        silu_made = sem("b_silu_made")
        gated = sem("b_gated")
        inner_high = sem("b_inner_high")
        inner_low = sem("b_inner_low")
        down_made = sem("b_down_made")
        added = sem("b_added")
        left_in = [sem(f"b_left_in{i}") for i in range(3)]
        found = sem("b_found")
        held, pool_held, sp_held = (sem(f"b_held_{e}") for e in ("dve", "pool", "sp"))
        mask_made = sem("b_mask_made")
        mask_out = sem("b_mask_out")
        block = st.enter_context(nc.Block())

        def size(un):
            which, _, _, r, _ = un
            return (r, HW) if which < 2 else (P, HW * r // P)

        def chunks(eng, chunk):
            with eng.Fori(0, CHUNKS - 2) as c:
                chunk(c)
            chunk(CHUNKS - 2)
            chunk(CHUNKS - 1)

        @block.sync
        def _(sp):
            sp.sem_inc(mask_out, 16)
            tiles = ctx_t.rearrange("b k p c -> (b k) p c")

            def load(t, i):
                sp.dma_start(left[i][:], tiles[bass.ds(t, 1)].rearrange("o p c -> (o p) c")).then_inc(left_in[i], 16)

            for t in range(3):
                load(t, t)

            def chunk(c):
                for k in range(TILE_CHUNK):
                    t = TILE_CHUNK * c + k
                    if isinstance(t, int) and t >= TILES:
                        return
                    sp.wait_ge(mask_made, t + 1)
                    sp.sem_inc(sp_held, 1)
                    sp.dma_start(mask_t[bass.ds(t, 1)].rearrange("o p c -> (o p) c"), mask[:]).then_inc(mask_out, 16)
                    if not (isinstance(t, int) and t + 3 >= TILES):
                        load(t + 3, k % 3)

            chunks(sp, chunk)
            sp.wait_ge(mask_out, 16 * (TILES + 1))

        @block.gpsimd
        def _(pool):
            pool.sem_inc(low_made, 2)
            pool.sem_inc(inner_low, 2)

            def low(c, j):
                a, n = size(unit(c, j))
                u = number(c, j)
                pool.wait_ge(high_made, u + 1)
                nc.gpsimd.tensor_tensor(parts[j % 2][0:a, 1, 0:n], weight[j % 2][0:a, 0:n], parts[j % 2][0:a, 0, 0:n],
                                        ALU.subtract).then_inc(low_made, 1)

            def pair(c, j, i):
                a, n = size(unit(c, j))
                side = (low_line, high_line)[i]
                pool.wait_ge(lined, 4 * number(c, j) + i + 1)
                nc.gpsimd.tensor_tensor(side[2][0:a, 0:n], side[2][0:a, 0:n], side[3][0:a, 0:n], ALU.add).then_inc(paired, 1)

            def difference(c, j):
                a, n = size(unit(c, j))
                u = number(c, j)
                pool.wait_ge(paired, 3 * u + 2)
                nc.gpsimd.tensor_tensor(high_line[2][0:a, 0:n], high_line[2][0:a, 0:n], low_line[2][0:a, 0:n],
                                        ALU.subtract).then_inc(paired, 1)
                if unit(c, j + 3) is not None:
                    pool.wait_ge(lined, 4 * u + 4)
                    pool.sem_inc(pool_held, 1)
                    load_codes(pool, codes_in, code, code_in, c, j + 3)

            def step(c, j):
                more = unit(c, j + 1) is not None
                if more:
                    pair(c, j + 1, 0)
                if unit(c, j) is not None:
                    low(c, j)
                if more:
                    pair(c, j + 1, 1)
                    difference(c, j + 1)

            for i in range(2):
                pair(-1, UNITS - EARLY, i)
            difference(-1, UNITS - EARLY)
            for j in range(UNITS - EARLY, UNITS):
                step(-1, j)

            def chunk(c):
                for s in range(UNITS):
                    step(c, s)
                    if s < CHUNK * GROUPS:
                        b, tg = s // GROUPS, s % GROUPS
                        r = LAST if at(CHUNK * c + b, NB - 1) else P
                        cols = slice(tg * HW, (tg + 1) * HW)
                        pool.wait_ge(inner_high, CHUNK * GROUPS * c + s + 1)
                        nc.gpsimd.tensor_tensor(inner[b][1][0:r, cols], act_in[tg % 2][0:r, :], inner[b][0][0:r, cols],
                                                ALU.subtract).then_inc(inner_low, 1)

            chunks(pool, chunk)

        @block.scalar
        def _(act):
            act.sem_inc(placed, 2)

            def lines(c, j, first):
                un = unit(c, j)
                if un is None:
                    return
                a, n = size(un)
                u = number(c, j)
                slot = code_slot(j)
                if first == 2:
                    act.wait_ge(code_in[slot], 16 * (4 * c + (j + EARLY) // 3 + 1))
                for side in range(2):
                    if first == 2 and not at(u, 0):
                        act.wait_ge((paired, decoded)[side], (3, 1)[side] * u)
                    for i in (first, first + 1):
                        ins = nc.scalar.activation((low_line, high_line)[side][i][0:a, 0:n], code[slot][0:a, 0:n], ACT.Relu,
                                                   bias=line_bias[0:a, side, i:i + 1], scale=(LOW, HIGH)[side][i][0])
                    ins.then_inc(lined, 1)

            def high(c, j):
                a, n = size(unit(c, j))
                u = number(c, j)
                act.wait_ge(scaled, u + 1)
                act.wait_ge(turned, u + 1)
                nc.scalar.activation(parts[j % 2][0:a, 0, 0:n], weight[j % 2][0:a, 0:n], ACT.Copy).then_inc(high_made, 1)

            def place(c, j):
                which, n, half, r, buf = unit(c, j)
                u = number(c, j)
                act.wait_ge(turned, u + 3)
                if which < 2:
                    w, lo = (0, which * r) if r < P and PACKED else (which, 0)
                    dst = gu_w[buf][:, w, :, 4 * half:4 * half + 4, lo:lo + r]
                    src = turn_ps[j % 2][:, :, 0:4 * r].rearrange("p h (k i) -> p h k i", k=4)
                else:
                    dst = dn_w[buf][0:r, :, half * HW:(half + 1) * HW]
                    src = turn_ps[j % 2][0:r, :, :]
                nc.scalar.activation(dst, src, ACT.Copy).then_inc(placed, 1)

            def step(c, j):
                lines(c, j + 1, 2)
                if unit(c, j) is not None:
                    high(c, j)
                lines(c, j + 1, 0)

            act.wait_ge(bias_made, 1)
            for first in (2, 0):
                lines(-1, UNITS - EARLY, first)
            for j in range(UNITS - EARLY, UNITS):
                step(-1, j)
                place(-1, j)

            def chunk(c):
                for s in range(UNITS):
                    step(c, s)
                    if s < CHUNK * GROUPS:
                        b, tg = s // GROUPS, s % GROUPS
                        r = LAST if at(CHUNK * c + b, NB - 1) else P
                        g = CHUNK * GROUPS * c + s
                        act.wait_ge(gu_made, g + 1)
                        act.wait_ge(inner_low, g + 1)
                        nc.scalar.activation(act_in[tg % 2][0:r, :], gate_ps[tg % 2][0:r, :], ACT.Silu).then_inc(silu_made, 1)
                        act.wait_ge(gated, g + 3)
                        nc.scalar.activation(inner[b][0][0:r, tg * HW:(tg + 1) * HW], act_in[tg % 2][0:r, :],
                                             ACT.Copy).then_inc(inner_high, 1)
                    if unit(c, s) is not None:
                        place(c, s)

            chunks(act, chunk)

        @block.tensor
        def _(pe):
            pe.sem_inc(turned, 2)

            def turn(c, j):
                which, n, half, r, buf = unit(c, j)
                u = number(c, j)
                pe.wait_ge(low_made, u + 3)
                pe.wait_ge(placed, u + 1)
                for h in range(2):
                    for k in range(4):
                        if which < 2:
                            ins = nc.tensor.transpose(turn_ps[j % 2][:, h, k * r:(k + 1) * r],
                                                      parts[j % 2][0:r, h, k * P:(k + 1) * P], identb[0:r, 0:r])
                        else:
                            ins = nc.tensor.transpose(turn_ps[j % 2][0:r, h, k * P:(k + 1) * P],
                                                      parts[j % 2][:, h, k * r:(k + 1) * r], identb[:])
                ins.then_inc(turned, 1)

            for j in range(UNITS - EARLY, UNITS):
                turn(-1, j)

            def chunk(c):
                for b in range(CHUNK):
                    r = LAST if at(CHUNK * c + b, NB - 1) else P
                    pe.wait_ge(placed, number(c, b * GROUPS - 1) + 2)
                    for tg in range(GROUPS):
                        g = 2 * GROUPS * c + GROUPS * b + tg
                        pe.wait_ge(gated, g + 1)
                        if b == 0 and tg == 1:
                            pe.wait_ge(added, 2 * NT * c + 4)
                        packed = r < P and PACKED
                        rows = 2 * r if packed else r
                        for which in range(1 if packed else 2):
                            out = (gate_ps, up_ps)[which][tg % 2][0:rows, :]
                            for k in range(KT):
                                for n, (wp, xp) in enumerate(PASSES):
                                    ins = nc.tensor.matmul(out, gu_w[b][:, which, wp, k, 0:rows], xT[xp][:, k, tg * HW:(tg + 1) * HW],
                                                           start=(k == 0 and n == 0), stop=(k == KT - 1 and n == 2))
                        ins.then_inc(gu_made, 1)
                        if unit(c, GROUPS * b + tg) is not None:
                            turn(c, GROUPS * b + tg)
                pe.wait_ge(placed, number(c, 7) + 2)
                for t in range(NT):
                    if t % 4 == 0:
                        pe.wait_ge(inner_low, 2 * GROUPS * c + GROUPS + t // 4 + 3)
                    for h in range(2):
                        o = 2 * t + h
                        if o == 2:
                            pe.wait_ge(gated, 2 * GROUPS * (c + 1) + 2)
                        pe.wait_ge(added, 2 * NT * c + o + 1)
                        for b in range(CHUNK):
                            r = LAST if at(CHUNK * c + b, NB - 1) else P
                            for n, (wp, xp) in enumerate(PASSES):
                                ins = nc.tensor.matmul(down_ps[o % 4][:], inner[b][xp][0:r, t * P:(t + 1) * P],
                                                       dn_w[b][0:r, wp, h * HW:(h + 1) * HW],
                                                       start=(b == 0 and n == 0), stop=(b == CHUNK - 1 and n == 2))
                        ins.then_inc(down_made, 1)
                    s = CHUNK * GROUPS + t // 4
                    if t % 4 == 3 and unit(c, s) is not None:
                        turn(c, s)

            chunks(pe, chunk)

        @block.vector
        def _(dve):
            def join(c, j, part):
                un = unit(c, j)
                if un is None:
                    return
                which, n, half, r, _ = un
                a, m = size(un)
                u = number(c, j)
                lo, hi = ([x[0:a, 0:m] for x in side] for side in (low_line, high_line))
                w = weight[j % 2][0:a, 0:m]
                if part == 0:
                    dve.wait_ge(lined, 4 * u + 3)
                    dve.wait_ge(low_made, u + 1)
                    nc.vector.tensor_tensor(w, lo[0], lo[1], ALU.max)
                    dve.wait_ge(lined, 4 * u + 4)
                    nc.vector.tensor_tensor(hi[0], hi[0], hi[1], ALU.max).then_inc(joined, 1)
                elif part == 1:
                    dve.wait_ge(joined, 2 * u + 1)
                    nc.vector.tensor_tensor(w, hi[0], w, ALU.subtract).then_inc(joined, 1)
                elif part == 2:
                    dve.wait_ge(joined, 2 * u + 2)
                    dve.wait_ge(paired, 3 * u + 3)
                    nc.vector.tensor_tensor(w, w, hi[2], ALU.add).then_inc(decoded, 1)
                else:
                    if which < 2:
                        scale = gu_scale[which][0:r, bass.ds(n, 1), 8 * half:8 * half + 8].rearrange("p o s -> p (o s)")
                        scale = scale.unsqueeze(2).to_broadcast([r, HW // SB, SB])
                        w = w.rearrange("p (s i) -> p s i", i=SB)
                    else:
                        scale = dn_scale[:, 4 * half:4 * half + 4, bass.ds(n * (P // SB), r // SB)]
                        scale = scale.unsqueeze(3).to_broadcast([P, 4, r // SB, SB])
                        w = w.rearrange("p (t s i) -> p t s i", t=4, i=SB)
                    dve.wait_ge(decoded, u + 1)
                    nc.vector.tensor_tensor(w, w, scale, ALU.mult).then_inc(scaled, 1)

            steps, last = None, [0, 0]

            def turn_of(c, lane, n):
                if lane == 0:
                    k, n = 2 * (n // ROUNDS) + 1, n % ROUNDS
                else:
                    n += AHEAD
                    k, n = 2 * (n // ROUNDS), n % ROUNDS
                t = TILE_CHUNK * c + k
                return None if isinstance(t, int) and t >= TILES else (k, n)

            def find(c, n, lanes=(0, 1)):
                for lane in lanes:
                    turn = turn_of(c, lane, n)
                    if turn is None:
                        continue
                    k, m = turn
                    if m == 0:
                        dve.wait_ge(left_in[k % 3], 16 * (2 * c + k // 3 + 1))
                        dve.sem_inc(held, 1)
                    elif last[lane]:
                        dve.wait_ge(found, last[lane])
                    steps.done(nc.vector.max(best[lane][:], left[k % 3][:, ::-1]))
                    last[lane] = steps.n

            def mark(c, n, lanes=(0, 1)):
                for lane in lanes:
                    turn = turn_of(c, lane, n)
                    if turn is None:
                        continue
                    k, m = turn
                    dve.wait_ge(found, last[lane])
                    if m == ROUNDS - 1 and REST % 8:
                        steps.done(nc.vector.memset(best[lane][:, REST % 8:8], GONE))
                        steps.wait()
                    row = left[k % 3][:, ::-1]
                    steps.done(nc.vector.match_replace(row, best[lane][:], row, GONE))
                    last[lane] = steps.n
                    if m == ROUNDS - 1:
                        steps.wait()
                        dve.wait_ge(mask_out, 16 * (TILE_CHUNK * c + k + 1))
                        nc.vector.tensor_scalar(mask[:], left[k % 3][:], GONE, None, ALU.is_gt).then_inc(mask_made, 1)

            def statistics(t):
                steps.wait()
                if t < NT:
                    dve.wait_ge(added, 2 * NT * (CHUNKS - 1) + 2 * t + 6)
                    for h in range(2):
                        ins = nc.vector.bn_stats(stats[:, t % 2, h, :], X[:, t, h * HW:(h + 1) * HW])
                    steps.done(ins)
                if t > 0:
                    steps.done(nc.vector.bn_aggr(x2_mv[:, t - 1, :], stats[:, (t - 1) % 2, :, :]))

            def clear():
                steps.wait()
                dve.sem_clear(found)
                last[:] = 0, 0

            dve.sem_inc(gated, 2)
            dve.sem_inc(added, 4)
            for side, table in enumerate((LOW, HIGH)):
                for i, (_, bias) in enumerate(table):
                    ins = nc.vector.memset(line_bias[:, side, i:i + 1], bias)
            ins.then_inc(bias_made, 1)
            dve.wait_ge(scale_in, 16 * 5)
            steps = Steps(dve, found)
            for j in range(UNITS - EARLY, UNITS):
                for part in range(4):
                    join(-1, j, part)
            for n in range(-AHEAD, 0):
                find(0, n, (1,))
                mark(0, n, (1,))
            clear()

            def chunk(c):
                nonlocal steps
                steps = Steps(dve, found)
                n = 0
                for s in range(CHUNK * GROUPS):
                    join(c, s, 0)
                    find(c, n)
                    join(c, s, 1)
                    mark(c, n)
                    join(c, s, 2)
                    find(c, n + 1)
                    join(c, s, 3)
                    mark(c, n + 1)
                    for m in range(n + 2, n + GROUP_ROUNDS):
                        find(c, m)
                        mark(c, m)
                    n += GROUP_ROUNDS
                    b, tg = s // GROUPS, s % GROUPS
                    r = LAST if at(CHUNK * c + b, NB - 1) else P
                    g = CHUNK * GROUPS * c + s
                    dve.wait_ge(silu_made, g + 1)
                    up = gate_ps[tg % 2][r:2 * r, :] if r < P and PACKED else up_ps[tg % 2][0:r, :]
                    nc.vector.tensor_tensor(act_in[tg % 2][0:r, :], act_in[tg % 2][0:r, :], up, ALU.mult).then_inc(gated, 1)
                for o in range(2 * NT):
                    s, m = CHUNK * GROUPS + o // 8, o % 8
                    t, h = o // 2, o % 2
                    piece = X[:, t, h * HW:(h + 1) * HW]
                    dve.wait_ge(down_made, 2 * NT * c + o + 1)
                    nc.vector.tensor_tensor(piece, piece, down_ps[o % 4][:], ALU.add).then_inc(added, 1)
                    if m < 4:
                        join(c, s, m)
                    elif n < LANE_ROUNDS:
                        if m % 2 == 0:
                            find(c, n)
                        else:
                            mark(c, n)
                            n += 1
                    if at(c, CHUNKS - 1) and h == 1 and t > 0:
                        statistics(t - 1)
                if at(c, CHUNKS - 1):
                    statistics(NT - 1)
                    statistics(NT)
                clear()

            chunks(dve, chunk)


def rows_variances(nc, dve, steps, held, X, n, stats, mv, ve, var):
    for a in range(CT):
        for h in range(2):
            ins = nc.vector.bn_stats(stats[:, a, h, :], X[:, bass.ds(CT * n + a, 1), h * HW:(h + 1) * HW])
    steps.done(ins)
    steps.wait(held)
    for a in range(CT):
        ins = nc.vector.bn_aggr(mv[:, a, :], stats[:, a, :, :])
    steps.done(ins)
    steps.wait()
    nc.vector.tensor_scalar(ve[:], mv[:, :, 1], EPS, None, ALU.add).then_inc(var, 1)


def there(b):
    return not isinstance(b, int) or 0 <= b < B


def reused(b):
    return not isinstance(b, int) or b >= 2


def pooled(nc, mask_t, conv, gamma, beta, w8_t, X, x2_mv, gates, norms, w8, mask, xn, ident):
    with ExitStack() as st:
        def sb(name, shape, dt=F32):
            return st.enter_context(nc.sbuf_tensor(name, shape, dt))

        def sem(name):
            return st.enter_context(nc.semaphore(name))

        xlT = [sb(f"c_xlT{p}", [P, KT, C]) for p in range(2)]
        inside = [sb(f"c_inside{p}", [P, KT, C]) for p in range(2)]
        outside = [sb(f"c_outside{p}", [P, KT, C]) for p in range(2)]
        junk = sb("c_junk", [P, KT, C])
        ve = sb("c_ve", [P, NT])
        power = sb("c_power", [P, NT])
        rate = [sb(f"c_rate{p}", [P, 2, CT]) for p in range(2)]
        feat = sb("c_feat", [P, 2, 2, TILES])
        sums = sb("c_sums", [P, 2, TILES])
        taps = sb("c_taps", [P, 2, 7])
        joint = sb("c_joint", [P, 3 * P + 6])
        band = sb("c_band", [P, 2, 3 * P])
        ones = sb("c_ones", [P, P])
        z = sb("c_z", [P, 2, TILES])
        zsq = sb("c_zsq", [P, 2, TILES])
        zsum = sb("c_zsum", [P, 2])
        mean = sb("c_mean", [P, 2])
        zvar = sb("c_zvar", [P, 2])
        zrstd = sb("c_zrstd", [P, 2])
        affine = sb("c_affine", [P, 2])
        gate = sb("c_gate", [P, 2, TILES])
        turn_ps = [st.enter_context(nc.psum_tensor(f"c_turn{i}", [P, 2, C], F32)) for i in range(4)]
        z_ps = st.enter_context(nc.psum_tensor("c_z_ps", [P, 2, TILES], F32))
        sum_ps = st.enter_context(nc.psum_tensor("c_sum_ps", [P, 2, 2], F32))

        small_in = sem("c_small_in")
        mask_in = [sem(f"c_mask_in{p}") for p in range(2)]
        w_in = sem("c_w_in")
        const = sem("c_const")
        var = sem("c_var")
        root = sem("c_root")
        rated = sem("c_rated")
        normed = sem("c_normed")
        turned = sem("c_turned")
        placed = sem("c_placed")
        in_made = sem("c_in_made")
        out_made = sem("c_out_made")
        out_max = sem("c_out_max")
        out_sum = sem("c_out_sum")
        averaged = sem("c_averaged")
        convolved = sem("c_convolved")
        summed = sem("c_summed")
        totalled = sem("c_totalled")
        zvared = sem("c_zvared")
        zroot = sem("c_zroot")
        znormed = sem("c_znormed")
        gated = sem("c_gated")
        step = sem("c_step")
        held, act_held = (sem(f"c_held_{e}") for e in ("dve", "act"))
        block = st.enter_context(nc.Block())
        masks = mask_t.rearrange("(b k) p c -> b p k c", k=KT)

        def bodies(eng, body):
            body(0, 0)
            body(1, 1)
            with eng.Fori(1, B // 2 - 1) as i:
                body(2 * i, 0)
                body(2 * i + 1, 1)
            body(B - 2, 0)
            body(B - 1, 1)

        @block.sync
        def _(sp):
            def load_mask(b, p):
                sp.dma_start(mask[p][:], masks[bass.ds(b, 1)].rearrange("o p k c -> (o p) k c")).then_inc(mask_in[p], 16)

            sp.dma_start(taps[:], conv.rearrange("o c t -> (o c) t").partition_broadcast(P)).then_inc(small_in, 16)
            sp.dma_start(affine[:, 0:1], gamma.partition_broadcast(P)).then_inc(small_in, 16)
            sp.dma_start(affine[:, 1:2], beta.partition_broadcast(P)).then_inc(small_in, 16)
            for p in range(2):
                load_mask(p, p)
            sp.dma_start(w8[:], w8_t.rearrange("k p n -> p k n")).then_inc(w_in, 16)
            with sp.Fori(0, B // 2 - 1) as i:
                for p in range(2):
                    b = 2 * i + p
                    sp.wait_ge(in_made, b + 1)
                    load_mask(b + 2, p)
            for p in range(2):
                sp.wait_ge(in_made, B - 1 + p)
                load_mask(p, p)
                sp.wait_ge(mask_in[p], 8 * B + 16)
            sp.wait_ge(w_in, 16)

        @block.gpsimd
        def _(pool):
            nc.gpsimd.memset(power[:], -0.5).then_inc(const, 1)
            nc.gpsimd.memset(ones[:], 1.0).then_inc(const, 1)

            nc.gpsimd.memset(joint[:], 0.0).then_inc(const, 1)
            pool.wait_ge(const, 3)
            nc.gpsimd.affine_select(out=joint[:], in_=joint[:], compare_op=ALU.not_equal, fill=1.0, base=P + 3,
                                    pattern=[[-1, 3 * P + 6]], channel_multiplier=1).then_inc(const, 1)
            pool.wait_ge(var, 1)
            nc.gpsimd.tensor_tensor(norms[:, 0, :], ve[:], power[:], ALU.pow).then_inc(root, 1)

            def body(b, p):
                pool.wait_ge(in_made, b + 1)
                if reused(b):
                    pool.wait_ge(out_max, b - 1)
                    pool.wait_ge(out_sum, KT * b - KT)
                nc.gpsimd.tensor_tensor(outside[p][:], xlT[p][:], inside[p][:], ALU.subtract).then_inc(out_made, 1)

            bodies(pool, body)
            pool.wait_ge(zvared, 1)
            nc.gpsimd.tensor_tensor(zrstd[:], zvar[:], power[:, 0:2], ALU.pow).then_inc(zroot, 1)

        @block.scalar
        def _(act):
            def norm(b, p):
                act.wait_ge(rated, b + 1)
                if reused(b):
                    act.wait_ge(turned, 4 * b - 4)
                act.sem_inc(act_held, 1)
                for a in range(CT):
                    t = CT * (b % B) + a if isinstance(b, int) else CT * b + a
                    ins = nc.scalar.activation(xn[p][:, a:a + 1, :], X[:, bass.ds(t, 1), :], ACT.Identity,
                                               scale=rate[p][:, 0, a:a + 1], bias=rate[p][:, 1, a:a + 1])
                ins.then_inc(normed, 1)

            def place(b, p):
                if reused(b):
                    act.wait_ge(out_made, b - 1)
                for f in range(4):
                    act.wait_ge(turned, 4 * b + f + 1)
                    nc.scalar.activation(xlT[p][:, 2 * f:2 * f + 2, :], turn_ps[f][:], ACT.Copy).then_inc(placed, 1)

            def sum_out(b, p):
                act.wait_ge(out_made, b + 1)
                if not at(b, 0):
                    act.wait_ge(out_sum, KT * b)
                act.sem_inc(act_held, 1)
                for k in range(KT):
                    nc.scalar.activation(junk[:, k, :], outside[p][:, k, :], ACT.Copy,
                                         accum_out=sums[:, 1, bass.ds(KT * b + k, 1)]).then_inc(out_sum, 1)

            norm(0, 0)
            place(0, 0)

            def body(b, p):
                if there(b + 1):
                    norm(b + 1, 1 - p)
                if not at(b, 0):
                    sum_out(b - 1, 1 - p)
                if there(b + 1):
                    place(b + 1, 1 - p)

            bodies(act, body)
            sum_out(B - 1, 1)
            for b in range(B, B + 2):
                norm(b, b % 2)
            act.wait_ge(znormed, 1)
            nc.scalar.activation(gate[:], z[:], ACT.Sigmoid).then_inc(gated, 1)

        @block.tensor
        def _(pe):
            def body(b, p):
                pe.wait_ge(normed, b + 1)
                for f in range(4):
                    if not at(b, 0):
                        pe.wait_ge(placed, 4 * b + f - 3)
                    for j in range(4):
                        k, a = 2 * f + j // 2, j % 2
                        ins = nc.tensor.transpose(turn_ps[f][:, j // 2, a * P:(a + 1) * P], xn[p][:, a, k * P:(k + 1) * P], ident[:])
                    ins.then_inc(turned, 1)

            bodies(pe, body)
            pe.wait_ge(averaged, 1)
            n = 0
            for c in range(2):
                f3 = feat[:, c, :, :].rearrange("p s (b k) -> p (s b) k", k=KT)
                z3 = z_ps[:].rearrange("p s (b k) -> p (s b) k", k=KT)
                for lo, dst, src in ((P, slice(0, KT), slice(0, KT)), (2 * P, slice(1, KT), slice(0, KT - 1)),
                                     (0, slice(0, KT - 1), slice(1, KT))):
                    ins = nc.tensor.matmul(z3[:, :, dst], band[:, c, lo:lo + P], f3[:, :, src], start=(n == 0), stop=(n == 5),
                                           skip_group_check=True)
                    n += 1
            ins.then_inc(convolved, 1)
            for i in range(2):
                pe.wait_ge(summed, i + 1)
                nc.tensor.matmul(sum_ps[:, i, :], ones[:], zsum[:], start=True, stop=True).then_inc(totalled, 1)

        @block.vector
        def _(dve):
            steps = Steps(dve, step)
            nc.vector.tensor_scalar(ve[:], x2_mv[:, :, 1], EPS, None, ALU.add).then_inc(var, 1)

            def taps_of(c):
                for t in range(7):
                    if t == 0:
                        steps.done(nc.vector.tensor_scalar(band[:, c, :], joint[:, t:t + 3 * P], taps[:, c, t:t + 1], None, ALU.mult))
                    else:
                        steps.wait()
                        steps.done(nc.vector.scalar_tensor_tensor(band[:, c, :], joint[:, t:t + 3 * P], taps[:, c, t:t + 1], band[:, c, :],
                                                                  ALU.mult, ALU.add))

            def rates(b, p):
                if reused(b):
                    dve.wait_ge(normed, b - 1)
                n = CT * (b % B) if isinstance(b, int) else CT * b
                nc.vector.tensor_copy(rate[p][:], norms[:, :, bass.ds(n, CT)]).then_inc(rated, 1)

            dve.wait_ge(const, 4)
            dve.wait_ge(small_in, 48)
            taps_of(0)
            dve.wait_ge(root, 1)
            steps.done(nc.vector.scalar_tensor_tensor(norms[:, 1, :], x2_mv[:, :, 0], -1.0, norms[:, 0, :], ALU.mult, ALU.mult))
            steps.wait()
            rates(0, 0)
            rates(1, 1)
            taps_of(1)

            def largest_out(b, p):
                dve.wait_ge(out_made, b + 1)
                nc.vector.tensor_reduce(feat[:, 0, 1, bass.ds(KT * b, KT)], outside[p][:], AX.X, ALU.max).then_inc(out_max, 1)

            def body(b, p):
                dve.wait_ge(placed, 4 * b + 4)
                dve.wait_ge(mask_in[p], 8 * (b - p) + 16)
                if reused(b):
                    dve.wait_ge(out_made, b - 1)
                dve.sem_inc(held, 1)
                for k in range(KT):
                    ins = nc.vector.scalar_tensor_tensor(inside[p][:, k, :], xlT[p][:, k, :], 1.0, mask[p][:, k, :], ALU.mult,
                                                         ALU.mult, accum_out=sums[:, 0, bass.ds(KT * b + k, 1)])
                ins.then_inc(in_made, 1)
                rates(b + 2, p)
                if not at(b, 0):
                    largest_out(b - 1, 1 - p)
                dve.wait_ge(in_made, b + 1)
                nc.vector.tensor_reduce(feat[:, 0, 0, bass.ds(KT * b, KT)], inside[p][:], AX.X, ALU.max)

            bodies(dve, body)
            largest_out(B - 1, 1)
            dve.wait_ge(out_sum, KT * B)
            for s, n in enumerate((TOPK, REST)):
                ins = nc.vector.tensor_scalar(feat[:, 1, s, :], sums[:, s, :], 1.0 / C, C / n, ALU.mult, ALU.mult)
            ins.then_inc(averaged, 1)
            dve.wait_ge(convolved, 1)
            steps.done(nc.vector.tensor_copy(z[:], z_ps[:]))
            steps.wait()
            nc.vector.tensor_reduce(zsum[:], z[:], AX.X, ALU.add).then_inc(summed, 1)
            dve.wait_ge(totalled, 1)
            steps.done(nc.vector.tensor_scalar(mean[:], sum_ps[:, 0, :], 1.0 / (B * D), None, ALU.mult))
            steps.wait()
            for s in range(2):
                ins = nc.vector.tensor_scalar(z[:, s, :], z[:, s, :], mean[:, s:s + 1], None, ALU.subtract)
            steps.done(ins)
            steps.wait()
            steps.done(nc.vector.tensor_tensor(zsq[:], z[:], z[:], ALU.mult))
            steps.wait()
            nc.vector.tensor_reduce(zsum[:], zsq[:], AX.X, ALU.add).then_inc(summed, 1)
            dve.wait_ge(totalled, 2)
            nc.vector.tensor_scalar(zvar[:], sum_ps[:, 1, :], 1.0 / (B * D), EPS, ALU.mult, ALU.add).then_inc(zvared, 1)
            dve.wait_ge(zroot, 1)
            for s in range(2):
                ins = nc.vector.tensor_scalar(z[:, s, :], z[:, s, :], zrstd[:, s:s + 1], affine[:, 0:1], ALU.mult, ALU.mult)
            steps.done(ins)
            steps.wait()
            nc.vector.tensor_scalar(z[:], z[:], affine[:, 1:2], 0.0, ALU.add, ALU.max).then_inc(znormed, 1)
            dve.wait_ge(gated, 1)
            nc.vector.tensor_tensor(gates[:, 0, :], gate[:, 0, :], gate[:, 1, :], ALU.subtract)
            nc.vector.tensor_copy(gates[:, 1, :], gate[:, 1, :])


def gates_and_fp8_ffn(nc, mask_t, bias, in_scale, w_scale, out, X, gates, norms, w8, mask, xn, ident, identb):
    with ExitStack() as st:
        def sb(name, shape, dt=F32):
            return st.enter_context(nc.sbuf_tensor(name, shape, dt))

        def ps(name, shape, dt=F32):
            return st.enter_context(nc.psum_tensor(name, shape, dt))

        def sem(name):
            return st.enter_context(nc.semaphore(name))

        own_gates = [sb(f"d_own_gates{p}", [P, 2, KT]) for p in range(2)]
        own_norm = [sb(f"d_own_norm{p}", [P, 2, CT]) for p in range(2)]
        part = [sb(f"d_part{p}", [P, KT, C]) for p in range(2)]
        stats = sb("d_stats", [P, CT, 2, 6])
        mv = sb("d_mv", [P, CT, 2])
        ve = sb("d_ve", [P, CT])
        rstd = sb("d_rstd", [P, CT])
        power = sb("d_power", [P, CT])
        rate = [sb(f"d_rate{p}", [P, CT]) for p in range(2)]
        offset = [sb(f"d_offset{p}", [P, CT]) for p in range(2)]
        y = [sb(f"d_y{p}", [P, CT, D]) for p in range(2)]
        grid = [sb(f"d_grid{p}", [P, CT, D]) for p in range(2)]
        x8 = [sb(f"d_x8_{p}", [P, CT, D], BF16) for p in range(2)]
        x8T = [sb(f"d_x8T{p}", [P, CT, KT, P], BF16) for p in range(2)]
        beyond = sb("d_beyond", [P, CT, D], BF16)
        nought = sb("d_nought", [P, CT, D], BF16)
        flag = [sb(f"d_flag{p}", [P, CT]) for p in range(2)]
        back = [sb(f"d_back{p}", [P, CT]) for p in range(2)]
        scales = sb("d_scales", [P, 4])
        bias_row = sb("d_bias", [P, 1, D])
        gate_ps = [ps(f"d_gate_ps{i}", [P, HW]) for i in range(3)]
        turn_ps = [ps(f"d_turn{i}", [P, KT, P], BF16) for i in range(2)]
        out_ps = [ps(f"d_out_ps{i}", [P, HW]) for i in range(3)]

        small_in = sem("d_small_in")
        mask_in = [sem(f"d_mask_in{p}") for p in range(2)]
        const = sem("d_const")
        owned = sem("d_owned")
        chosen = sem("d_chosen")
        normed = sem("d_normed")
        gate_turned = sem("d_gate_turned")
        gate_used = sem("d_gate_used")
        x3_made = sem("d_x3_made")
        var = sem("d_var")
        root = sem("d_root")
        rated = sem("d_rated")
        scaled = sem("d_scaled")
        gridded = sem("d_gridded")
        lifted = sem("d_lifted")
        biased = sem("d_biased")
        rounded = sem("d_rounded")
        overflowed = sem("d_overflowed")
        flagged = sem("d_flagged")
        backed = sem("d_backed")
        turned = sem("d_turned")
        placed = sem("d_placed")
        multiplied = sem("d_multiplied")
        finished = sem("d_finished")
        stored = sem("d_stored")
        step = sem("d_step")
        held, act_held = (sem(f"d_held_{e}") for e in ("dve", "act"))
        block = st.enter_context(nc.Block())
        out_rows = out.rearrange("b (a p) d -> b p a d", p=P)
        masks = mask_t.rearrange("(b k) p c -> b p k c", k=KT)

        def rounds(eng, body):
            body(0, 0)
            with eng.Fori(0, (B - 4) // 2) as i:
                body(2 * i + 1, 1)
                body(2 * i + 2, 0)
            for b in range(B - 3, B):
                body(b, b % 2)

        @block.sync
        def _(sp):
            def load_mask(b, p):
                sp.dma_start(mask[p][:], masks[bass.ds(b, 1)].rearrange("o p k c -> (o p) k c")).then_inc(mask_in[p], 16)

            for p in range(2):
                sp.sem_inc(mask_in[p], 16)
            sp.dma_start(scales[:, 0:1], in_scale.partition_broadcast(P)).then_inc(small_in, 16)
            sp.dma_start(scales[:, 1:2], w_scale.partition_broadcast(P)).then_inc(small_in, 16)
            sp.dma_start(bias_row[:, 0, :], bias.partition_broadcast(P)).then_inc(small_in, 16)
            for b in range(2, 5):
                sp.wait_ge(chosen, KT * (b - 1))
                load_mask(b, b % 2)

            def store(b):
                sp.wait_ge(finished, 4 * b + 8)
                sp.dma_start(out_rows[bass.ds(b, 1)].rearrange("o p a d -> (o p) a d"), X[:, bass.ds(CT * b, CT), :]).then_inc(stored, 16)

            for b in range(5, B):
                sp.wait_ge(chosen, KT * (b - 1))
                load_mask(b, b % 2)
                store(b - 5)
            with sp.Fori(B - 5, B) as b:
                store(b)
            sp.wait_ge(stored, 16 * B)

        @block.gpsimd
        def _(pool):
            nc.gpsimd.memset(power[:], -0.5).then_inc(const, 1)
            pool.wait_ge(const, 1)

            def root_of(b):
                pool.wait_ge(var, b + 1)
                nc.gpsimd.tensor_tensor(rstd[:], ve[:], power[:], ALU.pow).then_inc(root, 1)

            def add_gated(b, p):
                pool.wait_ge(gate_used, 4 * b + 4)
                rows = X[:, bass.ds(CT * b, CT), :]
                nc.gpsimd.tensor_tensor(rows, rows, xn[p][:], ALU.add).then_inc(x3_made, 1)

            add_gated(0, 0)
            root_of(0)
            add_gated(1, 1)
            pool.wait_ge(small_in, 48)

            def body(b, p):
                pool.wait_ge(gridded, b + 1)
                nc.gpsimd.tensor_tensor(y[p][:], y[p][:], grid[p][:], ALU.add).then_inc(lifted, 1)
                if there(b + 1):
                    root_of(b + 1)
                if there(b + 2):
                    add_gated(b + 2, p)
                rows = X[:, bass.ds(CT * b, CT), :]
                nc.gpsimd.tensor_tensor(rows, rows, bias_row[:].to_broadcast([P, CT, D]), ALU.add).then_inc(biased, 1)

            rounds(pool, body)

        @block.scalar
        def _(act):
            def choose(b, p):
                act.wait_ge(mask_in[p], 8 * (b - p) + 16)
                act.wait_ge(owned, b + 1)
                if reused(b):
                    act.wait_ge(gate_turned, 4 * b - 4)
                act.sem_inc(act_held, 1)
                for k in range(KT):
                    nc.scalar.activation(part[p][:, k, :], mask[p][:, k, :], ACT.Identity, scale=own_gates[p][:, 0, k:k + 1],
                                         bias=own_gates[p][:, 1, k:k + 1]).then_inc(chosen, 1)
                if reused(b):
                    act.wait_ge(x3_made, b - 1)
                    act.sem_inc(act_held, 1)
                if isinstance(b, int) and b < 2:
                    return
                for a in range(CT):
                    ins = nc.scalar.activation(xn[p][:, a:a + 1, :], X[:, bass.ds(CT * b + a, 1), :], ACT.Identity,
                                               scale=own_norm[p][:, 0, a:a + 1], bias=own_norm[p][:, 1, a:a + 1])
                ins.then_inc(normed, 1)

            def scale_rows(b, p):
                act.wait_ge(rated, b + 1)
                if reused(b):
                    act.wait_ge(rounded, b - 1)
                act.sem_inc(act_held, 1)
                for a in range(CT):
                    nc.scalar.activation(y[p][:, a:a + 1, :], X[:, bass.ds(CT * b + a, 1), :], ACT.Identity,
                                         scale=rate[p][:, a:a + 1], bias=offset[p][:, a:a + 1]).then_inc(scaled, 1)

            act.sem_inc(flagged, 2)
            act.sem_inc(normed, 2)
            choose(0, 0)
            choose(1, 1)
            choose(2, 0)
            scale_rows(0, 0)

            def body(b, p):
                if there(b + 3):
                    choose(b + 3, 1 - p)
                if there(b + 1):
                    scale_rows(b + 1, 1 - p)
                if reused(b):
                    act.wait_ge(multiplied, 4 * b)
                for a in range(CT):
                    act.wait_ge(turned, 2 * b + a + 3)
                    nc.scalar.activation(x8T[p][:, a, :, :], turn_ps[a][:], ACT.Copy).then_inc(placed, 1)
                if reused(b):
                    act.wait_ge(backed, b)
                act.wait_ge(flagged, 2 * b + 2)
                for a in range(CT):
                    nc.scalar.activation(beyond[:, a, :], x8[p][:, a, :], ACT.Copy, scale=OVERFLOW).then_inc(overflowed, 1)
                for a in range(CT):
                    act.wait_ge(overflowed, 2 * b + a + 1)
                    nc.scalar.activation(nought[:, a, :], beyond[:, a, :], ACT.Copy, scale=0.0,
                                         accum_out=flag[p][:, a:a + 1]).then_inc(flagged, 1)

            rounds(act, body)

        @block.tensor
        def _(pe):
            def turn_gate(b, p, f):
                a, h = f // 2, f % 2
                if f == 0:
                    pe.wait_ge(chosen, KT * b + KT)
                if f == 3 or not at(b, 0):
                    pe.wait_ge(gate_used, 4 * b + 1 if f == 3 else 4 * b if f == 0 else 4 * b + f - 3)
                for j in range(4):
                    ins = nc.tensor.transpose(gate_ps[f % 3][:, j * P:(j + 1) * P], part[p][:, 4 * h + j, a * P:(a + 1) * P], ident[:])
                ins.then_inc(gate_turned, 1)

            def turn(b, p):
                pe.wait_ge(rounded, b + 1)
                for a in range(CT):
                    if not at(b, 0):
                        pe.wait_ge(placed, 2 * b + a - 1)
                    for k in range(KT):
                        ins = nc.tensor.transpose(turn_ps[a][:, k, :], x8[p][:, a, k * P:(k + 1) * P], identb[:])
                    ins.then_inc(turned, 1)

            def multiply(b, p, o):
                a, h = o // 2, o % 2
                if h == 0:
                    pe.wait_ge(placed, 2 * b + a + 1)
                pe.wait_ge(finished, 4 * b + (4, 2, 3, 5)[o])
                for k in range(KT):
                    ins = nc.tensor.matmul(out_ps[o % 3][:], x8T[p][:, a, k, :], w8[:, k, h * HW:(h + 1) * HW],
                                           start=(k == 0), stop=(k == KT - 1))
                ins.then_inc(multiplied, 1)

            pe.sem_inc(turned, 2)
            pe.sem_inc(multiplied, 4)
            for b in range(2):
                for f in range(4):
                    turn_gate(b, b, f)
            for f in range(3):
                turn_gate(2, 0, f)

            def body(b, p):
                for o in range(4):
                    if not at(b, 0):
                        multiply(b - 1, 1 - p, o)
                    if o == 1 and there(b + 2):
                        turn_gate(b + 2, p, 3)
                if there(b + 3):
                    for f in range(3):
                        turn_gate(b + 3, 1 - p, f)
                turn(b, p)

            rounds(pe, body)
            for o in range(4):
                multiply(B - 1, 1, o)

        @block.vector
        def _(dve):
            def take(b, p):
                if reused(b):
                    dve.wait_ge(chosen, KT * b - KT)
                    dve.wait_ge(normed, b - 1)
                nc.vector.tensor_copy(own_gates[p][:], gates[:, :, bass.ds(KT * b, KT)])
                nc.vector.tensor_copy(own_norm[p][:], norms[:, :, bass.ds(CT * b, CT)]).then_inc(owned, 1)

            def use_gate(b, p, f):
                a, h = f // 2, f % 2
                piece = xn[p][:, a, h * HW:(h + 1) * HW]
                if f == 0:
                    dve.wait_ge(normed, b + 1)
                dve.wait_ge(gate_turned, 4 * b + f + 1)
                nc.vector.tensor_tensor(piece, piece, gate_ps[f % 3][:], ALU.mult).then_inc(gate_used, 1)

            def variances(b):
                dve.wait_ge(x3_made, b + 1)
                rows_variances(nc, dve, steps, held, X, b, stats, mv, ve, var)

            def rates(b, p):
                dve.wait_ge(root, b + 1)
                if reused(b):
                    dve.wait_ge(scaled, 2 * b - 2)
                steps.done(nc.vector.tensor_scalar(rate[p][:], rstd[:], scales[:, 2:3], None, ALU.mult))
                steps.wait()
                nc.vector.scalar_tensor_tensor(offset[p][:], mv[:, :, 0], -1.0, rate[p][:], ALU.mult, ALU.mult).then_inc(rated, 1)

            def finish(b, p, o):
                a, h = o // 2, o % 2
                if o == 0:
                    dve.wait_ge(flagged, 2 * b + 4)
                    nc.vector.tensor_scalar(back[p][:], flag[p][:], scales[:, 3:4], None, ALU.add).then_inc(backed, 1)
                    dve.wait_ge(backed, b + 2)
                    dve.wait_ge(biased, b + 1)
                piece = X[:, bass.ds(CT * b + a, 1), h * HW:(h + 1) * HW]
                dve.wait_ge(multiplied, 4 * b + o + 5)
                nc.vector.scalar_tensor_tensor(piece, out_ps[o % 3][:].unsqueeze(1), back[p][:, a:a + 1], piece,
                                               ALU.mult, ALU.add).then_inc(finished, 1)

            dve.sem_inc(backed, 1)
            dve.sem_inc(finished, 4)
            take(0, 0)
            take(1, 1)
            steps = Steps(dve, step)
            for f in range(4):
                use_gate(0, 0, f)
            take(2, 0)
            for f in range(4):
                use_gate(1, 1, f)
            variances(0)
            dve.wait_ge(small_in, 48)
            nc.vector.tensor_tensor(scales[:, 3:4], scales[:, 0:1], scales[:, 1:2], ALU.mult)
            steps.done(nc.vector.reciprocal(scales[:, 2:3], scales[:, 0:1]))
            steps.wait()
            rates(0, 0)
            before = steps.n

            def body(b, p):
                nonlocal steps
                steps = Steps(dve, step, before + 4 * b)
                if there(b + 3):
                    take(b + 3, 1 - p)
                dve.wait_ge(scaled, 2 * b + 2)
                steps.done(nc.vector.tensor_scalar(grid[p][:].bitcast(I32), y[p][:].bitcast(I32), EXPONENT, None, ALU.bitwise_and))
                steps.wait()
                nc.vector.tensor_scalar(grid[p][:], grid[p][:], FP8_LEAST, TO_GRID, ALU.max, ALU.mult).then_inc(gridded, 1)
                if there(b + 2):
                    for f in range(3):
                        use_gate(b + 2, p, f)
                if there(b + 1):
                    variances(b + 1)
                if there(b + 2):
                    use_gate(b + 2, p, 3)
                for o in range(4):
                    if not at(b, 0):
                        finish(b - 1, 1 - p, o)
                    if o == 1:
                        if there(b + 1):
                            rates(b + 1, 1 - p)
                        dve.wait_ge(lifted, b + 1)
                        if reused(b):
                            dve.wait_ge(turned, 2 * b)
                            dve.wait_ge(flagged, 2 * b)
                        nc.vector.tensor_tensor(x8[p][:], y[p][:], grid[p][:], ALU.subtract).then_inc(rounded, 1)

            rounds(dve, body)
            for o in range(4):
                finish(B - 1, 1, o)


def program(nc, x, ctx, gate_codes, gate_scales, up_codes, up_scales, down_codes, down_scales, conv_w, gamma, beta,
            weight, bias, in_scale, w_scale, out):
    ctx_t = nc.dram_tensor("ctx_t", [B, KT, P, C], F32, kind="Internal").ap()
    w8_t = nc.dram_tensor("w8_t", [KT, P, D], BF16, kind="Internal").ap()
    mask_t = nc.dram_tensor("mask_t", [TILES, P, C], BF16, kind="Internal").ap()
    with ExitStack() as st:
        X = st.enter_context(nc.sbuf_tensor("x_rows", [P, NT, D], F32))
        ident = st.enter_context(nc.sbuf_tensor("ident", [P, P], F32))
        identb = st.enter_context(nc.sbuf_tensor("identb", [P, P], BF16))
        x2_mv = st.enter_context(nc.sbuf_tensor("x2_mv", [P, NT, 2], F32))
        with ExitStack() as ffn:
            xT = [ffn.enter_context(nc.sbuf_tensor(f"xT_{n}", [P, KT, NT * P], BF16)) for n in ("high", "low")]
            code = [ffn.enter_context(nc.sbuf_tensor(f"code{i}", [P, HW], BF16)) for i in range(3)]
            code_in = [ffn.enter_context(nc.semaphore(f"code_in{i}")) for i in range(3)]
            gu_scale = [ffn.enter_context(nc.sbuf_tensor(f"gate_up_scale{i}", [P, NB, D // SB], F32)) for i in range(2)]
            dn_scale = ffn.enter_context(nc.sbuf_tensor("down_scale", [P, KT, I // SB], F32))
            codes = code, code_in, gu_scale, dn_scale, ffn.enter_context(nc.semaphore("scale_in"))
            codes_in, scales_in = (gate_codes, up_codes, down_codes), (gate_scales, up_scales, down_scales)
            attention(nc, x, ctx, weight, w_scale, codes_in, scales_in, ctx_t, w8_t, X, xT, codes, ident, identb)
            gated_ffn(nc, codes_in, ctx_t, mask_t, X, xT, codes, x2_mv, identb)
        w8 = st.enter_context(nc.sbuf_tensor("w8", [P, KT, D], BF16))
        gates = st.enter_context(nc.sbuf_tensor("gates", [P, 2, TILES], F32))
        mask = [st.enter_context(nc.sbuf_tensor(f"mask{p}", [P, KT, C], BF16)) for p in range(2)]
        xn = [st.enter_context(nc.sbuf_tensor(f"xn{p}", [P, CT, D], F32)) for p in range(2)]
        norms = st.enter_context(nc.sbuf_tensor("norms", [P, 2, NT], F32))
        pooled(nc, mask_t, conv_w, gamma, beta, w8_t, X, x2_mv, gates, norms, w8, mask, xn, ident)
        gates_and_fp8_ffn(nc, mask_t, bias, in_scale, w_scale, out, X, gates, norms, w8, mask, xn, ident, identb)


_INS = ["x", "ctx_4096", "L0_ffn_gate_codes", "L0_ffn_gate_scales", "L0_ffn_up_codes", "L0_ffn_up_scales",
        "L0_ffn_down_codes", "L0_ffn_down_scales", "L1_xattn_conv_w", "L1_xattn_bn_gamma", "L1_xattn_bn_beta",
        "L1_ffn_weight", "L1_ffn_bias", "L1_ffn_input_scale", "L1_ffn_weight_scale"]
_OUTS = [((B, C, D), "float32")]


def kernel(**inputs):
    import numpy as _np
    import concourse.bacc as _bacc
    from concourse import mybir as _mybir
    from concourse.bass_utils import run_bass_kernel_spmd as _run

    nc = _bacc.Bacc("TRN2", target_bir_lowering=False, num_devices=1)
    arrays, args = {}, []
    for name in _INS:
        a = _np.ascontiguousarray(inputs[name])
        arrays[f"in_{name}_dram"] = a
        args.append(nc.dram_tensor(f"in_{name}_dram", a.shape, _mybir.dt.from_np(a.dtype), kind="ExternalInput").ap())
    for i, (shape, dtype) in enumerate(_OUTS):
        dt = _mybir.dt.from_np(_np.dtype(dtype))
        args.append(nc.dram_tensor(f"out_{i}_dram", shape, dt, kind="ExternalOutput").ap())
    program(nc, *args)
    r = _run(nc, [arrays], core_ids=[0])
    got = tuple(r.results[0][f"out_{i}_dram"] for i in range(len(_OUTS)))
    return got[0]
```
